# Optimizing a Trainium2 kernel written in Bass

```python
import numpy as np
import jax
import jax.numpy as jnp

def _softmax(x, axis=-1):
    return jax.nn.softmax(x, axis=axis)

def _gelu(x):
    return jax.nn.gelu(x, approximate=True)

def _silu(x):
    return jax.nn.silu(x)

def _sigmoid(x):
    return jax.nn.sigmoid(x)

def _layernorm(x, axis=-1, eps=1e-05):
    m = jnp.mean(x, axis=axis, keepdims=True)
    v = jnp.var(x, axis=axis, keepdims=True)
    return (x - m) / jnp.sqrt(v + eps)

def _scatter_add(tgt, idx, src, axis=0):
    return tgt.at[idx].add(src)

def _segment_sum(src, seg, n):
    return jax.ops.segment_sum(src, seg, n)
kernel_name = 'mk_vit_tower_postln_d2_tok_img1024_r4_d6d796'

def setup_inputs(seed: int=0):
    np.random.seed(seed)
    _w = jnp.asarray

    def _rec_inputs():
        import jax
        import jax.numpy as jnp
        _rk = jax.random.key(seed)
        x = -0.00016672 + 0.999947 * jax.random.normal(jax.random.fold_in(_rk, 1), (16, 96, 96, 3), jnp.float32)
        return x
    x = _rec_inputs()

    def _L0_tok_setup():
        import jax, jax.numpy as jnp
        import numpy as np
        P = 16
        E = 256

        def patchify(images, patch_size):
            B, H, W, C = images.shape
            hp, wp = (H // patch_size, W // patch_size)
            x = images.reshape(B, hp, patch_size, wp, patch_size, C)
            x = x.transpose(0, 1, 3, 2, 4, 5)
            return x.reshape(B, hp * wp, patch_size * patch_size * C)
        key = jax.random.key(seed)
        k_img, k_w, k_b, k_pos = jax.random.split(key, 4)
        B, H, W, C = (64, 96, 96, 3)
        patch_dim = P * P * C
        patch_count = H // P * (W // P)
        images = jax.random.normal(k_img, (B, H, W, C), dtype=jnp.float32)
        W_proj = jax.random.normal(k_w, (E, patch_dim), dtype=jnp.float32) * patch_dim ** (-0.5)
        b_proj = jax.random.normal(k_b, (E,), dtype=jnp.float32) * 0.02
        pos_emb = jax.random.normal(k_pos, (patch_count, E), dtype=jnp.float32) * 0.02
        return {'images': images, 'W_proj': W_proj, 'b_proj': b_proj, 'pos_emb': pos_emb}
    _L0_tok_all = _L0_tok_setup()
    _L0_tok_in = {k: v for k, v in _L0_tok_all.items() if k in ('W_proj', 'b_proj', 'pos_emb')}
    del _L0_tok_all

    def _L0_attn_setup():
        import jax, jax.numpy as jnp
        import numpy as np
        D_MODEL = 256
        N_HEADS = 16
        N_KV = 4
        HD = D_MODEL // N_HEADS
        N_REP = N_HEADS // N_KV
        WINDOW = 128
        SCALE = HD ** (-0.5)
        B, T = (2, 512)

        def _rope(x):
            t = x.shape[2]
            hd = x.shape[-1]
            inv_freq = 1.0 / 10000.0 ** (jnp.arange(0, hd, 2, dtype=jnp.float32) / hd)
            freqs = jnp.arange(t, dtype=jnp.float32)[:, None] * inv_freq[None, :]
            cos = jnp.cos(freqs)[None, None]
            sin = jnp.sin(freqs)[None, None]
            x1, x2 = (x[..., :hd // 2], x[..., hd // 2:])
            return jnp.concatenate([x1 * cos - x2 * sin, x1 * sin + x2 * cos], axis=-1)
        key = jax.random.key(seed)
        ks = jax.random.split(key, 6)
        s = 0.02
        return {'query': jax.random.normal(ks[0], (B, T, D_MODEL), dtype=jnp.float32), 'Wq': jax.random.normal(ks[1], (D_MODEL, D_MODEL), dtype=jnp.float32) * s, 'Wk': jax.random.normal(ks[2], (N_KV * HD, D_MODEL), dtype=jnp.float32) * s, 'Wv': jax.random.normal(ks[3], (N_KV * HD, D_MODEL), dtype=jnp.float32) * s, 'W1': jax.random.normal(ks[4], (4 * D_MODEL, D_MODEL), dtype=jnp.float32) * s, 'W2': jax.random.normal(ks[5], (D_MODEL, 4 * D_MODEL), dtype=jnp.float32) * s}
    _L0_attn_all = _L0_attn_setup()
    _L0_attn_in = {k: v for k, v in _L0_attn_all.items() if k in ('Wq', 'Wk', 'Wv', 'W1', 'W2')}
    del _L0_attn_all

    def _L0_ffn_setup():
        import jax, jax.numpy as jnp
        import numpy as np

        def _bitlinear(x, w_latent):
            scale = jax.lax.stop_gradient(jnp.clip(jnp.mean(jnp.abs(w_latent), axis=1, keepdims=True), 1e-05, None))
            tern = jnp.clip(jnp.round(w_latent / scale), -1.0, 1.0)
            w = w_latent + jax.lax.stop_gradient(tern - w_latent)
            return x @ (w * scale).T
        key = jax.random.key(seed)
        ks = jax.random.split(key, 6)
        dim, hidden, rank = (256, 1024, 16)
        B, S = (4, 1024)
        x = jax.random.normal(ks[0], (B, S, dim), dtype=jnp.float32)
        w_fc = 0.02 * jax.random.normal(ks[1], (hidden, dim), dtype=jnp.float32)
        w_proj = 0.02 * jax.random.normal(ks[2], (dim, hidden), dtype=jnp.float32)
        u = 0.02 * jax.random.normal(ks[3], (hidden, rank), dtype=jnp.float32)
        v = 0.02 * jax.random.normal(ks[4], (rank, dim), dtype=jnp.float32)
        fast_b = jax.random.normal(ks[5], (rank, rank), dtype=jnp.float32)
        gate = jnp.float32(0.05)
        return {'x': x, 'fast_b': fast_b, 'w_fc': w_fc, 'w_proj': w_proj, 'u': u, 'v': v, 'gate': gate}
    _L0_ffn_all = _L0_ffn_setup()
    _L0_ffn_in = {k: v for k, v in _L0_ffn_all.items() if k in ('fast_b', 'w_fc', 'w_proj', 'u', 'v', 'gate')}
    del _L0_ffn_all

    def _L1_attn_setup():
        import jax, jax.numpy as jnp
        import numpy as np
        B, T, D, H = (4, 512, 256, 16)
        HEAD_DIM = D // H
        LOCAL_WINDOW = 128

        def _rotate_half(t):
            t1, t2 = jnp.split(t, 2, axis=-1)
            return jnp.concatenate([-t2, t1], axis=-1)

        def _apply_rope(q, k):
            Tq, d = (q.shape[2], q.shape[3])
            half = d // 2
            theta = 1.0 / 10000.0 ** (jnp.arange(half, dtype=jnp.float32) / half)
            pos = jnp.arange(Tq, dtype=jnp.float32)
            freqs = pos[:, None] * theta[None, :]
            freqs = jnp.concatenate([freqs, freqs], axis=-1)
            cos = jnp.cos(freqs)[None, None]
            sin = jnp.sin(freqs)[None, None]
            q = q * cos + _rotate_half(q) * sin
            k = k * cos + _rotate_half(k) * sin
            return (q, k)
        key = jax.random.key(seed)
        k1, k2, k3 = jax.random.split(key, 3)
        x = jax.random.normal(k1, (B, T, D), dtype=jnp.float32)
        Wqkv = jax.random.normal(k2, (D, 3 * D), dtype=jnp.float32) * 0.02
        Wout = jax.random.normal(k3, (D, D), dtype=jnp.float32) * 0.02
        return {'x': x, 'Wqkv': Wqkv, 'Wout': Wout}
    _L1_attn_all = _L1_attn_setup()
    _L1_attn_in = {k: v for k, v in _L1_attn_all.items() if k in ('Wqkv', 'Wout')}
    del _L1_attn_all

    def _L1_ffn_setup():
        import jax, jax.numpy as jnp
        import numpy as np
        H = 256
        I = 512
        E = 8
        B, S = (2, 1024)
        EPS = 1e-05
        INIT = 0.02

        def _layernorm(x, w, b):
            mu = jnp.mean(x, axis=-1, keepdims=True)
            var = jnp.mean(jnp.square(x - mu), axis=-1, keepdims=True)
            return (x - mu) * jax.lax.rsqrt(var + EPS) * w + b
        key = jax.random.key(seed)
        ks = jax.random.split(key, 9)
        return {'hidden_states': jax.random.normal(ks[0], (B, S, H), jnp.float32), 'ln_w': jnp.ones((H,), jnp.float32), 'ln_b': jnp.zeros((H,), jnp.float32), 'router_w': jax.random.normal(ks[1], (H, E), jnp.float32) * INIT, 'gate_w': jax.random.normal(ks[2], (E, H, I), jnp.float32) * INIT, 'up_w': jax.random.normal(ks[3], (E, H, I), jnp.float32) * INIT, 'down_w': jax.random.normal(ks[4], (E, I, H), jnp.float32) * INIT, 'sh_gate': jax.random.normal(ks[5], (H, I), jnp.float32) * INIT, 'sh_up': jax.random.normal(ks[6], (H, I), jnp.float32) * INIT, 'sh_down': jax.random.normal(ks[7], (I, H), jnp.float32) * INIT}
    _L1_ffn_all = _L1_ffn_setup()
    _L1_ffn_in = {k: v for k, v in _L1_ffn_all.items() if k in ('ln_w', 'ln_b', 'router_w', 'gate_w', 'up_w', 'down_w', 'sh_gate', 'sh_up', 'sh_down')}
    del _L1_ffn_all
    return {'x': x, 'L0_tok_W_proj': _L0_tok_in['W_proj'], 'L0_tok_b_proj': _L0_tok_in['b_proj'], 'L0_tok_pos_emb': _L0_tok_in['pos_emb'], 'L0_attn_Wq': _L0_attn_in['Wq'], 'L0_attn_Wk': _L0_attn_in['Wk'], 'L0_attn_Wv': _L0_attn_in['Wv'], 'L0_attn_W1': _L0_attn_in['W1'], 'L0_attn_W2': _L0_attn_in['W2'], 'L0_ffn_fast_b': _L0_ffn_in['fast_b'], 'L0_ffn_w_fc': _L0_ffn_in['w_fc'], 'L0_ffn_w_proj': _L0_ffn_in['w_proj'], 'L0_ffn_u': _L0_ffn_in['u'], 'L0_ffn_v': _L0_ffn_in['v'], 'L0_ffn_gate': _L0_ffn_in['gate'], 'L1_attn_Wqkv': _L1_attn_in['Wqkv'], 'L1_attn_Wout': _L1_attn_in['Wout'], 'L1_ffn_ln_w': _L1_ffn_in['ln_w'], 'L1_ffn_ln_b': _L1_ffn_in['ln_b'], 'L1_ffn_router_w': _L1_ffn_in['router_w'], 'L1_ffn_gate_w': _L1_ffn_in['gate_w'], 'L1_ffn_up_w': _L1_ffn_in['up_w'], 'L1_ffn_down_w': _L1_ffn_in['down_w'], 'L1_ffn_sh_gate': _L1_ffn_in['sh_gate'], 'L1_ffn_sh_up': _L1_ffn_in['sh_up'], 'L1_ffn_sh_down': _L1_ffn_in['sh_down']}

def reference(x, L0_tok_W_proj, L0_tok_b_proj, L0_tok_pos_emb, L0_attn_Wq, L0_attn_Wk, L0_attn_Wv, L0_attn_W1, L0_attn_W2, L0_ffn_fast_b, L0_ffn_w_fc, L0_ffn_w_proj, L0_ffn_u, L0_ffn_v, L0_ffn_gate, L1_attn_Wqkv, L1_attn_Wout, L1_ffn_ln_w, L1_ffn_ln_b, L1_ffn_router_w, L1_ffn_gate_w, L1_ffn_up_w, L1_ffn_down_w, L1_ffn_sh_gate, L1_ffn_sh_up, L1_ffn_sh_down):
    import jax
    import jax.numpy as jnp

    def _L0_tok_ref(images, W_proj, b_proj, pos_emb):
        import jax, jax.numpy as jnp
        import numpy as np
        P = 16
        E = 256

        def patchify(images, patch_size):
            B, H, W, C = images.shape
            hp, wp = (H // patch_size, W // patch_size)
            x = images.reshape(B, hp, patch_size, wp, patch_size, C)
            x = x.transpose(0, 1, 3, 2, 4, 5)
            return x.reshape(B, hp * wp, patch_size * patch_size * C)
        patches = patchify(images, P)
        out = jnp.einsum('bnd,ed->bne', patches, W_proj) + b_proj + pos_emb[None, :, :]
        return out

    def _L0_attn_ref(query, Wq, Wk, Wv, W1, W2):
        import jax, jax.numpy as jnp
        import numpy as np
        D_MODEL = 256
        N_HEADS = 16
        N_KV = 4
        HD = D_MODEL // N_HEADS
        N_REP = N_HEADS // N_KV
        WINDOW = 128
        SCALE = HD ** (-0.5)
        B, T = (2, 512)

        def _rope(x):
            t = x.shape[2]
            hd = x.shape[-1]
            inv_freq = 1.0 / 10000.0 ** (jnp.arange(0, hd, 2, dtype=jnp.float32) / hd)
            freqs = jnp.arange(t, dtype=jnp.float32)[:, None] * inv_freq[None, :]
            cos = jnp.cos(freqs)[None, None]
            sin = jnp.sin(freqs)[None, None]
            x1, x2 = (x[..., :hd // 2], x[..., hd // 2:])
            return jnp.concatenate([x1 * cos - x2 * sin, x1 * sin + x2 * cos], axis=-1)
        b, t, _ = query.shape
        q = (query @ Wq.T).reshape(b, t, N_HEADS, HD).transpose(0, 2, 1, 3)
        k = (query @ Wk.T).reshape(b, t, N_KV, HD).transpose(0, 2, 1, 3)
        v = (query @ Wv.T).reshape(b, t, N_KV, HD).transpose(0, 2, 1, 3)
        q = _rope(q)
        k = _rope(k)
        k = jnp.repeat(k, N_REP, axis=1)
        v = jnp.repeat(v, N_REP, axis=1)
        scores = jnp.einsum('bhqd,bhkd->bhqk', q, k) * SCALE
        i = jnp.arange(t)[:, None]
        j = jnp.arange(t)[None, :]
        mask = (j > i) | (j < i - (WINDOW - 1))
        scores = jnp.where(mask[None, None], jnp.float32(-1e+30), scores)
        attn = jax.nn.softmax(scores, axis=-1)
        out = jnp.einsum('bhqk,bhkd->bhqd', attn, v)
        out = out.transpose(0, 2, 1, 3).reshape(b, t, D_MODEL)
        h = out @ W1.T
        h = h * jax.nn.sigmoid(h)
        return h @ W2.T

    def _L0_ffn_ref(x, fast_b, w_fc, w_proj, u, v, gate):
        import jax, jax.numpy as jnp
        import numpy as np

        def _bitlinear(x, w_latent):
            scale = jax.lax.stop_gradient(jnp.clip(jnp.mean(jnp.abs(w_latent), axis=1, keepdims=True), 1e-05, None))
            tern = jnp.clip(jnp.round(w_latent / scale), -1.0, 1.0)
            w = w_latent + jax.lax.stop_gradient(tern - w_latent)
            return x @ (w * scale).T
        h = _bitlinear(x, w_fc) + gate * (x @ v.T @ fast_b.T @ u.T)
        r = jnp.maximum(h, 0.0)
        return _bitlinear(r * r, w_proj)

    def _L1_attn_ref(x, Wqkv, Wout):
        import jax, jax.numpy as jnp
        import numpy as np
        B, T, D, H = (4, 512, 256, 16)
        HEAD_DIM = D // H
        LOCAL_WINDOW = 128

        def _rotate_half(t):
            t1, t2 = jnp.split(t, 2, axis=-1)
            return jnp.concatenate([-t2, t1], axis=-1)

        def _apply_rope(q, k):
            Tq, d = (q.shape[2], q.shape[3])
            half = d // 2
            theta = 1.0 / 10000.0 ** (jnp.arange(half, dtype=jnp.float32) / half)
            pos = jnp.arange(Tq, dtype=jnp.float32)
            freqs = pos[:, None] * theta[None, :]
            freqs = jnp.concatenate([freqs, freqs], axis=-1)
            cos = jnp.cos(freqs)[None, None]
            sin = jnp.sin(freqs)[None, None]
            q = q * cos + _rotate_half(q) * sin
            k = k * cos + _rotate_half(k) * sin
            return (q, k)
        Bx, Tx, C = x.shape
        h, d, w = (H, HEAD_DIM, LOCAL_WINDOW)
        qkv = x @ Wqkv
        q, k, v = jnp.split(qkv, 3, axis=-1)
        q = q.reshape(Bx, Tx, h, d).transpose(0, 2, 1, 3)
        k = k.reshape(Bx, Tx, h, d).transpose(0, 2, 1, 3)
        v = v.reshape(Bx, Tx, h, d).transpose(0, 2, 1, 3)
        q, k = _apply_rope(q, k)
        idx = jnp.arange(Tx)
        dist = idx[None, :] - idx[:, None]
        allowed = (dist <= 0) & (dist >= -(w - 1))
        scores = jnp.einsum('bhqd,bhkd->bhqk', q, k) / jnp.sqrt(jnp.float32(d))
        scores = jnp.where(allowed[None, None], scores, -jnp.inf)
        weights = jax.nn.softmax(scores, axis=-1)
        out = jnp.einsum('bhqk,bhkd->bhqd', weights, v)
        out = out.transpose(0, 2, 1, 3).reshape(Bx, Tx, C)
        return out @ Wout

    def _L1_ffn_ref(hidden_states, ln_w, ln_b, router_w, gate_w, up_w, down_w, sh_gate, sh_up, sh_down):
        import jax, jax.numpy as jnp
        import numpy as np
        H = 256
        I = 512
        E = 8
        B, S = (2, 1024)
        EPS = 1e-05
        INIT = 0.02

        def _layernorm(x, w, b):
            mu = jnp.mean(x, axis=-1, keepdims=True)
            var = jnp.mean(jnp.square(x - mu), axis=-1, keepdims=True)
            return (x - mu) * jax.lax.rsqrt(var + EPS) * w + b
        b, s, h = hidden_states.shape
        normed = _layernorm(hidden_states, ln_w, ln_b)
        xf = normed.reshape(-1, h)
        logits = xf @ router_w
        top_idx = jnp.argmax(logits, axis=-1)
        top_score = jax.nn.sigmoid(jnp.max(logits, axis=-1))

        def body(acc, ew):
            g, u, d, e = ew
            w = jnp.where(top_idx == e, top_score, 0.0)[:, None]
            xe = xf * w
            hmid = jax.nn.silu(xe @ g) * (xe @ u)
            return (acc + hmid @ d, None)
        routed, _ = jax.lax.scan(body, jnp.zeros_like(xf), (gate_w, up_w, down_w, jnp.arange(E)))
        shared = jax.nn.silu(xf @ sh_gate) * (xf @ sh_up) @ sh_down
        moe_out = (routed + shared).reshape(b, s, h)
        return hidden_states + moe_out
    h = _L0_tok_ref(x, L0_tok_W_proj, L0_tok_b_proj, L0_tok_pos_emb)
    h = _layernorm(h + _L0_attn_ref(h, L0_attn_Wq, L0_attn_Wk, L0_attn_Wv, L0_attn_W1, L0_attn_W2), axis=-1)
    h = _layernorm(h + _L0_ffn_ref(h, L0_ffn_fast_b, L0_ffn_w_fc, L0_ffn_w_proj, L0_ffn_u, L0_ffn_v, L0_ffn_gate), axis=-1)
    h = _layernorm(h + _L1_attn_ref(h, L1_attn_Wqkv, L1_attn_Wout), axis=-1)
    h = _layernorm(h + _L1_ffn_ref(h, L1_ffn_ln_w, L1_ffn_ln_b, L1_ffn_router_w, L1_ffn_gate_w, L1_ffn_up_w, L1_ffn_down_w, L1_ffn_sh_gate, L1_ffn_sh_up, L1_ffn_sh_down), axis=-1)
    return h

_drawn_inputs = setup_inputs


def setup_inputs(seed=0):
    import zlib

    import numpy as np

    out = dict(_drawn_inputs(seed))
    spreads = {'L1_ffn_ln_w': (1.0, 0.6), 'L1_ffn_ln_b': (0.0, 0.8)}
    factors = {'L0_tok_b_proj': 2.716,
     'L0_tok_pos_emb': 2.837,
     'L0_attn_Wq': 8.0,
     'L0_attn_Wk': 8.0,
     'L0_attn_Wv': 4.941,
     'L0_attn_W1': 4.885,
     'L0_attn_W2': 4.867,
     'L0_ffn_fast_b': 8.0,
     'L0_ffn_u': 8.0,
     'L0_ffn_v': 8.0,
     'L1_ffn_router_w': 8.0,
     'L1_ffn_gate_w': 8.0,
     'L1_ffn_up_w': 8.0,
     'L1_ffn_down_w': 8.0,
     'L1_ffn_sh_gate': 4.475,
     'L1_ffn_sh_up': 4.44,
     'L1_ffn_sh_down': 4.443}
    for name, (base, spread) in spreads.items():
        noise = np.random.default_rng([zlib.crc32(name.encode()), seed]).standard_normal(out[name].shape)
        drawn = base * np.exp(spread * noise) if base else spread * noise
        out[name] = jnp.asarray(drawn.astype(out[name].dtype))
    for name, factor in factors.items():
        out[name] = (out[name] * factor).astype(out[name].dtype)
    return out
```

```python
from contextlib import ExitStack

import numpy as np

import concourse.bass as bass
from concourse import mybir

ALU = mybir.AluOpType
ACT = mybir.ActivationFunctionType
F32 = mybir.dt.float32
I32 = mybir.dt.int32
AX = mybir.AxisListType

P = 128
IMAGES = 16
SEQ = 36
TOK = IMAGES * SEQ
HALF = TOK // 2
PAD = 608
D = 256
DC = D // P
PATCH = 768
PC = PATCH // P
HID = 1024
HC = HID // P
HD = 16
RANK = 16
TILE = 96
NT = TOK // TILE
TH = NT // 2
EXPERTS = 8
INNER = 512
IC = INNER // P
EW = 2 * DC * INNER + IC * D
SLOT = 128
SLOTS = (TOK - EXPERTS) // SLOT + EXPERTS
SETS = 4
EPS = 1e-5
GATE0, UP0, DOWN0 = 0, DC * INNER, 2 * DC * INNER

CONST = {}
_at = 0
for _name, _n in (("ident", P), ("cos", SEQ), ("sin", SEQ), ("odd", 2), ("causal", SEQ), ("iota", EXPERTS),
                  ("steps", 5), ("before", EXPERTS * EXPERTS), ("slot", SLOTS), ("tri", TILE), ("ones", P)):
    CONST[_name] = (_at, _n)
    _at += _n
CONSTS = _at


def program(nc, patches, w_patch, patch_bias, pos, qkv0, w1, w2, w_fc, w_proj, u, v, fast_b, gate, qkv1, w_out,
            ln_w, ln_b, ln_w_row, ln_b_row, router, experts, shared, consts, out):
    ctx = ExitStack()
    with ctx:
        def sb(name, shape, dt=F32):
            return ctx.enter_context(nc.sbuf_tensor(name, shape, dt))

        def sem(name):
            return ctx.enter_context(nc.semaphore(name))

        slot_in = nc.dram_tensor("slot_in", (SLOTS * SLOT, D), F32, kind="Internal").ap()
        slot_out = nc.dram_tensor("slot_out", (SLOTS * SLOT, D), F32, kind="Internal").ap()

        ex = sb("ex", [P, EXPERTS * EW])
        sh = sb("sh", [P, EW])

        def under(e, at, *shape):
            n = int(np.prod(shape))
            flat = ex[:, e * EW + at:e * EW + at + n]
            return flat.rearrange("p (a b) -> p a b", a=shape[0])

        wp_sb = under(7, 0, PC, D)
        qkv0_sb = under(7, PC * D, DC, 3 * D)
        w1_sb = under(6, 0, DC, HID)
        w2_sb = under(5, 0, HC, D)
        pat_sb = under(3, 0, PC, TOK)
        fc_nat = under(3, PC * TOK, HC, D)
        proj_nat = under(2, 0, DC, HID)
        LATE = 2
        fcT = sb("fcT", [P, DC, HID])
        projT = sb("projT", [P, HC, D])
        qkv1_sb = sb("qkv1_sb", [P, DC, 3 * D])
        wo_sb = sb("wo_sb", [P, DC, D])
        hT = sb("hT", [P, DC, PAD])
        BIG = DC * PAD + 4 * TOK + 32 * SEQ
        big = sb("big", [P, BIG])
        mid = big[:, 0:HC * TOK].rearrange("p (a b) -> p a b", a=HC)
        qT = big[:, 0:DC * PAD].rearrange("p (a b) -> p a b", a=DC)
        kbd = big[:, DC * PAD:DC * PAD + 4 * TOK].rearrange("p (c h t) -> p c h t", c=DC, h=2)
        pT = big[:, DC * PAD + 4 * TOK:BIG].rearrange("p (t q i) -> p t q i", t=16, q=2)
        vbd = sb("vbd", [P, IMAGES, D])
        soft = sb("soft", [P, 2, 32, 64])
        oT = sb("oT", [P, DC, TOK])
        xT = sb("xT", [P, DC, TOK])
        tm = sb("tm", [P, NT, D])
        cst = sb("cst", [P, CONSTS])
        small = sb("small", [P, 512])
        _s = [0]

        def sm(n):
            a = _s[0]
            _s[0] += n
            return small[:, a:a + n]

        pbias = sb("pbias", [P, DC])
        pos_sb = sb("pos_sb", [P, DC, SEQ])
        u_sb = sb("u_sb", [P, HC, RANK])
        v_sb = sb("v_sb", [P, DC, RANK])
        fb_sb = sb("fb_sb", [RANK, RANK])
        gate_sb = sb("gate_sb", [P, 1])
        uT = under(2, DC * HID, 1, HID)[0:RANK, 0, :]
        t1, t2 = oT[0:RANK, 0, :], oT[0:RANK, 1, :]
        lnw = sb("lnw", [P, DC])
        lnb = sb("lnb", [P, DC])
        router_sb = sb("router_sb", [P, DC, EXPERTS])

        def const(name):
            a, n = CONST[name]
            return cst[:, a:a + n]

        ident, ones = const("ident"), const("ones")
        fc_scale, proj_scale = sm(HC), sm(DC)
        fc_half, fc_nhalf, proj_half, proj_nhalf = sm(HC), sm(HC), sm(DC), sm(DC)
        fc_rs = sm(HC)
        smax, ssum, srec = sm(32), sm(32), sm(32)
        stats, mv, rstd = sm(6 * TH), sm(2 * TH), sm(TH)
        veps = sm(TH)
        mhalf = sm(TH)
        raw = xT[:, :, :].rearrange("p a b -> p (a b)")
        swp = tm[:, :, :].rearrange("p a b -> p (a b)")[:, 0:4 * HALF]
        below = soft[:, :, :, :].rearrange("p a b c -> p (a b c)")[:, 0:2048]
        vflat = vbd[:, :, :].rearrange("p a b -> p (a b)")
        xn = vflat[:, 0:NT * D].rearrange("p (a b) -> p a b", a=NT)
        xe = vflat[:, NT * D:2 * NT * D].rearrange("p (a b) -> p a b", a=NT)
        lnw_row = vflat[:, 2 * NT * D:2 * NT * D + D]
        lnb_row = vflat[:, 2 * NT * D + D:2 * NT * D + 2 * D]
        sflat = soft[:, :, :, :].rearrange("p a b c -> p (a b c)")
        slot_x = sflat[:, 0:SLOTS * D].rearrange("p (a b) -> p a b", a=SLOTS)
        xsT = sflat[:, SLOTS * D:SLOTS * D + 2 * DC * SLOT].rearrange("p (n c t) -> p n c t", n=2, c=DC)
        bflat = big
        shmid = bflat[:, 0:IC * TOK].rearrange("p (a b) -> p a b", a=IC)
        _b = IC * TOK
        th = bflat[:, _b:_b + 2 * INNER].rearrange("p (n a) -> p n a", n=2)
        hm = th
        hmT = oT[:, :, :].rearrange("p a b -> p (a b)")[:, 0:2 * INNER].rearrange("p (n c t) -> p n c t", n=2, c=IC)
        yout = bflat[:, _b + 2 * INNER:_b + 2 * INNER + 2 * D].rearrange("p (n d) -> p n d", n=2)
        zero = fcT[:, 0, 0:D]
        yt = fcT[:, :, :].rearrange("p a b -> p (a b)")[:, 256:256 + NT * D].rearrange("p (a b) -> p a b", a=NT)
        fin = projT[:, :, :].rearrange("p a b -> p (a b)")[:, 0:NT * D].rearrange("p (a b) -> p a b", a=NT)
        lg, gt8, ohot, tmp8 = sm(48), sm(48), sm(48), sm(48)
        lmax, eidx, score, posf = sm(NT), sm(NT), sm(NT), sm(NT)
        cnt, nslot, sstart, send = sm(8), sm(8), sm(8), sm(8)
        eslot = sm(SLOTS)
        posi = sb("posi", [P, NT], I32)
        eint = sb("eint", [P, SLOTS], I32)
        wk = sb("wk", [P, SLOTS * EXPERTS])

        ps = ctx.enter_context(nc.psum_tensor("ps", [P, 8, 512], F32))

        def bank(i):
            return ps[:, i, :]

        L = {n: sem("in_" + n) for n in (
            "patches0", "patches1", "patches2", "patches3", "patches4", "patches5", "wp", "small", "consts", "qkv0",
            "w1", "w2", "fc", "proj", "qkv1", "wo", "shared", "rows")}
        in_ex = [sem(f"in_ex{e}") for e in range(EXPERTS)]
        dve_step = sem("dve_step")
        pool_step = sem("pool_step")
        embedded = sem("embedded")
        h_ready = sem("h_ready")
        pads_zero = sem("pads_zero")
        qk_done = sem("qk_done")
        raw_out = sem("raw_out")
        swapped = sem("swapped")
        cos_done = sem("cos_done")
        sin_done = sem("sin_done")
        roped = sem("roped")
        k_ready = sem("k_ready")
        v_done = sem("v_done")
        v_out = sem("v_out")
        s_done = sem("s_done")
        s_out = sem("s_out")
        s_sub = sem("s_sub")
        s_exp = sem("s_exp")
        p_ready = sem("p_ready")
        pt_done = sem("pt_done")
        pt_out = sem("pt_out")
        o_done = sem("o_done")
        o_out = sem("o_out")
        up_done = sem("up_done")
        up_act = sem("up_act")
        mid_ready = sem("mid_ready")
        down_done = sem("down_done")
        x_ready = sem("x_ready")
        tm_done = sem("tm_done")
        var_ready = sem("var_ready")
        rstd_ready = sem("rstd_ready")
        tm_ready = sem("tm_ready")
        fm_done = sem("fm_done")
        tern_ready = sem("tern_ready")
        half_const = sem("half_const")
        tern_done = sem("tern_done")
        tern_out = sem("tern_out")
        u_ready = sem("u_ready")
        r_done = sem("r_done")
        r_out = sem("r_out")
        vb_zero = sem("vb_zero")
        vb_free = sem("vb_free")
        sh_act = sem("sh_act")
        nf_ready = sem("nf_ready")
        route_done = sem("route_done")
        route_s = sem("route_s")
        score_t = sem("score_t")
        pos_ready = sem("pos_ready")
        xe_ready = sem("xe_ready")
        zero_ready = sem("zero_ready")
        slots_zero = sem("slots_zero")
        scattered = sem("scattered")
        slot_ld = [sem(f"slot_ld{s}") for s in range(SLOTS)]
        xs_done, xs_out = sem("xs_done"), sem("xs_out")
        gu_done, th_done, hm_ready = sem("gu_done"), sem("th_done"), sem("hm_ready")
        g_half = sem("g_half")
        hmT_done, hmT_out = sem("hmT_done"), sem("hmT_out")
        y_done, y_out = sem("y_done"), sem("y_out")
        y_st = [sem(f"y_st{i}") for i in range(2)]
        y_back = [sem(f"y_back{t}") for t in range(NT)]
        shdown_done, base_ready = sem("shdown_done"), sem("base_ready")
        fin_ready = sem("fin_ready")
        s_out_dma = sem("s_out_dma")

        def cols(H):
            return slice(H * HALF, (H + 1) * HALF)

        block = ctx.enter_context(nc.Block())

        def h_at(stage, H):
            return 4 * stage + 2 * H + 2

        @block.sync
        def _(sp):
            for k in range(PC):
                sp.dma_start(pat_sb[:, k, :], patches[k]).then_inc(L[f"patches{k}"], 16)
                if k == 0:
                    sp.dma_start(wp_sb, w_patch).then_inc(L["wp"], 16)
            for dst, src in ((pbias[:], patch_bias), (pos_sb[:], pos), (u_sb[:], u), (v_sb[:], v), (fb_sb[:], fast_b),
                             (gate_sb[:], gate), (lnw[:], ln_w), (lnb[:], ln_b), (router_sb[:], router)):
                sp.dma_start(dst, src).then_inc(L["small"], 16)
            sp.dma_start(cst[:], consts).then_inc(L["consts"], 16)
            sp.dma_start(qkv0_sb, qkv0).then_inc(L["qkv0"], 16)
            sp.dma_start(fc_nat, w_fc).then_inc(L["fc"], 16)
            sp.dma_start(proj_nat, w_proj).then_inc(L["proj"], 16)
            sp.dma_start(w1_sb, w1).then_inc(L["w1"], 16)
            sp.dma_start(w2_sb, w2).then_inc(L["w2"], 16)
            sp.dma_start(qkv1_sb[:], qkv1).then_inc(L["qkv1"], 16)
            sp.dma_start(wo_sb[:], w_out).then_inc(L["wo"], 16)
            sp.dma_start(sh[:], shared).then_inc(L["shared"], 16)
            for e in range(EXPERTS):
                if e == LATE:
                    sp.wait_ge(down_done, 8)
                sp.dma_start(ex[:, e * EW:(e + 1) * EW], experts[e]).then_inc(in_ex[e], 16)
            sp.wait_ge(o_done, 2 * SETS)
            sp.dma_start(lnw_row[0:TILE, :], ln_w_row).then_inc(L["rows"], 16)
            sp.dma_start(lnb_row[0:TILE, :], ln_b_row).then_inc(L["rows"], 16)
            sp.wait_ge(zero_ready, 1)
            for s in range(SLOTS):
                sp.dma_start(slot_in[s * SLOT:(s + 1) * SLOT, :], zero).then_inc(slots_zero, 16)
            sp.wait_ge(scattered, 16 * NT)
            for s in range(SLOTS):
                sp.dma_start(slot_x[:, s, :], slot_in[s * SLOT:(s + 1) * SLOT, :]).then_inc(slot_ld[s], 16)
            for s in range(SLOTS):
                sp.wait_ge(y_out, s + 1)
                sp.dma_start(slot_out[s * SLOT:(s + 1) * SLOT, :], yout[:, s % 2, :]).then_inc(y_st[s % 2], 16)
            for t in range(NT):
                sp.wait_ge(fin_ready, t + 1)
                sp.dma_start(out[t * TILE:(t + 1) * TILE, :], fin[0:TILE, t, :]).then_inc(s_out_dma, 16)
            sp.wait_ge(s_out_dma, 16 * NT)

        @block.gpsimd
        def _(pool):
            nc.gpsimd.memset(hT[:, :, TOK:PAD], 0.0).then_inc(pads_zero, 1)
            nc.gpsimd.memset(qT[:, :, TOK:PAD], 0.0).then_inc(pads_zero, 1)
            nc.gpsimd.memset(vbd[:, :, :], 0.0).then_inc(vb_zero, 1)
            nc.gpsimd.memset(mhalf, -0.5).then_inc(half_const, 1)
            pool.wait_ge(half_const, 1)

            def rope(layer):
                for H in range(2):
                    n = 2 * layer + H
                    r4 = raw.rearrange("p (a t) -> p a t", t=SEQ)
                    pool.wait_ge(L["consts"], 16)
                    pool.wait_ge(swapped, n + 1)
                    nc.gpsimd.tensor_tensor(r4, r4, const("cos").unsqueeze(1).to_broadcast([P, 32, SEQ]),
                                            ALU.mult).then_inc(cos_done, 1)
                    pool.wait_ge(cos_done, n + 1)
                    pool.wait_ge(sin_done, n + 1)
                    if layer and H == 0:
                        pool.wait_ge(down_done, 8)
                    q2 = raw[:, 0:2 * HALF].rearrange("p (a t) -> p a t", a=2)
                    s2 = swp[:, 0:2 * HALF].rearrange("p (a t) -> p a t", a=2)
                    nc.gpsimd.tensor_tensor(qT[:, :, cols(H)], q2, s2, ALU.add).then_inc(roped, 1)
                    nc.gpsimd.tensor_tensor(raw[:, 2 * HALF:4 * HALF], raw[:, 2 * HALF:4 * HALF],
                                            swp[:, 2 * HALF:4 * HALF], ALU.add).then_inc(roped, 1)

            def rsqrt(n):
                pool.wait_ge(var_ready, n + 1)
                if n:
                    pool.wait_ge(tm_ready, n)
                nc.gpsimd.tensor_tensor(rstd[0:TILE, :], veps[0:TILE, :], mhalf[0:TILE, :],
                                        ALU.pow).then_inc(rstd_ready, 1)

            rope(0)
            pool.wait_ge(tern_ready, 2)
            nc.gpsimd.memset(soft[:, :, :, SEQ:64], 0.0).then_inc(vb_zero, 1)
            for n in range(4):
                rsqrt(n)
            pool.wait_ge(down_done, 8)
            nc.gpsimd.memset(qT[:, :, TOK:PAD], 0.0).then_inc(pads_zero, 1)
            rope(1)
            nc.gpsimd.memset(zero, 0.0).then_inc(zero_ready, 1)
            for n in range(4, 8):
                rsqrt(n)
            pool.wait_ge(slots_zero, 16 * SLOTS)
            for t in range(NT):
                pool.wait_ge(pos_ready, 1)
                pool.wait_ge(xe_ready, t + 1)
                pool.indirect_dma_start(slot_in, bass.IndirectOffsetOnAxis(ap=posi[0:TILE, t:t + 1], axis=0),
                                        xe[0:TILE, t, :], None).then_inc(scattered, 16)
            pool.wait_ge(y_st[0], 16 * (SLOTS // 2))
            pool.wait_ge(y_st[1], 16 * (SLOTS // 2))
            for t in range(NT):
                pool.indirect_dma_start(yt[0:TILE, t, :], None, slot_out,
                                        bass.IndirectOffsetOnAxis(ap=posi[0:TILE, t:t + 1], axis=0)
                                        ).then_inc(y_back[t], 16)
            for n in range(8, 10):
                rsqrt(n)

        @block.scalar
        def _(act):
            def rope_in(layer, H):
                n = 2 * layer + H
                if n:
                    act.wait_ge(roped, 2 * n)
                    act.wait_ge(k_ready, n)
                for i in range(4):
                    act.wait_ge(qk_done, 4 * n + i + 1)
                    nc.scalar.activation(raw[:, i * HALF:(i + 1) * HALF], ps[:, i, 0:HALF], ACT.Copy,
                                         scale=0.25 if i < 2 else 1.0).then_inc(raw_out, 1)

            def v_in(layer):
                if layer == 0:
                    act.wait_ge(vb_zero, 1)
                for n in range(4):
                    act.wait_ge(v_done, 4 * layer + n + 1)
                    for q in range(2):
                        for hh in range(2):
                            src = ps[64 * q:64 * q + SEQ, 4 + n, :].rearrange("p (r b c) -> p r b c", r=2, b=8)
                            dst = vbd[64 * hh:64 * hh + SEQ, 4 * n + q:4 * n + q + 3:2, :].rearrange(
                                "p r (b c) -> p r b c", b=8)
                            last = nc.scalar.activation(dst[:, :, :, HD * hh:HD * hh + HD],
                                                        src[:, :, :, HD * hh:HD * hh + HD], ACT.Copy)
                    last.then_inc(v_out, 1)

            def softmax_exp(n):
                act.wait_ge(s_sub, n + 1)
                x = soft[:, n % 2, :, 0:SEQ]
                nc.scalar.activation(x, x, ACT.Exp).then_inc(s_exp, 1)

            def attn_out(n):
                for r in range(4):
                    act.wait_ge(pt_done, 4 * n + r + 1)
                    if r == 0 and n:
                        act.wait_ge(o_done, n)
                    src = ps[:, 4 + r % 2, :].rearrange("p (t q i) -> p t q i", t=4, q=2)[:, :, :, 0:SEQ]
                    nc.scalar.activation(pT[:, 4 * r:4 * r + 4, :, :], src, ACT.Copy).then_inc(pt_out, 1)
                act.wait_ge(o_done, n + 1)
                s = n % SETS
                nc.scalar.activation(oT[:, :, s * 4 * SEQ:(s + 1) * 4 * SEQ],
                                     ps[:, 6 + n % 2, 0:8 * SEQ].rearrange("p (c t) -> p c t", c=DC),
                                     ACT.Copy).then_inc(o_out, 1)

            def attention(layer):
                rope_in(layer, 0)
                rope_in(layer, 1)
                v_in(layer)
                n0 = SETS * layer
                softmax_exp(n0)
                for s in range(SETS):
                    if s < SETS - 1:
                        softmax_exp(n0 + s + 1)
                    attn_out(n0 + s)

            attention(0)
            for i in range(2 * HC):
                act.wait_ge(up_done, i + 1)
                nc.scalar.activation(mid[:, i % HC, cols(i // HC)], ps[:, i % 4, 0:HALF], ACT.Tanh,
                                     scale=0.5).then_inc(up_act, 1)
            for r in range(8):
                act.wait_ge(tern_done, r + 1)
                if r < 4:
                    dst = fcT[:, r // 2, (r % 2) * 512:(r % 2) * 512 + 512]
                else:
                    dst = projT[:, 2 * (r - 4):2 * (r - 4) + 2, :].rearrange("p a b -> p (a b)")
                nc.scalar.activation(dst, bank(r % 4), ACT.Copy).then_inc(tern_out, 1)
            for r in range(2):
                act.wait_ge(r_done, r + 1)
                nc.scalar.activation(uT[:, r * 512:(r + 1) * 512], ps[0:RANK, r, :], ACT.Copy).then_inc(r_out, 1)
            for H in range(2):
                act.wait_ge(r_done, 3 + 2 * H)
                nc.scalar.activation(t1[:, cols(H)], ps[0:RANK, 2, 0:HALF], ACT.Copy).then_inc(r_out, 1)
                act.wait_ge(r_done, 4 + 2 * H)
                nc.scalar.activation(t2[:, cols(H)], ps[0:RANK, 3, 0:HALF], ACT.Copy).then_inc(r_out, 1)
                for i in range(HC * H, HC * H + HC):
                    act.wait_ge(up_done, 2 * HC + i + 1)
                    nc.scalar.activation(mid[:, i % HC, cols(H)], ps[:, i % 4, 0:HALF], ACT.Relu,
                                         scale=fc_scale[:, i % HC:i % HC + 1]).then_inc(up_act, 1)
                    act.wait_ge(up_act, 2 * HC + i + 1)
                    nc.scalar.activation(mid[:, i % HC, cols(H)], mid[:, i % HC, cols(H)],
                                         ACT.Square).then_inc(mid_ready, 1)
            attention(1)
            act.wait_ge(route_s, 1)
            nc.scalar.activation(score[0:TILE, :], lmax[0:TILE, :], ACT.Tanh, scale=0.5).then_inc(score_t, 1)
            for i in range(2 * IC):
                act.wait_ge(up_done, 4 * HC + 2 * i + 1)
                nc.scalar.activation(shmid[:, i % IC, cols(i // IC)], ps[:, 2 * (i % 2), 0:HALF], ACT.Tanh,
                                     scale=0.5).then_inc(sh_act, 1)
            for s in range(SLOTS):
                act.wait_ge(xs_done, s + 1)
                if s >= 2:
                    act.wait_ge(gu_done, s - 1)
                nc.scalar.activation(xsT[:, s % 2, :, :], bank(0)[:, 0:2 * SLOT].rearrange("p (c t) -> p c t", c=DC),
                                     ACT.Copy).then_inc(xs_out, 1)
                act.wait_ge(gu_done, s + 1)
                if s >= 2:
                    act.wait_ge(hmT_done, s - 1)
                nc.scalar.activation(th[:, s % 2, :], bank(1 + 2 * (s % 2)), ACT.Tanh, scale=0.5).then_inc(th_done, 1)
                act.wait_ge(hmT_done, s + 1)
                if s >= 2:
                    act.wait_ge(y_done, s - 1)
                nc.scalar.activation(hmT[:, s % 2, :, :], bank(5).rearrange("p (c t) -> p c t", c=IC),
                                     ACT.Copy).then_inc(hmT_out, 1)
                act.wait_ge(y_done, s + 1)
                if s >= 2:
                    act.wait_ge(y_st[s % 2], 16 * (s // 2))
                nc.scalar.activation(yout[:, s % 2, :], bank(6)[:, 0:D], ACT.Copy).then_inc(y_out, 1)

        @block.vector
        def _(dve):
            chain = [0]

            def link(ins):
                chain[0] += 1
                ins.then_inc(dve_step, 1)
                dve.wait_ge(dve_step, chain[0])

            V = nc.vector
            dve.wait_ge(L["small"], 16 * 9)
            for i in range(4):
                H, m = i // 2, i % 2
                dve.wait_ge(embedded, i + 1)
                V.scalar_tensor_tensor(
                    hT[:, m, cols(H)].rearrange("p (b t) -> p b t", t=SEQ),
                    ps[:, i, 0:HALF].rearrange("p (b t) -> p b t", t=SEQ), pbias[:, m:m + 1],
                    pos_sb[:, m, :].unsqueeze(1).to_broadcast([P, 8, SEQ]), ALU.add, ALU.add).then_inc(h_ready, 1)

            def ternary(nat, half, nhalf, scale, blocks, name):
                n = nat.shape[2]
                dve.wait_ge(L[name], 16)
                link(V.tensor_reduce(scale, nat, AX.X, ALU.add, apply_absolute_value=True))
                link(V.tensor_scalar(scale, scale, 1.0 / n, 1e-5, ALU.mult, ALU.max))
                V.tensor_scalar(half, scale, 0.5, None, ALU.mult)
                link(V.tensor_scalar(nhalf, scale, -0.5, None, ALU.mult))
                for b in range(blocks):
                    V.tensor_scalar(below[:, b * n:(b + 1) * n], nat[:, b, :], nhalf[:, b:b + 1], None, ALU.is_lt)
                link(V.tensor_scalar(small[:, 508:509], scale[:, 0:1], 1.0, None, ALU.mult))
                for b in range(blocks):
                    last = V.scalar_tensor_tensor(nat[:, b, :], nat[:, b, :], half[:, b:b + 1],
                                                  below[:, b * n:(b + 1) * n], ALU.is_gt, ALU.subtract)
                last.then_inc(tern_ready, 1)

            def rope_mid(layer, H):
                n = 2 * layer + H
                dve.wait_ge(raw_out, 4 * n + 4)
                if n:
                    dve.wait_ge(roped, 2 * n)
                V.stream_shuffle(swp, raw[:, 0:4 * HALF], [(i // HD) * HD + (i + HD // 2) % HD for i in range(32)]
                                 ).then_inc(swapped, 1)
                dve.wait_ge(swapped, n + 1)
                s4 = swp.rearrange("p (a t) -> p a t", t=SEQ)
                dve.wait_ge(L["consts"], 16)
                V.tensor_tensor(s4, s4, const("sin").unsqueeze(1).to_broadcast([P, 32, SEQ]),
                                ALU.mult).then_inc(sin_done, 1)

            def rope_k(layer, H):
                n = 2 * layer + H
                dve.wait_ge(roped, 2 * n + 2)
                for hh in range(2):
                    last = V.tensor_scalar(kbd[:, :, hh, cols(H)],
                                           raw[:, 2 * HALF:4 * HALF].rearrange("p (c t) -> p c t", c=DC),
                                           const("odd")[:, hh:hh + 1], None, ALU.mult)
                last.then_inc(k_ready, 1)

            def scores_in(n):
                dve.wait_ge(s_done, n + 1)
                if n >= 2:
                    dve.wait_ge(pt_done, 4 * (n - 1))
                if n % SETS == 0:
                    dve.wait_ge(vb_zero, 2)
                src = ps[:, 0:4, 0:8 * SEQ].rearrange("p g (s j) -> p g s j", j=SEQ)
                dst = soft[:, n % 2, :, 0:SEQ].rearrange("p (g s) j -> p g s j", g=4)
                mask = const("causal").unsqueeze(1).unsqueeze(1).to_broadcast([P, 4, 8, SEQ])
                V.tensor_tensor(dst, src, mask, ALU.add).then_inc(s_out, 1)

            def scores_max(n):
                x = soft[:, n % 2, :, 0:SEQ]
                dve.wait_ge(s_out, n + 1)
                link(V.tensor_reduce(smax, x, AX.X, ALU.max))
                V.tensor_tensor(x, x, smax.unsqueeze(2).to_broadcast([P, 32, SEQ]), ALU.subtract).then_inc(s_sub, 1)

            def scores_norm(n):
                x = soft[:, n % 2, :, 0:SEQ]
                dve.wait_ge(s_exp, n + 1)
                link(V.tensor_reduce(ssum, x, AX.X, ALU.add))
                link(V.reciprocal(srec, ssum))
                V.tensor_tensor(x, x, srec.unsqueeze(2).to_broadcast([P, 32, SEQ]), ALU.mult).then_inc(p_ready, 1)

            def attention(layer):
                rope_mid(layer, 0)
                rope_k(layer, 0)
                rope_mid(layer, 1)
                rope_k(layer, 1)
                n0 = SETS * layer
                scores_in(n0)
                scores_max(n0)
                for s in range(SETS):
                    if s < SETS - 1:
                        scores_in(n0 + s + 1)
                        scores_max(n0 + s + 1)
                    scores_norm(n0 + s)

            def residual(n, H, scale=None):
                for m in range(2):
                    dve.wait_ge(down_done, 4 * n + 2 * H + m + 1)
                    s = 1.0 if scale is None else scale(m)
                    V.scalar_tensor_tensor(xT[:, m, cols(H)], ps[:, 4 + 2 * H + m, 0:HALF], s, hT[:, m, cols(H)],
                                           ALU.mult, ALU.add).then_inc(x_ready, 1)

            def moments(src, n):
                for t in range(TH):
                    V.bn_stats(stats[0:TILE, 6 * t:6 * t + 6], src(t))
                link(V.tensor_scalar(small[:, 508:509], small[:, 509:510], 0.0, None, ALU.mult))
                for t in range(TH):
                    last = V.bn_aggr(mv[0:TILE, 2 * t:2 * t + 2], stats[0:TILE, 6 * t:6 * t + 6])
                link(last)
                V.tensor_scalar(veps[0:TILE, :], mv[0:TILE, 1:2 * TH:2], EPS, None, ALU.add).then_inc(var_ready, 1)
                dve.wait_ge(rstd_ready, n + 1)

            def normalize(dst, src, t):
                return V.tensor_scalar(dst, src, mv[0:TILE, 2 * t:2 * t + 1], rstd[0:TILE, t:t + 1],
                                       ALU.subtract, ALU.mult)

            def norm(n, H):
                dve.wait_ge(tm_done, 2 * n + H + 1)
                if n:
                    dve.wait_ge(fm_done, 4 * (n - 1) + 2 * H + 2)

                def rows(t):
                    return ps[0:TILE, 2 * H + t // 2, (t % 2) * D:(t % 2) * D + D]

                moments(rows, 2 * n + H)
                for t in range(TH):
                    last = normalize(tm[0:TILE, TH * H + t, :], rows(t), t)
                last.then_inc(tm_ready, 1)

            def feature_major(n, H):
                for m in range(2):
                    dve.wait_ge(fm_done, 4 * n + 2 * H + m + 1)
                    V.tensor_copy(hT[:, m, cols(H)], ps[:, 4 + 2 * H + m, 0:HALF]).then_inc(h_ready, 1)

            V.memset(small[:, 500:512], 0.0)
            ternary(fc_nat, fc_half, fc_nhalf, fc_scale, HC, "fc")
            ternary(proj_nat, proj_half, proj_nhalf, proj_scale, DC, "proj")
            link(V.reciprocal(fc_rs, fc_scale))
            link(V.tensor_scalar(fc_rs, fc_rs, gate_sb[:, 0:1], None, ALU.mult))
            V.tensor_tensor(u_sb[:], u_sb[:], fc_rs.unsqueeze(2).to_broadcast([P, HC, RANK]),
                            ALU.mult).then_inc(u_ready, 1)
            attention(0)
            for i in range(2 * HC):
                dve.wait_ge(up_act, i + 1)
                m = mid[:, i % HC, cols(i // HC)]
                V.scalar_tensor_tensor(m, m, 1.0, ps[:, i % 4, 0:HALF], ALU.add, ALU.mult).then_inc(mid_ready, 1)
            residual(0, 0, lambda m: 0.5)
            residual(0, 1, lambda m: 0.5)
            norm(0, 0)
            norm(0, 1)
            feature_major(0, 0)
            feature_major(0, 1)
            residual(1, 0, lambda m: proj_scale[:, m:m + 1])
            residual(1, 1, lambda m: proj_scale[:, m:m + 1])
            norm(1, 0)
            norm(1, 1)
            feature_major(1, 0)
            feature_major(1, 1)
            attention(1)
            residual(2, 0)
            residual(2, 1)
            norm(2, 0)
            norm(2, 1)
            for H in range(2):
                dve.wait_ge(tm_ready, 5 + H)
                if H == 0:
                    dve.wait_ge(o_done, 2 * SETS)
                moments(lambda t: tm[0:TILE, TH * H + t, :], 6 + H)
                for t in range(TH):
                    last = normalize(xn[0:TILE, TH * H + t, :], tm[0:TILE, TH * H + t, :], t)
                last.then_inc(tm_ready, 1)
            for H in range(2):
                for m in range(2):
                    dve.wait_ge(fm_done, 8 + 2 * H + m + 1)
                    V.tensor_scalar(hT[:, m, cols(H)], ps[:, 4 + 2 * H + m, 0:HALF], lnw[:, m:m + 1], lnb[:, m:m + 1],
                                    ALU.mult, ALU.add).then_inc(h_ready, 1)

            T8 = [TILE, NT, EXPERTS]

            def t8(a):
                return a[0:TILE, :].rearrange("p (t e) -> p t e", e=EXPERTS)

            iota = const("iota")[0:TILE, :].unsqueeze(1).to_broadcast(T8)
            dve.wait_ge(route_done, 1)
            link(V.tensor_copy(lg[0:TILE, :], ps[0:TILE, 0, 0:NT * EXPERTS]))
            V.tensor_reduce(lmax[0:TILE, :], t8(lg), AX.X, ALU.max).then_inc(route_s, 1)
            dve.wait_ge(route_s, 1)
            link(V.tensor_tensor(t8(gt8), t8(lg), lmax[0:TILE, :].unsqueeze(2).to_broadcast(T8), ALU.is_lt))
            link(V.scalar_tensor_tensor(t8(gt8), t8(gt8), float(EXPERTS), iota, ALU.mult, ALU.add))
            link(V.tensor_reduce(eidx[0:TILE, :], t8(gt8), AX.X, ALU.min))
            V.tensor_tensor(t8(ohot), iota, eidx[0:TILE, :].unsqueeze(2).to_broadcast(T8),
                            ALU.is_equal).then_inc(route_s, 1)
            dve.wait_ge(score_t, 1)
            link(V.tensor_scalar(score[0:TILE, :], score[0:TILE, :], 1.0, 0.5, ALU.add, ALU.mult))
            dve.wait_ge(L["rows"], 32)
            dve.wait_ge(tm_ready, 8)
            B6 = [TILE, NT, D]
            link(V.tensor_tensor(xe[0:TILE], xn[0:TILE], lnw_row[0:TILE, :].unsqueeze(1).to_broadcast(B6), ALU.mult))
            link(V.tensor_tensor(xe[0:TILE], xe[0:TILE], lnb_row[0:TILE, :].unsqueeze(1).to_broadcast(B6), ALU.add))
            for t in range(NT):
                V.tensor_scalar(xe[0:TILE, t, :], xe[0:TILE, t, :], score[0:TILE, t:t + 1], None,
                                ALU.mult).then_inc(xe_ready, 1)
            dve.wait_ge(route_done, 2)
            link(V.tensor_copy(cnt, ps[:, 2, 0:EXPERTS]))
            w5 = wk[:, 0:5 * EXPERTS].rearrange("p (e k) -> p e k", k=5)
            link(V.tensor_tensor(w5, cnt.unsqueeze(2).to_broadcast([P, EXPERTS, 5]),
                                 const("steps").unsqueeze(1).to_broadcast([P, EXPERTS, 5]), ALU.is_gt))
            link(V.tensor_reduce(nslot, w5, AX.X, ALU.add))
            w8 = wk[:, 0:EXPERTS * EXPERTS].rearrange("p (e k) -> p e k", k=EXPERTS)
            link(V.tensor_tensor(w8, nslot.unsqueeze(1).to_broadcast([P, EXPERTS, EXPERTS]),
                                 const("before").rearrange("p (e k) -> p e k", k=EXPERTS), ALU.mult))
            link(V.tensor_reduce(sstart, w8, AX.X, ALU.add))
            link(V.tensor_tensor(send, sstart, nslot, ALU.add))
            link(V.scalar_tensor_tensor(t8(tmp8), sstart[0:TILE, :].unsqueeze(1).to_broadcast(T8), float(SLOT),
                                        ps[0:TILE, 1, 0:NT * EXPERTS].rearrange("p (t e) -> p t e", e=EXPERTS),
                                        ALU.mult, ALU.add))
            link(V.tensor_tensor(tmp8[0:TILE, :], tmp8[0:TILE, :], ohot[0:TILE, :], ALU.mult))
            link(V.tensor_reduce(posf[0:TILE, :], t8(tmp8), AX.X, ALU.add))
            V.tensor_copy(posi[0:TILE, :], posf[0:TILE, :]).then_inc(pos_ready, 1)
            ws = wk[:, :].rearrange("p (s e) -> p s e", e=EXPERTS)
            link(V.tensor_tensor(ws, const("slot").unsqueeze(2).to_broadcast([P, SLOTS, EXPERTS]),
                                 send.unsqueeze(1).to_broadcast([P, SLOTS, EXPERTS]), ALU.is_ge))
            link(V.tensor_reduce(eslot, ws, AX.X, ALU.add))
            link(V.tensor_scalar(eslot, eslot, float(EXPERTS - 1), None, ALU.min))
            V.tensor_copy(eint[:, :], eslot).then_inc(pos_ready, 1)

            for i in range(2 * IC):
                dve.wait_ge(sh_act, i + 1)
                m = shmid[:, i % IC, cols(i // IC)]
                link(V.scalar_tensor_tensor(m, m, 1.0, ps[:, 2 * (i % 2), 0:HALF], ALU.add, ALU.mult))
                dve.wait_ge(up_done, 4 * HC + 2 * i + 2)
                V.scalar_tensor_tensor(m, m, 0.5, ps[:, 2 * (i % 2) + 1, 0:HALF], ALU.mult,
                                       ALU.mult).then_inc(mid_ready, 1)
            for t in range(NT):
                dve.wait_ge(shdown_done, t + 1)
                V.scalar_tensor_tensor(tm[0:TILE, t, :], tm[0:TILE, t, :], 2.0, ps[0:TILE, 4 + t % 4, 0:D], ALU.mult,
                                       ALU.add).then_inc(base_ready, 1)
            for s in range(SLOTS):
                dve.wait_ge(th_done, s + 1)
                h = hm[:, s % 2, :]
                V.scalar_tensor_tensor(h, h, 1.0, bank(1 + 2 * (s % 2)), ALU.add, ALU.mult).then_inc(g_half, 1)
                dve.wait_ge(g_half, s + 1)
                V.scalar_tensor_tensor(h, h, 0.5, bank(2 + 2 * (s % 2)), ALU.mult, ALU.mult).then_inc(hm_ready, 1)
            dve.wait_ge(base_ready, NT)
            for t in range(NT):
                dve.wait_ge(y_back[t], 16)
                last = V.tensor_tensor(yt[0:TILE, t, :], yt[0:TILE, t, :], tm[0:TILE, t, :], ALU.add)
            link(last)
            for H in range(2):
                moments(lambda t: yt[0:TILE, TH * H + t, :], 8 + H)
                for t in range(TH):
                    last = normalize(fin[0:TILE, TH * H + t, :], yt[0:TILE, TH * H + t, :], t)
                    last.then_inc(fin_ready, 1)
                V.tensor_scalar(small[:, 508:509], small[:, 509:510], 0.0, None, ALU.mult).then_inc(tm_ready, 1)
                dve.wait_ge(tm_ready, 9 + H)

        @block.tensor
        def _(pe):
            mm, tr = nc.tensor.matmul, nc.tensor.transpose
            pe.wait_ge(L["wp"], 16)
            for k in range(PC):
                pe.wait_ge(L[f"patches{k}"], 16)
                for i in range(4):
                    H, m = i // 2, i % 2
                    last = mm(ps[:, i, 0:HALF], wp_sb[:, k, m * P:(m + 1) * P], pat_sb[:, k, cols(H)],
                              start=(k == 0), stop=(k == PC - 1))
                    if k == PC - 1:
                        last.then_inc(embedded, 1)

            def projections(layer, w, stage):
                for H in range(2):
                    pe.wait_ge(h_ready, h_at(stage, H))
                    if H:
                        pe.wait_ge(raw_out, 4 * (2 * layer + 1))
                    for i in range(4):
                        for k in range(DC):
                            last = mm(ps[:, i, 0:HALF], w[:, k, i * P:(i + 1) * P], hT[:, k, cols(H)],
                                      start=(k == 0), stop=(k == DC - 1))
                        last.then_inc(qk_done, 1)
                pe.wait_ge(h_ready, h_at(stage, 1))
                for n in range(4):
                    for r in range(2):
                        for q in range(2):
                            b = 4 * n + 2 * r + q
                            for k in range(DC):
                                last = mm(ps[64 * q:64 * q + SEQ, 4 + n, r * D:(r + 1) * D],
                                          hT[:, k, SEQ * b:SEQ * b + SEQ], w[:, k, 2 * D:3 * D],
                                          start=(k == 0), stop=(k == DC - 1))
                    last.then_inc(v_done, 1)

            def scores(n):
                s = n % SETS
                if n % SETS:
                    pe.wait_ge(s_out, n)
                for r in range(2):
                    for q in range(2):
                        b = 4 * s + 2 * r + q
                        for c in range(DC):
                            for g in range(4):
                                at = (2 * r + c) * 2 * SEQ
                                last = mm(ps[64 * q:64 * q + 64, g, at:at + 2 * SEQ],
                                          qT[32 * g:32 * g + 32, c, SEQ * b:SEQ * b + 64],
                                          kbd[32 * g:32 * g + 32, c, :, SEQ * b:SEQ * b + SEQ],
                                          start=True, stop=True)
                last.then_inc(s_done, 1)

            def values(n, layer):
                s = n % SETS
                pe.wait_ge(p_ready, n + 1)
                for r in range(4):
                    if 4 * n + r >= 2:
                        pe.wait_ge(pt_out, 4 * n + r - 1)
                    for j in range(4):
                        t = 4 * r + j
                        last = tr(ps[:, 4 + r % 2, j * P:(j + 1) * P],
                                  soft[:, n % 2, 2 * t:2 * t + 2, :].rearrange("p a b -> p (a b)"), ident)
                    last.then_inc(pt_done, 1)
                pe.wait_ge(pt_out, 4 * n + 4)
                if n >= 2:
                    pe.wait_ge(o_out, n - 1)
                for r in range(2):
                    for q in range(2):
                        for c in range(DC):
                            for g in range(4):
                                t = 4 * g + 2 * r + c
                                at = c * 4 * SEQ + (2 * r + q) * SEQ
                                b = 4 * s + 2 * r + q
                                last = mm(ps[32 * g:32 * g + 32, 6 + n % 2, at:at + SEQ],
                                          vbd[:, b, (4 * c + g) * 32:(4 * c + g) * 32 + 32],
                                          pT[:, t, q, :], start=True, stop=True)
                last.then_inc(o_done, 1)

            def attention(layer, w, stage):
                projections(layer, w, stage)
                n0 = SETS * layer
                pe.wait_ge(roped, 4 * layer + 4)
                pe.wait_ge(k_ready, 2 * layer + 2)
                pe.wait_ge(raw_out, 8 * layer + 8)
                pe.wait_ge(pads_zero, 2 + layer)
                scores(n0)
                pe.wait_ge(v_out, 4 * layer + 4)
                for s in range(SETS):
                    if s < SETS - 1:
                        scores(n0 + s + 1)
                    values(n0 + s, layer)

            def down(n, H, w, src, chunks, wait):
                for m in range(2):
                    for k in range(chunks):
                        if m == 0:
                            wait(k)
                        last = mm(ps[:, 4 + 2 * H + m, 0:HALF], w[:, k, m * P:(m + 1) * P], src[:, k, cols(H)],
                                  start=(k == 0), stop=(k == chunks - 1))
                    last.then_inc(down_done, 1)

            def token_major(n, H):
                pe.wait_ge(x_ready, 4 * n + 2 * H + 2)
                for t in range(TH):
                    for m in range(2):
                        at = (t % 2) * D + m * P
                        last = tr(ps[0:TILE, 2 * H + t // 2, at:at + P],
                                  xT[:, m, H * HALF + t * TILE:H * HALF + (t + 1) * TILE], ident)
                last.then_inc(tm_done, 1)

            def back(n, H, src):
                for m in range(2):
                    for t in range(TH):
                        last = tr(ps[:, 4 + 2 * H + m, t * TILE:(t + 1) * TILE],
                                  src[0:TILE, TH * H + t, m * P:(m + 1) * P], ident[0:TILE, 0:TILE])
                    last.then_inc(fm_done, 1)

            pe.wait_ge(L["qkv0"], 16)
            pe.wait_ge(L["consts"], 16)
            pe.wait_ge(h_ready, 4)
            attention(0, qkv0_sb, 0)

            pe.wait_ge(L["w1"], 16)
            pe.wait_ge(s_out, 4)
            for i in range(2 * HC):
                H, m = i // HC, i % HC
                if m == 0:
                    pe.wait_ge(o_out, 4 if H else 4)
                if i >= 4:
                    pe.wait_ge(mid_ready, i - 3)
                for k in range(DC):
                    last = mm(ps[:, i % 4, 0:HALF], w1_sb[:, k, m * P:(m + 1) * P], oT[:, k, cols(H)],
                              start=(k == 0), stop=(k == DC - 1))
                last.then_inc(up_done, 1)
            pe.wait_ge(L["w2"], 16)
            for H in range(2):
                down(0, H, w2_sb, mid, HC, lambda k: pe.wait_ge(mid_ready, HC * H + k + 1))
            pe.wait_ge(tern_ready, 2)
            pe.wait_ge(mid_ready, 2 * HC)
            for r in range(8):
                if r >= 4:
                    pe.wait_ge(tern_out, r - 3)
                for j in range(4):
                    if r < 4:
                        k, m = r // 2, 4 * (r % 2) + j
                        src = fc_nat[:, m, k * P:(k + 1) * P]
                    else:
                        k, m = 2 * (r - 4) + j // 2, j % 2
                        src = proj_nat[:, m, k * P:(k + 1) * P]
                    last = tr(ps[:, r % 4, j * P:(j + 1) * P], src, ident)
                last.then_inc(tern_done, 1)
            pe.wait_ge(tern_out, 8)
            pe.wait_ge(u_ready, 1)
            for r in range(2):
                for j in range(4):
                    last = tr(ps[0:RANK, r, j * P:(j + 1) * P], u_sb[:, 4 * r + j, :], ident)
                last.then_inc(r_done, 1)
            pe.wait_ge(r_out, 2)
            token_major(0, 0)
            token_major(0, 1)
            pe.wait_ge(tm_ready, 1)
            back(0, 0, tm)
            pe.wait_ge(tm_ready, 2)
            back(0, 1, tm)
            for H in range(2):
                pe.wait_ge(h_ready, h_at(1, H))
                if H:
                    pe.wait_ge(up_act, 2 * HC + HC)
                for k in range(DC):
                    last = mm(ps[0:RANK, 2, 0:HALF], v_sb[:, k, :], hT[:, k, cols(H)], start=(k == 0), stop=(k == 1))
                last.then_inc(r_done, 1)
                pe.wait_ge(r_out, 3 + 2 * H)
                mm(ps[0:RANK, 3, 0:HALF], fb_sb[:, :], t1[:, cols(H)], start=True, stop=True).then_inc(r_done, 1)
                pe.wait_ge(r_out, 4 + 2 * H)
                for m in range(HC):
                    i = HC * H + m
                    if m >= 4:
                        pe.wait_ge(up_act, 2 * HC + i - 3)
                    for k in range(DC):
                        mm(ps[:, i % 4, 0:HALF], fcT[:, k, m * P:(m + 1) * P], hT[:, k, cols(H)],
                           start=(k == 0), stop=False)
                    mm(ps[:, i % 4, 0:HALF], uT[:, m * P:(m + 1) * P], t2[:, cols(H)], start=False,
                       stop=True).then_inc(up_done, 1)
            for H in range(2):
                down(1, H, projT, mid, HC, lambda k: pe.wait_ge(mid_ready, 2 * HC + HC * H + k + 1))
            token_major(1, 0)
            token_major(1, 1)
            pe.wait_ge(tm_ready, 3)
            back(1, 0, tm)
            pe.wait_ge(tm_ready, 4)
            back(1, 1, tm)
            pe.wait_ge(L["qkv1"], 16)
            attention(1, qkv1_sb, 2)
            pe.wait_ge(L["wo"], 16)
            pe.wait_ge(o_out, 8)
            for H in range(2):
                down(2, H, wo_sb, oT, DC, lambda k: None)
            pe.wait_ge(s_out, 8)
            token_major(2, 0)
            token_major(2, 1)
            pe.wait_ge(tm_ready, 7)
            back(2, 0, xn)
            pe.wait_ge(tm_ready, 8)
            back(2, 1, xn)
            pe.wait_ge(h_ready, h_at(3, 1))
            for t in range(NT):
                for k in range(DC):
                    last = mm(ps[0:TILE, 0, t * EXPERTS:(t + 1) * EXPERTS], hT[:, k, t * TILE:(t + 1) * TILE],
                              router_sb[:, k, :], start=(k == 0), stop=(k == DC - 1))
            last.then_inc(route_done, 1)

            def shared_up(i):
                H, m = i // IC, i % IC
                if i >= 2:
                    pe.wait_ge(mid_ready, 4 * HC + i - 1)
                for g, at in ((0, GATE0), (1, UP0)):
                    for k in range(DC):
                        last = mm(ps[:, 2 * (i % 2) + g, 0:HALF],
                                  sh[:, at + k * INNER + m * P:at + k * INNER + (m + 1) * P], hT[:, k, cols(H)],
                                  start=(k == 0), stop=(k == DC - 1))
                    last.then_inc(up_done, 1)

            pe.wait_ge(route_s, 2)
            oh = ohot[0:TILE, :].rearrange("p (t e) -> p t e", e=EXPERTS)
            for t in range(NT):
                dst = ps[0:TILE, 1, t * EXPERTS:(t + 1) * EXPERTS]
                for b in range(t):
                    mm(dst, ones[0:TILE, 0:TILE], oh[:, b, :], start=(b == 0), stop=False)
                mm(dst, const("tri")[0:TILE, :], oh[:, t, :], start=(t == 0), stop=True)
            for t in range(NT):
                last = mm(ps[:, 2, 0:EXPERTS], ones[0:TILE, :], oh[:, t, :], start=(t == 0), stop=(t == NT - 1))
            last.then_inc(route_done, 1)
            pe.wait_ge(pos_ready, 1)
            pe.wait_ge(L["shared"], 16)
            for i in range(2 * IC):
                shared_up(i)
            for t in range(NT):
                pe.wait_ge(mid_ready, 4 * HC + (IC if t < TH else 2 * IC))
                if t >= 4:
                    pe.wait_ge(base_ready, t - 3)
                for k in range(IC):
                    last = mm(ps[0:TILE, 4 + t % 4, 0:D], shmid[:, k, t * TILE:(t + 1) * TILE],
                              sh[:, DOWN0 + k * D:DOWN0 + (k + 1) * D], start=(k == 0), stop=(k == IC - 1))
                last.then_inc(shdown_done, 1)
            pe.wait_ge(base_ready, NT)
            pe.wait_ge(pos_ready, 2)
            for e in range(EXPERTS):
                pe.wait_ge(in_ex[e], 16)
            for s in range(SLOTS):
                e = pe.value_load(eint[0:1, s:s + 1], min_val=0, max_val=EXPERTS - 1)
                pe.wait_ge(slot_ld[s], 16)
                if s >= 1:
                    pe.wait_ge(xs_out, s)
                for c in range(DC):
                    last = tr(bank(0)[:, c * P:(c + 1) * P], slot_x[:, s, c * P:(c + 1) * P], ident)
                last.then_inc(xs_done, 1)
                pe.wait_ge(xs_out, s + 1)
                if s >= 2:
                    pe.wait_ge(hm_ready, s - 1)
                for g, at in ((0, GATE0), (1, UP0)):
                    for k in range(DC):
                        last = mm(bank(1 + 2 * (s % 2) + g), xsT[:, s % 2, k, :],
                                  ex[:, bass.ds(e * EW + (at + k * INNER), INNER)], start=(k == 0), stop=(k == DC - 1))
                last.then_inc(gu_done, 1)
                pe.wait_ge(hm_ready, s + 1)
                if s >= 1:
                    pe.wait_ge(hmT_out, s)
                for c in range(IC):
                    last = tr(bank(5)[:, c * P:(c + 1) * P], hm[:, s % 2, c * P:(c + 1) * P], ident)
                last.then_inc(hmT_done, 1)
                pe.wait_ge(hmT_out, s + 1)
                if s >= 1:
                    pe.wait_ge(y_out, s)
                for k in range(IC):
                    last = mm(bank(6)[:, 0:D], hmT[:, s % 2, k, :],
                              ex[:, bass.ds(e * EW + (DOWN0 + k * D), D)], start=(k == 0), stop=(k == IC - 1))
                last.then_inc(y_done, 1)


def chunked(w):
    return np.ascontiguousarray(w.reshape(w.shape[0] // P, P, w.shape[1]).transpose(1, 0, 2))


def constants():
    c = np.zeros((P, CONSTS), np.float32)

    def put(name, a):
        at, n = CONST[name]
        c[:, at:at + n] = a

    p = np.arange(P)[:, None]
    freq = (np.float32(1.0) / np.float32(10000.0) ** (np.arange(0, HD, 2, dtype=np.float32) / np.float32(HD)))
    ang = np.arange(SEQ, dtype=np.float32)[None, :] * freq[p[:, 0] % (HD // 2)][:, None]
    put("ident", np.eye(P))
    put("cos", np.cos(ang))
    put("sin", np.sin(ang) * np.where(p % HD < HD // 2, -1.0, 1.0))
    put("odd", (p // HD % 2 == np.arange(2)[None, :]))
    put("causal", np.where(np.arange(SEQ)[None, :] <= p % 64, 0.0, -1e30))
    put("iota", np.arange(EXPERTS)[None, :])
    put("steps", SLOT * np.arange(5)[None, :])
    e = np.arange(EXPERTS)
    put("before", (e[None, :] < e[:, None]).reshape(1, -1))
    put("slot", np.arange(SLOTS)[None, :])
    put("tri", p < np.arange(TILE)[None, :])
    put("ones", 1.0)
    return c


def kernel(x, L0_tok_W_proj, L0_tok_b_proj, L0_tok_pos_emb, L0_attn_Wq, L0_attn_Wk, L0_attn_Wv, L0_attn_W1,
           L0_attn_W2, L0_ffn_fast_b, L0_ffn_w_fc, L0_ffn_w_proj, L0_ffn_u, L0_ffn_v, L0_ffn_gate, L1_attn_Wqkv,
           L1_attn_Wout, L1_ffn_ln_w, L1_ffn_ln_b, L1_ffn_router_w, L1_ffn_gate_w, L1_ffn_up_w, L1_ffn_down_w,
           L1_ffn_sh_gate, L1_ffn_sh_up, L1_ffn_sh_down):
    import concourse.bacc as bacc
    from concourse.bass_utils import run_bass_kernel_spmd

    def a(v):
        return np.asarray(v)

    def heads(w):
        return np.repeat(a(w).reshape(4, HD, D), 4, axis=0).reshape(D, D).T

    def expert(g, u, d):
        return np.concatenate([chunked(m).reshape(P, -1) for m in (g, u, d)], axis=1)

    ims = a(x).reshape(IMAGES, 6, 16, 6, 16, 3).transpose(2, 4, 5, 0, 1, 3).reshape(PC, P, TOK)
    rows = {
        "patches": ims,
        "w_patch": chunked(a(L0_tok_W_proj).T),
        "patch_bias": a(L0_tok_b_proj).reshape(DC, P).T,
        "pos": chunked(a(L0_tok_pos_emb).T),
        "qkv0": chunked(np.concatenate([a(L0_attn_Wq).T, heads(L0_attn_Wk), heads(L0_attn_Wv)], axis=1)),
        "w1": chunked(a(L0_attn_W1).T),
        "w2": chunked(a(L0_attn_W2).T),
        "w_fc": chunked(a(L0_ffn_w_fc)),
        "w_proj": chunked(a(L0_ffn_w_proj)),
        "u": chunked(a(L0_ffn_u)),
        "v": chunked(a(L0_ffn_v).T),
        "fast_b": a(L0_ffn_fast_b).T,
        "gate": np.broadcast_to(a(L0_ffn_gate).reshape(1, 1), (P, 1)),
        "qkv1": chunked(a(L1_attn_Wqkv)),
        "w_out": chunked(a(L1_attn_Wout)),
        "ln_w": a(L1_ffn_ln_w).reshape(DC, P).T,
        "ln_b": a(L1_ffn_ln_b).reshape(DC, P).T,
        "ln_w_row": np.broadcast_to(a(L1_ffn_ln_w).reshape(1, D), (TILE, D)),
        "ln_b_row": np.broadcast_to(a(L1_ffn_ln_b).reshape(1, D), (TILE, D)),
        "router": chunked(a(L1_ffn_router_w)),
        "experts": np.stack([expert(a(L1_ffn_gate_w)[e], a(L1_ffn_up_w)[e], a(L1_ffn_down_w)[e])
                             for e in range(EXPERTS)]),
        "shared": expert(a(L1_ffn_sh_gate), a(L1_ffn_sh_up), a(L1_ffn_sh_down)),
        "consts": constants(),
    }
    nc = bacc.Bacc("TRN2", target_bir_lowering=False, num_devices=1)
    arrays, args = {}, []
    for name, v in rows.items():
        v = np.ascontiguousarray(v)
        arrays["in_" + name] = v
        args.append(nc.dram_tensor("in_" + name, v.shape, mybir.dt.from_np(v.dtype), kind="ExternalInput").ap())
    args.append(nc.dram_tensor("result", (TOK, D), F32, kind="ExternalOutput").ap())
    program(nc, *args)
    r = run_bass_kernel_spmd(nc, [arrays], core_ids=[0])
    return r.results[0]["result"].reshape(IMAGES, SEQ, D)
```

```python
from contextlib import ExitStack

import numpy as np

import concourse.bass as bass
from concourse import mybir

ALU = mybir.AluOpType
ACT = mybir.ActivationFunctionType
F32 = mybir.dt.float32
F32R = mybir.dt.float32r
I32 = mybir.dt.int32
AX = mybir.AxisListType

P = 128
IMAGES = 16
SEQ = 36
TOK = IMAGES * SEQ
HALF = TOK // 2
PAD = 608
D = 256
DC = D // P
PATCH = 768
PC = PATCH // P
HID = 1024
HC = HID // P
HD = 16
KVW = 4 * HD
RANK = 16
TILE = 96
NT = TOK // TILE
TH = NT // 2
EXPERTS = 8
INNER = 512
IC = INNER // P
EW = 2 * DC * INNER + IC * D
SLOT = 128
PART = SLOT // 2
SLOTS = EXPERTS
STEPS = TOK // PART - 1
assert SLOTS * PART >= TOK - PART
SETS = 4
EPS = 1e-5
GATE0, UP0, DOWN0 = 0, DC * INNER, 2 * DC * INNER

CONST = {}
_at = 0
for _name, _n in (("ident", P), ("cos", SEQ), ("sin", SEQ), ("odd", 2), ("causal", SEQ), ("iota", EXPERTS),
                  ("steps", STEPS), ("before", EXPERTS * EXPERTS), ("slot", SLOTS), ("tri", TILE), ("ones", P)):
    CONST[_name] = (_at, _n)
    _at += _n
CONSTS = _at


def program(nc, patches, w_patch, patch_bias, pos, qkv0, w1, w2, w_fc, w_proj, u, v, fast_b, gate, qkv1, w_out,
            ln_w, ln_b, ln_w_row, ln_b_row, router, experts, shared, consts, out):
    ctx = ExitStack()
    with ctx:
        def sb(name, shape, dt=F32):
            return ctx.enter_context(nc.sbuf_tensor(name, shape, dt))

        def sem(name):
            return ctx.enter_context(nc.semaphore(name))

        slot_in = nc.dram_tensor("slot_in", (SLOTS * SLOT, D), F32, kind="Internal").ap()
        slot_out = nc.dram_tensor("slot_out", (SLOTS * SLOT, D), F32, kind="Internal").ap()

        def next_place():
            return -(-nc.sbuf_base // 32) * 32

        ex_base = next_place()
        ex = sb("ex", [P, EXPERTS * EW])
        sh = sb("sh", [P, EW])

        def under(e, at, *shape):
            n = int(np.prod(shape))
            flat = ex[:, e * EW + at:e * EW + at + n]
            return flat.rearrange("p (a b) -> p a b", a=shape[0])

        wp_sb = under(7, 0, PC, D)
        qkv0_sb = under(7, PC * D, DC, 2 * D + KVW)
        w1_sb = under(6, 0, DC, HID)
        w2_sb = under(5, 0, HC, D)
        pat_sb = under(3, 0, PC, TOK)
        fc_nat = under(3, PC * TOK, HC, D)
        proj_nat = under(2, 0, DC, HID)
        LATE = 2
        def rounded_at(name, base, at, shape):
            return nc.alloc_sbuf_tensor_at(name, [P] + shape, F32R, offset=base + 4 * at)

        fcT = sb("fcT", [P, DC, HID], F32R)
        projT = sb("projT", [P, HC, D], F32R)
        x_hi = rounded_at("x_hi", ex_base, 3 * EW, [DC, TOK])
        x_lo = rounded_at("x_lo", ex_base, 3 * EW + DC * TOK, [DC, TOK])
        t4 = rounded_at("t4", ex_base, 3 * EW + 2 * DC * TOK, [TOK])
        r_lo = rounded_at("r_lo", ex_base, 6 * EW, [HC, TOK])
        uT = rounded_at("uT", ex_base, 2 * EW + DC * HID, [HID])
        qkv1_sb = sb("qkv1_sb", [P, DC, 3 * D])
        wo_sb = sb("wo_sb", [P, DC, D])
        hT = sb("hT", [P, DC, PAD])
        BIG = DC * PAD + 4 * TOK + 32 * SEQ
        r_hi = rounded_at("r_hi", next_place(), 0, [HC, TOK])
        big = sb("big", [P, BIG])
        mid = big[:, 0:HC * TOK].rearrange("p (a b) -> p a b", a=HC)
        qT = big[:, 0:DC * PAD].rearrange("p (a b) -> p a b", a=DC)
        kbd = big[:, DC * PAD:DC * PAD + 4 * TOK].rearrange("p (c h t) -> p c h t", c=DC, h=2)
        pT = big[:, DC * PAD + 4 * TOK:BIG].rearrange("p (t q i) -> p t q i", t=16, q=2)
        vbd = sb("vbd", [P, 2, IMAGES // 2, D])
        soft = sb("soft", [P, 2, 32, 64])
        oT = sb("oT", [P, DC, TOK])
        xT = sb("xT", [P, DC, TOK])
        tm = sb("tm", [P, NT, D])
        cst = sb("cst", [P, CONSTS])
        small = sb("small", [P, 512])
        _s = [0]

        def sm(n):
            a = _s[0]
            _s[0] += n
            return small[:, a:a + n]

        pbias = sb("pbias", [P, DC])
        pos_sb = sb("pos_sb", [P, DC, SEQ])
        u_sb = sb("u_sb", [P, HC, RANK])
        v_sb = sb("v_sb", [P, DC, RANK])
        fb_sb = sb("fb_sb", [RANK, RANK])
        gate_sb = sb("gate_sb", [P, 1])
        fb4 = under(4, PC * TOK + HC * D - EW, 4, 32)[0:RANK]
        relus = xT[:, :, :].rearrange("p a b -> p (a b)").rearrange("p (n t) -> p n t", n=4)
        squares = under(7, HC * TOK - EW, 4, HALF)
        u4 = under(5, HC * D, HC, 4 * 32).rearrange("p m (g r) -> p m g r", g=4)
        t1 = oT[0:RANK, 0, :]
        lnw = sb("lnw", [P, DC])
        lnb = sb("lnb", [P, DC])
        router_sb = sb("router_sb", [P, DC, EXPERTS])

        def const(name):
            a, n = CONST[name]
            return cst[:, a:a + n]

        ident, ones = const("ident"), const("ones")
        fc_scale, proj_scale = sm(HC), sm(DC)
        fc_half, fc_nhalf, proj_half, proj_nhalf = sm(HC), sm(HC), sm(DC), sm(DC)
        fc_rs = sm(HC)
        smax, ssum, srec = sm(32), sm(32), sm(32)
        stats, mv, rstd = sm(6 * TH), sm(2 * TH), sm(TH)
        veps = sm(TH)
        mhalf, epsc, rstd2 = sm(TH), sm(TH), sm(TH)
        raws = [xT[:, :, :].rearrange("p a b -> p (a b)"), pT.rearrange("p t q i -> p (t q i)")]
        swps = [tm[:, :, :].rearrange("p a b -> p (a b)")[:, 0:4 * HALF],
                soft[:, 1, :, :].rearrange("p a b -> p (a b)")[:, 0:4 * HALF]]
        below = soft[:, :, :, :].rearrange("p a b c -> p (a b c)")[:, 0:2048]
        vflat = vbd[:, :, :, :].rearrange("p a b c -> p (a b c)")
        xn = vflat[:, 0:NT * D].rearrange("p (a b) -> p a b", a=NT)
        xe = vflat[:, NT * D:2 * NT * D].rearrange("p (a b) -> p a b", a=NT)
        lnw_row = vflat[:, 2 * NT * D:2 * NT * D + D]
        lnb_row = vflat[:, 2 * NT * D + D:2 * NT * D + 2 * D]
        sflat = soft[:, :, :, :].rearrange("p a b c -> p (a b c)")
        slot_x = sflat[:, 0:SLOTS * D].rearrange("p (a b) -> p a b", a=SLOTS)
        xsT = sflat[:, SLOTS * D:SLOTS * D + 2 * DC * SLOT].rearrange("p (n c t) -> p n c t", n=2, c=DC)
        bflat = big
        shmid = bflat[:, 0:IC * TOK].rearrange("p (a b) -> p a b", a=IC)
        _b = IC * TOK
        th = bflat[:, _b:_b + 2 * INNER].rearrange("p (n a) -> p n a", n=2)
        hm = th
        hmT = oT[:, :, :].rearrange("p a b -> p (a b)")[:, 0:2 * INNER].rearrange("p (n c t) -> p n c t", n=2, c=IC)
        yout = bflat[:, _b + 2 * INNER:_b + 2 * INNER + 2 * D].rearrange("p (n d) -> p n d", n=2)
        zero = vflat[:, 2 * NT * D + 2 * D:2 * NT * D + 3 * D]
        yt, fin = xn, xe
        lg, gt8, ohot, tmp8 = sm(48), sm(48), sm(48), sm(48)
        lmax, eidx, score, posf = sm(NT), sm(NT), sm(NT), sm(NT)
        rank, npart, first = sm(NT), sm(NT), sm(NT)
        cnt, nslot, sstart, send = sm(8), sm(8), sm(8), sm(8)
        eslot = sm(SLOTS)
        posi = sb("posi", [P, NT], I32)
        eint = sb("eint", [P, SLOTS], I32)
        wk = sb("wk", [P, SLOTS * EXPERTS])

        ps = ctx.enter_context(nc.psum_tensor("ps", [P, 8, 512], F32))

        def bank(i):
            return ps[:, i, :]

        L = {n: sem("in_" + n) for n in (
            "patches0", "patches1", "patches2", "patches3", "patches4", "patches5", "wp", "small", "consts", "qkv0",
            "w1", "w2", "fc", "proj", "qkv1", "wo", "shared", "rows")}
        in_ex = [sem(f"in_ex{e}") for e in range(EXPERTS)]
        dve_step = sem("dve_step")
        pool_step = sem("pool_step")
        embedded = sem("embedded")
        h_ready = sem("h_ready")
        pads_zero = sem("pads_zero")
        qk_done = sem("qk_done")
        raw_out = sem("raw_out")
        swapped = sem("swapped")
        cos_done = sem("cos_done")
        sin_done = sem("sin_done")
        roped = sem("roped")
        k_ready = sem("k_ready")
        v_done = sem("v_done")
        v_out = sem("v_out")
        s_done = sem("s_done")
        s_out = sem("s_out")
        s_sub = sem("s_sub")
        s_exp = sem("s_exp")
        p_ready = sem("p_ready")
        pt_done = sem("pt_done")
        pt_out = sem("pt_out")
        o_done = sem("o_done")
        o_out = sem("o_out")
        up_done = sem("up_done")
        up_act = sem("up_act")
        relu_ready = sem("relu_ready")
        hi_ready = sem("hi_ready")
        sq_ready = sem("sq_ready")
        x_hi_ready = sem("x_hi_ready")
        x_lo_ready = sem("x_lo_ready")
        t_hi_ready = sem("t_hi_ready")
        t_lo_ready = sem("t_lo_ready")
        u_zero = sem("u_zero")
        fb_ready = sem("fb_ready")
        fb_zero = sem("fb_zero")
        mid_ready = sem("mid_ready")
        down_done = sem("down_done")
        x_ready = sem("x_ready")
        tm_done = sem("tm_done")
        rstd2_ready = sem("rstd2_ready")
        xe_sum = sem("xe_sum")
        var_ready = sem("var_ready")
        rstd_ready = sem("rstd_ready")
        tm_ready = sem("tm_ready")
        fm_done = sem("fm_done")
        tern_ready = sem("tern_ready")
        half_const = sem("half_const")
        tern_done = sem("tern_done")
        tern_out = sem("tern_out")
        u_ready = sem("u_ready")
        r_done = sem("r_done")
        r_out = sem("r_out")
        vb_zero = sem("vb_zero")
        vb_free = sem("vb_free")
        sh_act = sem("sh_act")
        nf_ready = sem("nf_ready")
        route_done = sem("route_done")
        route_s = sem("route_s")
        score_t = sem("score_t")
        pos_ready = sem("pos_ready")
        xe_ready = sem("xe_ready")
        zero_ready = sem("zero_ready")
        slots_zero = sem("slots_zero")
        scattered = sem("scattered")
        slot_ld = [sem(f"slot_ld{s}") for s in range(SLOTS)]
        xs_done, xs_out = sem("xs_done"), sem("xs_out")
        gu_done, th_done, hm_ready = sem("gu_done"), sem("th_done"), sem("hm_ready")
        g_half = sem("g_half")
        hmT_done, hmT_out = sem("hmT_done"), sem("hmT_out")
        y_done, y_out = sem("y_done"), sem("y_out")
        y_st = [sem(f"y_st{i}") for i in range(2)]
        y_back = [sem(f"y_back{t}") for t in range(NT)]
        shdown_done, base_ready = sem("shdown_done"), sem("base_ready")
        fin_ready = sem("fin_ready")
        s_out_dma = sem("s_out_dma")

        def cols(H):
            return slice(H * HALF, (H + 1) * HALF)

        block = ctx.enter_context(nc.Block())

        def h_at(stage, H):
            return 4 * stage + 2 * H + 2

        @block.sync
        def _(sp):
            for k in range(PC):
                sp.dma_start(pat_sb[:, k, :], patches[k]).then_inc(L[f"patches{k}"], 16)
                if k == 0:
                    sp.dma_start(wp_sb, w_patch).then_inc(L["wp"], 16)
            for dst, src in ((pbias[:], patch_bias), (pos_sb[:], pos), (u_sb[:], u), (v_sb[:], v), (fb_sb[:], fast_b),
                             (gate_sb[:], gate), (lnw[:], ln_w), (lnb[:], ln_b), (router_sb[:], router)):
                sp.dma_start(dst, src).then_inc(L["small"], 16)
            sp.dma_start(cst[:], consts).then_inc(L["consts"], 16)
            sp.dma_start(qkv0_sb, qkv0).then_inc(L["qkv0"], 16)
            sp.dma_start(fc_nat, w_fc).then_inc(L["fc"], 16)
            sp.dma_start(proj_nat, w_proj).then_inc(L["proj"], 16)
            sp.dma_start(w1_sb, w1).then_inc(L["w1"], 16)
            sp.dma_start(w2_sb, w2).then_inc(L["w2"], 16)
            sp.dma_start(qkv1_sb[:], qkv1).then_inc(L["qkv1"], 16)
            sp.dma_start(wo_sb[:], w_out).then_inc(L["wo"], 16)
            sp.dma_start(sh[:], shared).then_inc(L["shared"], 16)
            for e in range(EXPERTS):
                if e == LATE:
                    sp.wait_ge(down_done, 8)
                sp.dma_start(ex[:, e * EW:(e + 1) * EW], experts[e]).then_inc(in_ex[e], 16)
            sp.wait_ge(o_done, 2 * SETS)
            sp.dma_start(lnw_row[0:TILE, :], ln_w_row).then_inc(L["rows"], 16)
            sp.dma_start(lnb_row[0:TILE, :], ln_b_row).then_inc(L["rows"], 16)
            sp.wait_ge(zero_ready, 1)
            for s in range(SLOTS):
                sp.dma_start(slot_in[s * SLOT:(s + 1) * SLOT, :], zero).then_inc(slots_zero, 16)
            sp.wait_ge(scattered, 16 * NT)
            for s in range(SLOTS):
                sp.dma_start(slot_x[:, s, :], slot_in[s * SLOT:(s + 1) * SLOT, :]).then_inc(slot_ld[s], 16)
            for s in range(SLOTS):
                sp.wait_ge(y_out, s + 1)
                sp.dma_start(slot_out[s * SLOT:(s + 1) * SLOT, :], yout[:, s % 2, :]).then_inc(y_st[s % 2], 16)
            for t in range(NT):
                sp.wait_ge(fin_ready, t + 1)
                sp.dma_start(out[t * TILE:(t + 1) * TILE, :], fin[0:TILE, t, :]).then_inc(s_out_dma, 16)
            sp.wait_ge(s_out_dma, 16 * NT)

        @block.gpsimd
        def _(pool):
            nc.gpsimd.memset(hT[:, :, TOK:PAD], 0.0).then_inc(pads_zero, 1)
            nc.gpsimd.memset(qT[:, :, TOK:PAD], 0.0).then_inc(pads_zero, 1)
            nc.gpsimd.memset(vbd[:, :, :, :], 0.0).then_inc(vb_zero, 1)
            nc.gpsimd.memset(soft[:, 0, :, SEQ:64], 0.0).then_inc(vb_zero, 1)
            nc.gpsimd.memset(mhalf, -0.5).then_inc(half_const, 1)
            nc.gpsimd.memset(epsc, EPS).then_inc(half_const, 1)
            pool.wait_ge(half_const, 2)

            def rope(layer):
                for H in range(2):
                    n = 2 * layer + H
                    raw, swp = raws[H], swps[H]
                    r4 = raw.rearrange("p (a t) -> p a t", t=SEQ)
                    pool.wait_ge(L["consts"], 16)
                    pool.wait_ge(swapped, n + 1)
                    nc.gpsimd.tensor_tensor(r4, r4, const("cos").unsqueeze(1).to_broadcast([P, 32, SEQ]),
                                            ALU.mult).then_inc(cos_done, 1)
                    pool.wait_ge(cos_done, n + 1)
                    pool.wait_ge(sin_done, n + 1)
                    if layer and H == 0:
                        pool.wait_ge(down_done, 8)
                    q2 = raw[:, 0:2 * HALF].rearrange("p (a t) -> p a t", a=2)
                    s2 = swp[:, 0:2 * HALF].rearrange("p (a t) -> p a t", a=2)
                    nc.gpsimd.tensor_tensor(qT[:, :, cols(H)], q2, s2, ALU.add).then_inc(roped, 1)
                    nc.gpsimd.tensor_tensor(raw[:, 2 * HALF:4 * HALF], raw[:, 2 * HALF:4 * HALF],
                                            swp[:, 2 * HALF:4 * HALF], ALU.add).then_inc(roped, 1)
                pool.wait_ge(roped, 4 * layer + 4)
                nc.gpsimd.memset(soft[:, 1, :, SEQ:64], 0.0).then_inc(vb_zero, 1)

            def rsqrt(n):
                pool.wait_ge(var_ready, n + 1)
                if n:
                    pool.wait_ge(tm_ready, n)
                nc.gpsimd.tensor_tensor(rstd[0:TILE, :], veps[0:TILE, :], mhalf[0:TILE, :],
                                        ALU.pow).then_inc(rstd_ready, 1)

            rope(0)
            nc.gpsimd.memset(fb4[:, :, :], 0.0).then_inc(fb_zero, 1)
            pool.wait_ge(fb_zero, 1)
            pool.wait_ge(L["small"], 16 * 9)
            nc.gpsimd.tensor_copy(fb4[:, :, 0:RANK],
                                  fb_sb[:, :].unsqueeze(1).to_broadcast([RANK, 4, RANK])).then_inc(fb_ready, 1)
            pool.wait_ge(L["w2"], 16)
            nc.gpsimd.memset(u4, 0.0).then_inc(u_zero, 1)
            for n in range(2):
                rsqrt(n)
            for i in range(2 * HC):
                pool.wait_ge(relu_ready, i + 1)
                if i >= 4:
                    pool.wait_ge(mid_ready, 2 * HC + i - 3)
                nc.gpsimd.tensor_tensor(squares[:, i % 4, :], relus[:, i % 4, :], relus[:, i % 4, :],
                                        ALU.mult).then_inc(sq_ready, 1)
            pool.wait_ge(tern_ready, HC + DC)
            nc.gpsimd.memset(soft[:, 0, :, SEQ:64], 0.0).then_inc(vb_zero, 1)
            for n in range(2, 4):
                rsqrt(n)
            pool.wait_ge(down_done, 8)
            nc.gpsimd.memset(qT[:, :, TOK:PAD], 0.0).then_inc(pads_zero, 1)
            rope(1)
            pool.wait_ge(o_done, 2 * SETS)
            nc.gpsimd.memset(zero, 0.0).then_inc(zero_ready, 1)
            for n in range(4, 6):
                rsqrt(n)
                r2 = rstd2[0:TILE, :]
                for j, (a, b, op) in enumerate((
                        (rstd[0:TILE, :], rstd[0:TILE, :], ALU.mult), (r2, mv[0:TILE, 1:2 * TH:2], ALU.mult),
                        (r2, epsc[0:TILE, :], ALU.add), (r2, mhalf[0:TILE, :], ALU.pow),
                        (r2, rstd[0:TILE, :], ALU.mult))):
                    pool.wait_ge(rstd_ready, n + 1)
                    if j:
                        pool.wait_ge(pool_step, 4 * (n - 4) + j)
                    nc.gpsimd.tensor_tensor(r2, a, b, op).then_inc(pool_step if j < 4 else rstd2_ready, 1)
            pool.wait_ge(L["rows"], 32)
            pool.wait_ge(tm_ready, 6)
            B6 = [TILE, NT, D]
            nc.gpsimd.tensor_tensor(xe[0:TILE], xn[0:TILE], lnw_row[0:TILE, :].unsqueeze(1).to_broadcast(B6),
                                    ALU.mult).then_inc(xe_sum, 1)
            pool.wait_ge(xe_sum, 1)
            nc.gpsimd.tensor_tensor(xe[0:TILE], xe[0:TILE], lnb_row[0:TILE, :].unsqueeze(1).to_broadcast(B6),
                                    ALU.add).then_inc(xe_sum, 1)
            pool.wait_ge(slots_zero, 16 * SLOTS)
            for t in range(NT):
                pool.wait_ge(pos_ready, 1)
                pool.wait_ge(xe_ready, t + 1)
                pool.indirect_dma_start(slot_in, bass.IndirectOffsetOnAxis(ap=posi[0:TILE, t:t + 1], axis=0),
                                        xe[0:TILE, t, :], None).then_inc(scattered, 16)
            pool.wait_ge(y_st[0], 16 * (SLOTS // 2))
            pool.wait_ge(y_st[1], 16 * (SLOTS // 2))
            for t in range(NT):
                pool.indirect_dma_start(yt[0:TILE, t, :], None, slot_out,
                                        bass.IndirectOffsetOnAxis(ap=posi[0:TILE, t:t + 1], axis=0)
                                        ).then_inc(y_back[t], 16)
            for n in range(6, 8):
                rsqrt(n)

        @block.scalar
        def _(act):
            def rope_in(layer, H):
                n = 2 * layer + H
                raw = raws[H]
                if layer and H:
                    act.wait_ge(down_done, 8)
                for i in range(4):
                    act.wait_ge(qk_done, 4 * n + i + 1)
                    nc.scalar.activation(raw[:, i * HALF:(i + 1) * HALF], ps[:, i, 0:HALF], ACT.Copy,
                                         scale=0.25 if i < 2 else 1.0).then_inc(raw_out, 1)

            def v_in(layer):
                if layer == 0:
                    act.wait_ge(vb_zero, 1)
                    act.wait_ge(v_done, 1)
                    for q in range(2):
                        for hh in range(2):
                            src = ps[64 * q:64 * q + SEQ, 4, :].rearrange("p (a c) -> p a c", c=HD)
                            dst = vbd[64 * hh:64 * hh + SEQ, q, :, :].rearrange("p r (k b c) -> p (r k) b c", k=4, b=2)
                            nc.scalar.activation(dst[:, :, :, HD * hh:HD * hh + HD],
                                                 src.unsqueeze(2).to_broadcast([SEQ, 32, 2, HD]),
                                                 ACT.Copy).then_inc(v_out, 1)
                for n in range(4 * layer):
                    act.wait_ge(v_done, n + 2)
                    for q in range(2):
                        for hh in range(2):
                            src = ps[64 * q:64 * q + SEQ, 4 + n, :].rearrange("p (r b c) -> p r b c", r=2, b=8)
                            dst = vbd[64 * hh:64 * hh + SEQ, q, 2 * n:2 * n + 2, :].rearrange(
                                "p r (b c) -> p r b c", b=8)
                            last = nc.scalar.activation(dst[:, :, :, HD * hh:HD * hh + HD],
                                                        src[:, :, :, HD * hh:HD * hh + HD], ACT.Copy)
                    last.then_inc(v_out, 1)

            def softmax_exp(n):
                act.wait_ge(s_sub, n + 1)
                x = soft[:, n % 2, :, 0:SEQ]
                nc.scalar.activation(x, x, ACT.Exp).then_inc(s_exp, 1)

            def attn_out(n, last):
                for r in range(4):
                    act.wait_ge(pt_done, 4 * n + r + 1)
                    if r == 0 and n:
                        act.wait_ge(o_done, n)
                    src = ps[:, 4 + r % 2, :].rearrange("p (t q i) -> p t q i", t=4, q=2)[:, :, :, 0:SEQ]
                    nc.scalar.activation(pT[:, 4 * r:4 * r + 4, :, :], src, ACT.Copy).then_inc(pt_out, 1)
                if not last:
                    softmax_exp(n + 1)
                act.wait_ge(o_done, n + 1)
                s = n % SETS
                nc.scalar.activation(oT[:, :, s * 4 * SEQ:(s + 1) * 4 * SEQ],
                                     ps[:, 6 + n % 2, 0:8 * SEQ].rearrange("p (c t) -> p c t", c=DC),
                                     ACT.Copy).then_inc(o_out, 1)

            def attention(layer):
                rope_in(layer, 0)
                rope_in(layer, 1)
                v_in(layer)
                n0 = SETS * layer
                softmax_exp(n0)
                for s in range(SETS):
                    attn_out(n0 + s, s == SETS - 1)

            attention(0)
            for i in range(2 * HC):
                act.wait_ge(up_done, i + 1)
                nc.scalar.activation(mid[:, i % HC, cols(i // HC)], ps[:, i % 4, 0:HALF], ACT.Tanh,
                                     scale=0.5).then_inc(up_act, 1)
            def ternary_out(r):
                act.wait_ge(tern_done, r + 1)
                if r < 4:
                    dst = fcT[:, r // 2, (r % 2) * 512:(r % 2) * 512 + 512]
                else:
                    dst = projT[:, 2 * (r - 4):2 * (r - 4) + 2, :].rearrange("p a b -> p (a b)")
                nc.scalar.activation(dst, bank(r % 4), ACT.Copy).then_inc(tern_out, 1)

            def x_high(H):
                for m in range(2):
                    act.wait_ge(fm_done, 2 * H + m + 1)
                    nc.scalar.activation(x_hi[:, m, cols(H)], ps[:, 4 + 2 * H + m, 0:HALF],
                                         ACT.Copy).then_inc(x_hi_ready, 1)

            for r in range(4):
                ternary_out(r)
            x_high(0)
            for r in range(4, 8):
                ternary_out(r)
            for r in range(2):
                act.wait_ge(r_done, r + 1)
                nc.scalar.activation(uT[:, r * 512:(r + 1) * 512], bank(r), ACT.Copy).then_inc(r_out, 1)
            for H in range(2):
                act.wait_ge(r_done, 3 + 2 * H)
                nc.scalar.activation(t1[:, cols(H)], ps[0:RANK, 2, 0:HALF], ACT.Copy).then_inc(r_out, 1)
                act.wait_ge(r_done, 4 + 2 * H)
                nc.scalar.activation(t4[:, cols(H)], ps[:, 3, 0:HALF], ACT.Copy).then_inc(t_hi_ready, 1)
                for i in range(HC * H, HC * H + HC):
                    act.wait_ge(up_done, 2 * HC + i + 1)
                    if i >= 4:
                        act.wait_ge(sq_ready, i - 3)
                    nc.scalar.activation(relus[:, i % 4, :], ps[:, i % 4, 0:HALF], ACT.Relu,
                                         scale=fc_scale[:, i % HC:i % HC + 1]).then_inc(relu_ready, 1)
                    act.wait_ge(relu_ready, i + 1)
                    nc.scalar.activation(r_hi[:, i % HC, cols(H)], relus[:, i % 4, :],
                                         ACT.Square).then_inc(hi_ready, 1)
                    if i == 2:
                        x_high(1)
            attention(1)
            act.wait_ge(route_s, 1)
            nc.scalar.activation(score[0:TILE, :], lmax[0:TILE, :], ACT.Tanh, scale=0.5).then_inc(score_t, 1)
            for i in range(2 * IC):
                act.wait_ge(up_done, 4 * HC + 2 * i + 1)
                nc.scalar.activation(shmid[:, i % IC, cols(i // IC)], ps[:, 2 * (i % 2), 0:HALF], ACT.Tanh,
                                     scale=0.5).then_inc(sh_act, 1)
            def tokens_out(s):
                act.wait_ge(xs_done, s + 1)
                if s >= 2:
                    act.wait_ge(gu_done, s - 1)
                nc.scalar.activation(xsT[:, s % 2, :, :], bank(0)[:, 0:2 * SLOT].rearrange("p (c t) -> p c t", c=DC),
                                     ACT.Copy).then_inc(xs_out, 1)

            def gate_tanh(s):
                act.wait_ge(gu_done, s + 1)
                if s >= 2:
                    act.wait_ge(hmT_done, s - 1)
                nc.scalar.activation(th[:, s % 2, :], bank(1 + 2 * (s % 2)), ACT.Tanh, scale=0.5).then_inc(th_done, 1)

            tokens_out(0)
            gate_tanh(0)
            tokens_out(1)
            for s in range(SLOTS):
                act.wait_ge(hmT_done, s + 1)
                if s >= 2:
                    act.wait_ge(y_done, s - 1)
                nc.scalar.activation(hmT[:, s % 2, :, :], bank(5).rearrange("p (c t) -> p c t", c=IC),
                                     ACT.Copy).then_inc(hmT_out, 1)
                if s + 1 < SLOTS:
                    gate_tanh(s + 1)
                if s + 2 < SLOTS:
                    tokens_out(s + 2)
                act.wait_ge(y_done, s + 1)
                if s >= 2:
                    act.wait_ge(y_st[s % 2], 16 * (s // 2))
                nc.scalar.activation(yout[:, s % 2, :], bank(6)[:, 0:D], ACT.Copy).then_inc(y_out, 1)

        @block.vector
        def _(dve):
            chain = [0]

            def link(ins):
                chain[0] += 1
                ins.then_inc(dve_step, 1)
                dve.wait_ge(dve_step, chain[0])

            V = nc.vector
            dve.wait_ge(L["small"], 16 * 9)
            for i in range(4):
                H, m = i // 2, i % 2
                dve.wait_ge(embedded, i + 1)
                V.scalar_tensor_tensor(
                    hT[:, m, cols(H)].rearrange("p (b t) -> p b t", t=SEQ),
                    ps[:, i, 0:HALF].rearrange("p (b t) -> p b t", t=SEQ), pbias[:, m:m + 1],
                    pos_sb[:, m, :].unsqueeze(1).to_broadcast([P, 8, SEQ]), ALU.add, ALU.add).then_inc(h_ready, 1)

            def ternary_scale(nat, half, nhalf, scale, name):
                dve.wait_ge(L[name], 16)
                link(V.tensor_reduce(scale, nat, AX.X, ALU.add, apply_absolute_value=True))
                link(V.tensor_scalar(scale, scale, 1.0 / nat.shape[2], 1e-5, ALU.mult, ALU.max))
                V.tensor_scalar(half, scale, 0.5, None, ALU.mult)
                link(V.tensor_scalar(nhalf, scale, -0.5, None, ALU.mult))

            def ternary(nat, half, nhalf, b, scratch_read):
                n = nat.shape[2]
                scratch = below[:, (b % 2) * n:(b % 2) * n + n]
                if scratch_read > 0:
                    dve.wait_ge(tern_ready, scratch_read)
                link(V.tensor_scalar(scratch, nat[:, b, :], nhalf[:, b:b + 1], None, ALU.is_lt))
                V.scalar_tensor_tensor(nat[:, b, :], nat[:, b, :], half[:, b:b + 1], scratch,
                                       ALU.is_gt, ALU.subtract).then_inc(tern_ready, 1)

            def rope_mid(layer, H):
                n = 2 * layer + H
                raw, swp = raws[H], swps[H]
                dve.wait_ge(raw_out, 4 * n + 4)
                V.stream_shuffle(swp, raw[:, 0:4 * HALF], [(i // HD) * HD + (i + HD // 2) % HD for i in range(32)]
                                 ).then_inc(swapped, 1)
                dve.wait_ge(swapped, n + 1)
                s4 = swp.rearrange("p (a t) -> p a t", t=SEQ)
                dve.wait_ge(L["consts"], 16)
                V.tensor_tensor(s4, s4, const("sin").unsqueeze(1).to_broadcast([P, 32, SEQ]),
                                ALU.mult).then_inc(sin_done, 1)

            def rope_k(layer, H):
                n = 2 * layer + H
                dve.wait_ge(roped, 2 * n + 2)
                raw = raws[H]
                for hh in range(2):
                    last = V.tensor_scalar(kbd[:, :, hh, cols(H)],
                                           raw[:, 2 * HALF:4 * HALF].rearrange("p (c t) -> p c t", c=DC),
                                           const("odd")[:, hh:hh + 1], None, ALU.mult)
                last.then_inc(k_ready, 1)

            def scores_in(n):
                dve.wait_ge(s_done, n + 1)
                if n >= 2:
                    dve.wait_ge(pt_done, 4 * (n - 1))
                if n % SETS < 2:
                    dve.wait_ge(vb_zero, (2, 3, 4, 5)[2 * (n // SETS) + n % SETS])
                src = ps[:, 0:4, 0:8 * SEQ].rearrange("p g (s j) -> p g s j", j=SEQ)
                dst = soft[:, n % 2, :, 0:SEQ].rearrange("p (g s) j -> p g s j", g=4)
                mask = const("causal").unsqueeze(1).unsqueeze(1).to_broadcast([P, 4, 8, SEQ])
                V.tensor_tensor(dst, src, mask, ALU.add).then_inc(s_out, 1)

            def scores_max(n):
                x = soft[:, n % 2, :, 0:SEQ]
                dve.wait_ge(s_out, n + 1)
                link(V.tensor_reduce(smax, x, AX.X, ALU.max))
                V.tensor_tensor(x, x, smax.unsqueeze(2).to_broadcast([P, 32, SEQ]), ALU.subtract).then_inc(s_sub, 1)

            def scores_norm(n):
                x = soft[:, n % 2, :, 0:SEQ]
                dve.wait_ge(s_exp, n + 1)
                link(V.tensor_reduce(ssum, x, AX.X, ALU.add))
                link(V.reciprocal(srec, ssum))
                V.tensor_tensor(x, x, srec.unsqueeze(2).to_broadcast([P, 32, SEQ]), ALU.mult).then_inc(p_ready, 1)

            def attention(layer):
                rope_mid(layer, 0)
                rope_mid(layer, 1)
                rope_k(layer, 0)
                rope_k(layer, 1)
                n0 = SETS * layer
                scores_in(n0)
                scores_max(n0)
                for s in range(SETS):
                    scores_norm(n0 + s)
                    if s < SETS - 1:
                        scores_in(n0 + s + 1)
                        scores_max(n0 + s + 1)

            def residual(n, H, scale=None):
                for m in range(2):
                    dve.wait_ge(down_done, 4 * n + 2 * H + m + 1)
                    s = 1.0 if scale is None else scale(m)
                    V.scalar_tensor_tensor(xT[:, m, cols(H)], ps[:, 4 + 2 * H + m, 0:HALF], s, hT[:, m, cols(H)],
                                           ALU.mult, ALU.add).then_inc(x_ready, 1)

            def moments(src, n, twice=False):
                for t in range(TH):
                    V.bn_stats(stats[0:TILE, 6 * t:6 * t + 6], src(t))
                link(V.tensor_scalar(small[:, 508:509], small[:, 509:510], 0.0, None, ALU.mult))
                for t in range(TH):
                    last = V.bn_aggr(mv[0:TILE, 2 * t:2 * t + 2], stats[0:TILE, 6 * t:6 * t + 6])
                link(last)
                V.tensor_scalar(veps[0:TILE, :], mv[0:TILE, 1:2 * TH:2], EPS, None, ALU.add).then_inc(var_ready, 1)
                dve.wait_ge(rstd_ready, n + 1)
                if twice:
                    dve.wait_ge(rstd2_ready, n - 3)

            def normalize(dst, src, t):
                return V.tensor_scalar(dst, src, mv[0:TILE, 2 * t:2 * t + 1], rstd[0:TILE, t:t + 1],
                                       ALU.subtract, ALU.mult)

            def norm(n, H):
                dve.wait_ge(tm_done, 2 * n + H + 1)
                if n:
                    dve.wait_ge(fm_done, 4 * (n - 1) + 2 * H + 2)

                def rows(t):
                    return ps[0:TILE, 4 + 2 * H + t // 2, (t % 2) * D:(t % 2) * D + D]

                moments(rows, 2 * n + H, n == 2)
                for t in range(TH):
                    last = normalize(tm[0:TILE, TH * H + t, :], rows(t), t)
                for t in range(TH if n == 2 else 0):
                    last = V.tensor_scalar(xn[0:TILE, TH * H + t, :], rows(t), mv[0:TILE, 2 * t:2 * t + 1],
                                           rstd2[0:TILE, t:t + 1], ALU.subtract, ALU.mult)
                last.then_inc(tm_ready, 1)

            def feature_major(n, H):
                for m in range(2):
                    dve.wait_ge(fm_done, 4 * n + 2 * H + m + 1)
                    V.tensor_copy(hT[:, m, cols(H)], ps[:, 4 + 2 * H + m, 0:HALF]).then_inc(h_ready, 1)

            def x_low(H):
                for m in range(2):
                    dve.wait_ge(x_hi_ready, 2 * H + m + 1)
                    V.tensor_tensor(x_lo[:, m, cols(H)], ps[:, 4 + 2 * H + m, 0:HALF],
                                    x_hi[:, m, cols(H)].bitcast(F32), ALU.subtract).then_inc(x_lo_ready, 1)

            def t_low(H):
                dve.wait_ge(t_hi_ready, H + 1)
                for g in (1, 3):
                    rows = slice(32 * g, 32 * g + 32)
                    V.tensor_tensor(t4[rows, cols(H)], ps[rows, 3, 0:HALF], t4[rows, cols(H)].bitcast(F32),
                                    ALU.subtract).then_inc(t_lo_ready, 1)

            def square_low(i):
                dve.wait_ge(hi_ready, i + 1)
                dve.wait_ge(sq_ready, i + 1)
                r = (slice(None), i % HC, cols(i // HC))
                V.tensor_tensor(r_lo[r], squares[:, i % 4, :], r_hi[r].bitcast(F32),
                                ALU.subtract).then_inc(mid_ready, 1)

            V.memset(small[:, 500:512], 0.0)
            attention(0)
            for i in range(2 * HC):
                dve.wait_ge(up_act, i + 1)
                m = mid[:, i % HC, cols(i // HC)]
                V.scalar_tensor_tensor(m, m, 1.0, ps[:, i % 4, 0:HALF], ALU.add, ALU.mult).then_inc(mid_ready, 1)
                if i == 0:
                    ternary_scale(fc_nat, fc_half, fc_nhalf, fc_scale, "fc")
                elif i < 2 + HC and i > 1:
                    ternary(fc_nat, fc_half, fc_nhalf, i - 2, i - 3)
                elif i == 3 + HC:
                    ternary_scale(proj_nat, proj_half, proj_nhalf, proj_scale, "proj")
            for b in range(DC):
                ternary(proj_nat, proj_half, proj_nhalf, b, HC)
            link(V.reciprocal(fc_rs, fc_scale))
            link(V.tensor_scalar(fc_rs, fc_rs, gate_sb[:, 0:1], None, ALU.mult))
            link(V.tensor_tensor(u_sb[:], u_sb[:], fc_rs.unsqueeze(2).to_broadcast([P, HC, RANK]), ALU.mult))
            dve.wait_ge(u_zero, 1)
            B4 = [P, HC, 2, RANK]
            whole = u_sb[:, :, :].unsqueeze(2).to_broadcast(B4)
            u_hi, u_lo = u4[:, :, 0:2, 0:RANK].bitcast(F32R), u4[:, :, 2:4, 0:RANK].bitcast(F32R)
            link(V.tensor_copy(u_hi, whole))
            V.tensor_tensor(u_lo, whole, u4[:, :, 0:2, 0:RANK], ALU.subtract).then_inc(u_ready, 1)
            residual(0, 0, lambda m: 0.5)
            norm(0, 0)
            residual(0, 1, lambda m: 0.5)
            x_low(0)
            feature_major(0, 0)
            norm(0, 1)
            for H in range(2):
                t_low(H)
                for i in range(HC * H, HC * H + HC):
                    square_low(i)
                    if i == 1:
                        x_low(1)
                        feature_major(0, 1)
            residual(1, 0, lambda m: proj_scale[:, m:m + 1])
            norm(1, 0)
            residual(1, 1, lambda m: proj_scale[:, m:m + 1])
            feature_major(1, 0)
            norm(1, 1)
            feature_major(1, 1)
            attention(1)
            residual(2, 0)
            residual(2, 1)
            norm(2, 0)
            norm(2, 1)
            for H in range(2):
                for m in range(2):
                    dve.wait_ge(fm_done, 8 + 2 * H + m + 1)
                    V.tensor_scalar(hT[:, m, cols(H)], ps[:, 4 + 2 * H + m, 0:HALF], lnw[:, m:m + 1], lnb[:, m:m + 1],
                                    ALU.mult, ALU.add).then_inc(h_ready, 1)

            T8 = [TILE, NT, EXPERTS]

            def t8(a):
                return a[0:TILE, :].rearrange("p (t e) -> p t e", e=EXPERTS)

            iota = const("iota")[0:TILE, :].unsqueeze(1).to_broadcast(T8)
            dve.wait_ge(route_done, 1)
            link(V.tensor_copy(lg[0:TILE, :], ps[0:TILE, 4, 0:NT * EXPERTS]))
            V.tensor_reduce(lmax[0:TILE, :], t8(lg), AX.X, ALU.max).then_inc(route_s, 1)
            dve.wait_ge(route_s, 1)
            link(V.tensor_tensor(t8(gt8), t8(lg), lmax[0:TILE, :].unsqueeze(2).to_broadcast(T8), ALU.is_lt))
            link(V.scalar_tensor_tensor(t8(gt8), t8(gt8), float(EXPERTS), iota, ALU.mult, ALU.add))
            link(V.tensor_reduce(eidx[0:TILE, :], t8(gt8), AX.X, ALU.min))
            V.tensor_tensor(t8(ohot), iota, eidx[0:TILE, :].unsqueeze(2).to_broadcast(T8),
                            ALU.is_equal).then_inc(route_s, 1)

            def shared_gate(i):
                dve.wait_ge(sh_act, i + 1)
                m = shmid[:, i % IC, cols(i // IC)]
                link(V.scalar_tensor_tensor(m, m, 1.0, ps[:, 2 * (i % 2), 0:HALF], ALU.add, ALU.mult))
                dve.wait_ge(up_done, 4 * HC + 2 * i + 2)
                V.scalar_tensor_tensor(m, m, 0.5, ps[:, 2 * (i % 2) + 1, 0:HALF], ALU.mult,
                                       ALU.mult).then_inc(mid_ready, 1)

            for i in range(2):
                shared_gate(i)
            dve.wait_ge(score_t, 1)
            link(V.tensor_scalar(score[0:TILE, :], score[0:TILE, :], 1.0, 0.5, ALU.add, ALU.mult))
            dve.wait_ge(xe_sum, 2)
            for t in range(NT):
                V.tensor_scalar(xe[0:TILE, t, :], xe[0:TILE, t, :], score[0:TILE, t:t + 1], None,
                                ALU.mult).then_inc(xe_ready, 1)
            dve.wait_ge(route_done, 2)
            V.tensor_copy(cnt, ps[:, 6, 0:EXPERTS])
            ohot8 = t8(ohot)
            link(V.tensor_tensor(tmp8[0:TILE, :], ps[0:TILE, 5, 0:NT * EXPERTS], ohot[0:TILE, :], ALU.mult))
            link(V.tensor_reduce(rank[0:TILE, :], t8(tmp8), AX.X, ALU.add))
            w6 = wk[0:TILE, 0:NT * STEPS].rearrange("p (t k) -> p t k", k=STEPS)
            link(V.tensor_tensor(w6, rank[0:TILE, :].unsqueeze(2).to_broadcast([TILE, NT, STEPS]),
                                 const("steps")[0:TILE, :].unsqueeze(1).to_broadcast([TILE, NT, STEPS]), ALU.is_ge))
            link(V.tensor_reduce(npart[0:TILE, :], w6, AX.X, ALU.add))
            w8 = wk[:, 0:EXPERTS * STEPS].rearrange("p (e k) -> p e k", k=STEPS)
            link(V.tensor_tensor(w8, cnt.unsqueeze(2).to_broadcast([P, EXPERTS, STEPS]),
                                 const("steps").unsqueeze(1).to_broadcast([P, EXPERTS, STEPS]), ALU.is_gt))
            link(V.tensor_reduce(nslot, w8, AX.X, ALU.add))
            w8 = wk[:, 0:EXPERTS * EXPERTS].rearrange("p (e k) -> p e k", k=EXPERTS)
            link(V.tensor_tensor(w8, nslot.unsqueeze(1).to_broadcast([P, EXPERTS, EXPERTS]),
                                 const("before").rearrange("p (e k) -> p e k", k=EXPERTS), ALU.mult))
            link(V.tensor_reduce(sstart, w8, AX.X, ALU.add))
            V.tensor_tensor(t8(lg), ohot8, sstart[0:TILE, :].unsqueeze(1).to_broadcast(T8), ALU.mult)
            link(V.tensor_tensor(send, sstart, nslot, ALU.add))
            ws = wk[:, :].rearrange("p (s e) -> p s e", e=EXPERTS)
            V.tensor_reduce(first[0:TILE, :], t8(lg), AX.X, ALU.add)
            link(V.tensor_tensor(ws, const("slot").unsqueeze(2).to_broadcast([P, SLOTS, EXPERTS]),
                                 send.unsqueeze(1).to_broadcast([P, SLOTS, EXPERTS]), ALU.is_ge))
            link(V.tensor_reduce(eslot, ws, AX.X, ALU.add))
            row, n = posf[0:TILE, :], npart[0:TILE, :]
            link(V.scalar_tensor_tensor(row, n, float(PART), rank[0:TILE, :], ALU.mult, ALU.add))
            link(V.tensor_scalar(n, n, 1.0, None, ALU.min))
            V.tensor_scalar(eslot, eslot, float(EXPERTS - 1), None, ALU.min)
            V.scalar_tensor_tensor(first[0:TILE, :], first[0:TILE, :], -1.0, eidx[0:TILE, :], ALU.add, ALU.subtract)
            link(V.scalar_tensor_tensor(row, eidx[0:TILE, :], float(SLOT), row, ALU.mult, ALU.add))
            link(V.tensor_scalar(first[0:TILE, :], first[0:TILE, :], float(SLOT), -float(PART), ALU.mult, ALU.add))
            link(V.tensor_tensor(first[0:TILE, :], first[0:TILE, :], n, ALU.mult))
            link(V.scalar_tensor_tensor(row, row, float(PART), first[0:TILE, :], ALU.add, ALU.add))
            V.tensor_copy(posi[0:TILE, :], row).then_inc(pos_ready, 1)
            V.tensor_copy(eint[:, :], eslot).then_inc(pos_ready, 1)
            for i in range(2, 2 * IC):
                shared_gate(i)
            for s in range(SLOTS):
                dve.wait_ge(th_done, s + 1)
                h = hm[:, s % 2, :]
                V.scalar_tensor_tensor(h, h, 1.0, bank(1 + 2 * (s % 2)), ALU.add, ALU.mult).then_inc(g_half, 1)
                dve.wait_ge(g_half, s + 1)
                V.scalar_tensor_tensor(h, h, 0.5, bank(2 + 2 * (s % 2)), ALU.mult, ALU.mult).then_inc(hm_ready, 1)
            for H in range(2):
                for t in range(TH * H, TH * H + TH):
                    dve.wait_ge(shdown_done, t + 1)
                    V.scalar_tensor_tensor(tm[0:TILE, t, :], tm[0:TILE, t, :], 2.0, ps[0:TILE, 1 + t % 4, 0:D],
                                           ALU.mult, ALU.add).then_inc(base_ready, 1)
                for t in range(TH * H, TH * H + TH):
                    dve.wait_ge(base_ready, t + 1)
                    dve.wait_ge(y_back[t], 16)
                    last = V.tensor_tensor(yt[0:TILE, t, :], yt[0:TILE, t, :], tm[0:TILE, t, :], ALU.add)
                link(last)
                moments(lambda t: yt[0:TILE, TH * H + t, :], 6 + H)
                for t in range(TH):
                    normalize(fin[0:TILE, TH * H + t, :], yt[0:TILE, TH * H + t, :], t).then_inc(fin_ready, 1)
                dve.wait_ge(fin_ready, TH * H + TH)
                V.tensor_scalar(small[:, 508:509], small[:, 509:510], 0.0, None, ALU.mult).then_inc(tm_ready, 1)

        @block.tensor
        def _(pe):
            mm, tr = nc.tensor.matmul, nc.tensor.transpose
            pe.wait_ge(L["wp"], 16)
            for k in range(PC):
                pe.wait_ge(L[f"patches{k}"], 16)
                for i in range(4):
                    H, m = i // 2, i % 2
                    last = mm(ps[:, i, 0:HALF], wp_sb[:, k, m * P:(m + 1) * P], pat_sb[:, k, cols(H)],
                              start=(k == 0), stop=(k == PC - 1))
                    if k == PC - 1:
                        last.then_inc(embedded, 1)

            def projections(layer, w, stage, between):
                for H in range(2):
                    if H and between:
                        between()
                    pe.wait_ge(h_ready, h_at(stage, H))
                    if H:
                        pe.wait_ge(raw_out, 4 * (2 * layer + 1))
                    for i in range(4):
                        for k in range(DC):
                            last = mm(ps[:, i, 0:HALF], w[:, k, i * P:(i + 1) * P], hT[:, k, cols(H)],
                                      start=(k == 0), stop=(k == DC - 1))
                        last.then_inc(qk_done, 1)
                pe.wait_ge(h_ready, h_at(stage, 1))
                if layer == 0:
                    for b in range(IMAGES):
                        for k in range(DC):
                            last = mm(ps[64 * (b % 2):64 * (b % 2) + SEQ, 4, (b // 2) * KVW:(b // 2 + 1) * KVW],
                                      hT[:, k, SEQ * b:SEQ * b + SEQ], w[:, k, 2 * D:2 * D + KVW],
                                      start=(k == 0), stop=(k == DC - 1))
                    last.then_inc(v_done, 1)
                for n in range(4 * layer):
                    for r in range(2):
                        for q in range(2):
                            b = 4 * n + 2 * r + q
                            for k in range(DC):
                                last = mm(ps[64 * q:64 * q + SEQ, 4 + n, r * D:(r + 1) * D],
                                          hT[:, k, SEQ * b:SEQ * b + SEQ], w[:, k, 2 * D:3 * D],
                                          start=(k == 0), stop=(k == DC - 1))
                    last.then_inc(v_done, 1)

            def scores(n):
                s = n % SETS
                if n % SETS:
                    pe.wait_ge(s_out, n)
                for r in range(2):
                    for q in range(2):
                        b = 4 * s + 2 * r + q
                        for c in range(DC):
                            for g in range(4):
                                at = (2 * r + c) * 2 * SEQ
                                last = mm(ps[64 * q:64 * q + 64, g, at:at + 2 * SEQ],
                                          qT[32 * g:32 * g + 32, c, SEQ * b:SEQ * b + 64],
                                          kbd[32 * g:32 * g + 32, c, :, SEQ * b:SEQ * b + SEQ],
                                          start=True, stop=True)
                last.then_inc(s_done, 1)

            def values(n, layer):
                s = n % SETS
                pe.wait_ge(p_ready, n + 1)
                for r in range(4):
                    if 4 * n + r >= 2:
                        pe.wait_ge(pt_out, 4 * n + r - 1)
                    for j in range(4):
                        t = 4 * r + j
                        last = tr(ps[:, 4 + r % 2, j * P:(j + 1) * P],
                                  soft[:, n % 2, 2 * t:2 * t + 2, :].rearrange("p a b -> p (a b)"), ident)
                    last.then_inc(pt_done, 1)
                pe.wait_ge(pt_out, 4 * n + 4)
                if n >= 2:
                    pe.wait_ge(o_out, n - 1)
                for r in range(2):
                    for q in range(2):
                        for c in range(DC):
                            for g in range(4):
                                t = 4 * g + 2 * r + c
                                at = c * 4 * SEQ + (2 * r + q) * SEQ
                                last = mm(ps[32 * g:32 * g + 32, 6 + n % 2, at:at + SEQ],
                                          vbd[:, q, 2 * s + r, (4 * c + g) * 32:(4 * c + g) * 32 + 32],
                                          pT[:, t, q, :], start=True, stop=True)
                last.then_inc(o_done, 1)

            def attention(layer, w, stage, between=None):
                projections(layer, w, stage, between)
                n0 = SETS * layer
                pe.wait_ge(roped, 4 * layer + 2)
                pe.wait_ge(k_ready, 2 * layer + 1)
                pe.wait_ge(raw_out, 8 * layer + 8)
                pe.wait_ge(pads_zero, 2 + layer)
                scores(n0)
                for s in range(SETS):
                    if s == 0:
                        pe.wait_ge(roped, 4 * layer + 4)
                        pe.wait_ge(k_ready, 2 * layer + 2)
                    if s < SETS - 1:
                        scores(n0 + s + 1)
                    if s == 0:
                        pe.wait_ge(v_out, 4 * layer + 4)
                    values(n0 + s, layer)

            def down(n, H, w, src, depth, wait, chunks=(0, 1)):
                for m in chunks:
                    for k in range(depth):
                        if m == 0:
                            wait(k)
                        last = mm(ps[:, 4 + 2 * H + m, 0:HALF], w[:, k, m * P:(m + 1) * P], src[:, k, cols(H)],
                                  start=(k == 0), stop=(k == depth - 1))
                    last.then_inc(down_done, 1)

            def token_major(n, H):
                pe.wait_ge(x_ready, 4 * n + 2 * H + 2)
                for t in range(TH):
                    for m in range(2):
                        at = (t % 2) * D + m * P
                        last = tr(ps[0:TILE, 4 + 2 * H + t // 2, at:at + P],
                                  xT[:, m, H * HALF + t * TILE:H * HALF + (t + 1) * TILE], ident)
                last.then_inc(tm_done, 1)

            def back(n, H, src):
                for m in range(2):
                    for t in range(TH):
                        last = tr(ps[:, 4 + 2 * H + m, t * TILE:(t + 1) * TILE],
                                  src[0:TILE, TH * H + t, m * P:(m + 1) * P], ident[0:TILE, 0:TILE])
                    last.then_inc(fm_done, 1)

            pe.wait_ge(L["qkv0"], 16)
            pe.wait_ge(L["consts"], 16)
            pe.wait_ge(h_ready, 4)
            attention(0, qkv0_sb, 0)

            pe.wait_ge(L["w1"], 16)
            pe.wait_ge(s_out, 4)
            for i in range(2 * HC):
                H, m = i // HC, i % HC
                if m == 0:
                    pe.wait_ge(o_out, 4 if H else 4)
                if i >= 4:
                    pe.wait_ge(mid_ready, i - 3)
                for k in range(DC):
                    last = mm(ps[:, i % 4, 0:HALF], w1_sb[:, k, m * P:(m + 1) * P], oT[:, k, cols(H)],
                              start=(k == 0), stop=(k == DC - 1))
                last.then_inc(up_done, 1)
            pe.wait_ge(L["w2"], 16)
            down(0, 0, w2_sb, mid, HC, lambda k: pe.wait_ge(mid_ready, k + 1))
            down(0, 1, w2_sb, mid, HC, lambda k: pe.wait_ge(mid_ready, HC + k + 1), chunks=(0,))
            token_major(0, 0)
            down(0, 1, w2_sb, mid, HC, lambda k: None, chunks=(1,))
            def transpose_ternary(r):
                pe.wait_ge(tern_ready, 4 * (r % 2) + 4 if r < 4 else HC + DC)
                if r >= 4:
                    pe.wait_ge(tern_out, r - 3)
                for j in range(4):
                    if r < 4:
                        k, m = r // 2, 4 * (r % 2) + j
                        src = fc_nat[:, m, k * P:(k + 1) * P]
                    else:
                        k, m = 2 * (r - 4) + j // 2, j % 2
                        src = proj_nat[:, m, k * P:(k + 1) * P]
                    last = tr(ps[:, r % 4, j * P:(j + 1) * P], src, ident)
                last.then_inc(tern_done, 1)

            for r in range(4):
                transpose_ternary(r)
            pe.wait_ge(tm_ready, 1)
            back(0, 0, tm)
            token_major(0, 1)
            for r in range(4, 8):
                transpose_ternary(r)
            pe.wait_ge(tern_out, 6)
            pe.wait_ge(u_ready, 1)
            for r in range(2):
                for j in range(4):
                    last = tr(bank(r)[:, j * P:(j + 1) * P], u4[:, 4 * r + j, :, :].rearrange("p g r -> p (g r)"),
                              ident)
                last.then_inc(r_done, 1)
            pe.wait_ge(tern_out, 8)
            pe.wait_ge(r_out, 2)
            pe.wait_ge(fb_ready, 1)
            for H in range(2):
                if H:
                    pe.wait_ge(relu_ready, HC)
                pe.wait_ge(h_ready, h_at(1, H))
                for k in range(DC):
                    last = mm(ps[0:RANK, 2, 0:HALF], v_sb[:, k, :], hT[:, k, cols(H)], start=(k == 0), stop=(k == 1))
                last.then_inc(r_done, 1)
                pe.wait_ge(r_out, 3 + H)
                mm(ps[:, 3, 0:HALF], fb4[:, :, :].rearrange("p g r -> p (g r)"), t1[:, cols(H)], start=True,
                   stop=True).then_inc(r_done, 1)
                pe.wait_ge(x_lo_ready, 2 * H + 2)
                for m in range(HC):
                    i = HC * H + m
                    if m == 3:
                        pe.wait_ge(t_lo_ready, 2 * H + 2)
                    if m >= 4:
                        pe.wait_ge(relu_ready, i - 3)
                    for k in range(DC):
                        for x in (x_hi, x_lo):
                            mm(ps[:, i % 4, 0:HALF], fcT[:, k, m * P:(m + 1) * P], x[:, k, cols(H)],
                               start=(k == 0 and x is x_hi), stop=False)
                    pe.wait_ge(t_lo_ready, 2 * H + 2)
                    mm(ps[:, i % 4, 0:HALF], uT[:, m * P:(m + 1) * P], t4[:, cols(H)], start=False,
                       stop=True).then_inc(up_done, 1)
                    if i == 2:
                        pe.wait_ge(tm_ready, 2)
                        back(0, 1, tm)

            def down_parts(H, chunks=(0, 1)):
                for m in chunks:
                    for k in range(HC):
                        if m == 0:
                            pe.wait_ge(mid_ready, (2 + H) * HC + k + 1)
                        for x in (r_hi, r_lo):
                            last = mm(ps[:, 4 + 2 * H + m, 0:HALF], projT[:, k, m * P:(m + 1) * P],
                                      x[:, k, cols(H)], start=(k == 0 and x is r_hi), stop=(k == HC - 1 and x is r_lo))
                    last.then_inc(down_done, 1)

            down_parts(0)
            down_parts(1, chunks=(0,))
            token_major(1, 0)
            down_parts(1, chunks=(1,))
            pe.wait_ge(tm_ready, 3)
            back(1, 0, tm)
            token_major(1, 1)

            def second_half_back():
                pe.wait_ge(tm_ready, 4)
                back(1, 1, tm)

            pe.wait_ge(L["qkv1"], 16)
            attention(1, qkv1_sb, 2, second_half_back)
            pe.wait_ge(L["wo"], 16)
            pe.wait_ge(o_out, 6)
            down(2, 0, wo_sb, oT, DC, lambda k: None)
            pe.wait_ge(o_out, 8)
            down(2, 1, wo_sb, oT, DC, lambda k: None)
            token_major(2, 0)
            token_major(2, 1)
            pe.wait_ge(tm_ready, 5)
            back(2, 0, xn)
            pe.wait_ge(tm_ready, 6)
            back(2, 1, xn)
            pe.wait_ge(h_ready, h_at(3, 1))
            for t in range(NT):
                for k in range(DC):
                    last = mm(ps[0:TILE, 4, t * EXPERTS:(t + 1) * EXPERTS], hT[:, k, t * TILE:(t + 1) * TILE],
                              router_sb[:, k, :], start=(k == 0), stop=(k == DC - 1))
            last.then_inc(route_done, 1)

            def shared_up(i):
                H, m = i // IC, i % IC
                if i >= 2:
                    pe.wait_ge(mid_ready, 4 * HC + i - 1)
                for g, at in ((0, GATE0), (1, UP0)):
                    for k in range(DC):
                        last = mm(ps[:, 2 * (i % 2) + g, 0:HALF],
                                  sh[:, at + k * INNER + m * P:at + k * INNER + (m + 1) * P], hT[:, k, cols(H)],
                                  start=(k == 0), stop=(k == DC - 1))
                    last.then_inc(up_done, 1)

            pe.wait_ge(L["shared"], 16)
            for i in range(2):
                shared_up(i)
            pe.wait_ge(route_s, 2)
            oh = ohot[0:TILE, :].rearrange("p (t e) -> p t e", e=EXPERTS)
            for t in range(NT):
                dst = ps[0:TILE, 5, t * EXPERTS:(t + 1) * EXPERTS]
                for b in range(t):
                    mm(dst, ones[0:TILE, 0:TILE], oh[:, b, :], start=(b == 0), stop=False)
                mm(dst, const("tri")[0:TILE, :], oh[:, t, :], start=(t == 0), stop=True)
            for t in range(NT):
                last = mm(ps[:, 6, 0:EXPERTS], ones[0:TILE, :], oh[:, t, :], start=(t == 0), stop=(t == NT - 1))
            last.then_inc(route_done, 1)
            for i in range(2, 2 * IC):
                shared_up(i)

            expert = [None] * SLOTS

            def slot_tokens(s):
                pe.wait_ge(slot_ld[s], 16)
                if s:
                    pe.wait_ge(xs_out, s)
                for c in range(DC):
                    last = tr(bank(0)[:, c * P:(c + 1) * P], slot_x[:, s, c * P:(c + 1) * P], ident)
                last.then_inc(xs_done, 1)

            def slot_up(s, part):
                steps = [(g, at, k) for g, at in ((0, GATE0), (1, UP0)) for k in range(DC)]
                if part == 0:
                    expert[s] = pe.value_load(eint[0:1, s:s + 1], min_val=0, max_val=EXPERTS - 1)
                    pe.wait_ge(xs_out, s + 1)
                    if s >= 2:
                        pe.wait_ge(hm_ready, s - 1)
                    steps = steps[:-1]
                else:
                    steps = steps[-1:]
                for g, at, k in steps:
                    into, begin = bank(1 + 2 * (s % 2) + g), at + k * INNER
                    mm(into[0:PART, :], xsT[:, s % 2, k, 0:PART], ex[:, bass.ds(expert[s] * EW + begin, INNER)],
                       start=(k == 0), stop=(k == DC - 1))
                    last = mm(into[PART:SLOT, :], xsT[:, s % 2, k, PART:SLOT],
                              ex[:, s * EW + begin:s * EW + begin + INNER], start=(k == 0), stop=(k == DC - 1))
                if part:
                    last.then_inc(gu_done, 1)

            def slot_middle(s):
                pe.wait_ge(hm_ready, s + 1)
                if s:
                    pe.wait_ge(hmT_out, s)
                for c in range(IC):
                    last = tr(bank(5)[:, c * P:(c + 1) * P], hm[:, s % 2, c * P:(c + 1) * P], ident)
                last.then_inc(hmT_done, 1)

            def slot_down(s):
                pe.wait_ge(hmT_out, s + 1)
                if s:
                    pe.wait_ge(y_out, s)
                for k in range(IC):
                    begin = DOWN0 + k * D
                    mm(bank(6)[0:PART, 0:D], hmT[:, s % 2, k, 0:PART], ex[:, bass.ds(expert[s] * EW + begin, D)],
                       start=(k == 0), stop=(k == IC - 1))
                    last = mm(bank(6)[PART:SLOT, 0:D], hmT[:, s % 2, k, PART:SLOT],
                              ex[:, s * EW + begin:s * EW + begin + D], start=(k == 0), stop=(k == IC - 1))
                last.then_inc(y_done, 1)

            pe.wait_ge(pos_ready, 2)
            pe.wait_ge(mid_ready, 4 * HC + 2 * IC)
            for e in range(EXPERTS):
                pe.wait_ge(in_ex[e], 16)
            slot_tokens(0)
            slot_up(0, 0)
            slot_up(0, 1)
            slot_tokens(1)
            for s in range(SLOTS):
                if s + 1 < SLOTS:
                    slot_up(s + 1, 0)
                slot_middle(s)
                if s + 1 < SLOTS:
                    slot_up(s + 1, 1)
                if s + 2 < SLOTS:
                    slot_tokens(s + 2)
                slot_down(s)
            for t in range(NT):
                if t == 0:
                    pe.wait_ge(hm_ready, SLOTS)
                if t >= 4:
                    pe.wait_ge(base_ready, t - 3)
                for k in range(IC):
                    last = mm(ps[0:TILE, 1 + t % 4, 0:D], shmid[:, k, t * TILE:(t + 1) * TILE],
                              sh[:, DOWN0 + k * D:DOWN0 + (k + 1) * D], start=(k == 0), stop=(k == IC - 1))
                last.then_inc(shdown_done, 1)


def chunked(w):
    return np.ascontiguousarray(w.reshape(w.shape[0] // P, P, w.shape[1]).transpose(1, 0, 2))


def constants():
    c = np.zeros((P, CONSTS), np.float32)

    def put(name, a):
        at, n = CONST[name]
        c[:, at:at + n] = a

    p = np.arange(P)[:, None]
    freq = (np.float32(1.0) / np.float32(10000.0) ** (np.arange(0, HD, 2, dtype=np.float32) / np.float32(HD)))
    ang = np.arange(SEQ, dtype=np.float32)[None, :] * freq[p[:, 0] % (HD // 2)][:, None]
    put("ident", np.eye(P))
    put("cos", np.cos(ang))
    put("sin", np.sin(ang) * np.where(p % HD < HD // 2, -1.0, 1.0))
    put("odd", (p // HD % 2 == np.arange(2)[None, :]))
    put("causal", np.where(np.arange(SEQ)[None, :] <= p % 64, 0.0, -1e30))
    put("iota", np.arange(EXPERTS)[None, :])
    put("steps", PART * np.arange(1, STEPS + 1)[None, :])
    e = np.arange(EXPERTS)
    put("before", (e[None, :] < e[:, None]).reshape(1, -1))
    put("slot", np.arange(SLOTS)[None, :])
    put("tri", p < np.arange(TILE)[None, :])
    put("ones", 1.0)
    return c


def kernel(x, L0_tok_W_proj, L0_tok_b_proj, L0_tok_pos_emb, L0_attn_Wq, L0_attn_Wk, L0_attn_Wv, L0_attn_W1,
           L0_attn_W2, L0_ffn_fast_b, L0_ffn_w_fc, L0_ffn_w_proj, L0_ffn_u, L0_ffn_v, L0_ffn_gate, L1_attn_Wqkv,
           L1_attn_Wout, L1_ffn_ln_w, L1_ffn_ln_b, L1_ffn_router_w, L1_ffn_gate_w, L1_ffn_up_w, L1_ffn_down_w,
           L1_ffn_sh_gate, L1_ffn_sh_up, L1_ffn_sh_down):
    import concourse.bacc as bacc
    from concourse.bass_utils import run_bass_kernel_spmd

    def a(v):
        return np.asarray(v)

    def heads(w):
        return np.repeat(a(w).reshape(4, HD, D), 4, axis=0).reshape(D, D).T

    def expert(g, u, d):
        return np.concatenate([chunked(m).reshape(P, -1) for m in (g, u, d)], axis=1)

    ims = a(x).reshape(IMAGES, 6, 16, 6, 16, 3).transpose(2, 4, 5, 0, 1, 3).reshape(PC, P, TOK)
    rows = {
        "patches": ims,
        "w_patch": chunked(a(L0_tok_W_proj).T),
        "patch_bias": a(L0_tok_b_proj).reshape(DC, P).T,
        "pos": chunked(a(L0_tok_pos_emb).T),
        "qkv0": chunked(np.concatenate([a(L0_attn_Wq).T, heads(L0_attn_Wk), a(L0_attn_Wv).T], axis=1)),
        "w1": chunked(a(L0_attn_W1).T),
        "w2": chunked(a(L0_attn_W2).T),
        "w_fc": chunked(a(L0_ffn_w_fc)),
        "w_proj": chunked(a(L0_ffn_w_proj)),
        "u": chunked(a(L0_ffn_u)),
        "v": chunked(a(L0_ffn_v).T),
        "fast_b": a(L0_ffn_fast_b).T,
        "gate": np.broadcast_to(a(L0_ffn_gate).reshape(1, 1), (P, 1)),
        "qkv1": chunked(a(L1_attn_Wqkv)),
        "w_out": chunked(a(L1_attn_Wout)),
        "ln_w": a(L1_ffn_ln_w).reshape(DC, P).T,
        "ln_b": a(L1_ffn_ln_b).reshape(DC, P).T,
        "ln_w_row": np.broadcast_to(a(L1_ffn_ln_w).reshape(1, D), (TILE, D)),
        "ln_b_row": np.broadcast_to(a(L1_ffn_ln_b).reshape(1, D), (TILE, D)),
        "router": chunked(a(L1_ffn_router_w)),
        "experts": np.stack([expert(a(L1_ffn_gate_w)[e], a(L1_ffn_up_w)[e], a(L1_ffn_down_w)[e])
                             for e in range(EXPERTS)]),
        "shared": expert(a(L1_ffn_sh_gate), a(L1_ffn_sh_up), a(L1_ffn_sh_down)),
        "consts": constants(),
    }
    nc = bacc.Bacc("TRN2", target_bir_lowering=False, num_devices=1)
    arrays, args = {}, []
    for name, v in rows.items():
        v = np.ascontiguousarray(v)
        arrays["in_" + name] = v
        args.append(nc.dram_tensor("in_" + name, v.shape, mybir.dt.from_np(v.dtype), kind="ExternalInput").ap())
    args.append(nc.dram_tensor("result", (TOK, D), F32, kind="ExternalOutput").ap())
    program(nc, *args)
    r = run_bass_kernel_spmd(nc, [arrays], core_ids=[0])
    return r.results[0]["result"].reshape(IMAGES, SEQ, D)
```

```python
from contextlib import ExitStack

import numpy as np

import concourse.bass as bass
from concourse import mybir

ALU = mybir.AluOpType
ACT = mybir.ActivationFunctionType
F32 = mybir.dt.float32
F32R = mybir.dt.float32r
I32 = mybir.dt.int32
AX = mybir.AxisListType

P = 128
IMAGES = 16
SEQ = 36
TOK = IMAGES * SEQ
HALF = TOK // 2
PAD = 608
D = 256
DC = D // P
PATCH = 768
PC = PATCH // P
HID = 1024
HC = HID // P
HD = 16
KVW = 4 * HD
RANK = 16
TILE = 96
NT = TOK // TILE
TH = NT // 2
EXPERTS = 8
INNER = 512
IC = INNER // P
EW = 2 * DC * INNER + IC * D
SLOT = 128
PART = SLOT // 2
SLOTS = EXPERTS
STEPS = TOK // PART - 1
assert SLOTS * PART >= TOK - PART
SETS = 4
EPS = 1e-5
GATE0, UP0, DOWN0 = 0, DC * INNER, 2 * DC * INNER

CONST = {}
_at = 0
for _name, _n in (("ident", P), ("cos", SEQ), ("sin", SEQ), ("odd", 2), ("causal", SEQ), ("iota", EXPERTS),
                  ("steps", STEPS), ("before", EXPERTS * EXPERTS), ("slot", SLOTS), ("tri", TILE), ("ones", P)):
    CONST[_name] = (_at, _n)
    _at += _n
CONSTS = _at


def program(nc, patches, w_patch, patch_bias, pos, qkv0, w1, w2, w_fc, w_proj, u, v, fast_b, gate, qkv1, w_out,
            ln_w, ln_b, ln_w_row, ln_b_row, router, experts, shared, consts, out):
    ctx = ExitStack()
    with ctx:
        def sb(name, shape, dt=F32):
            return ctx.enter_context(nc.sbuf_tensor(name, shape, dt))

        def sem(name):
            return ctx.enter_context(nc.semaphore(name))

        slot_in = nc.dram_tensor("slot_in", (SLOTS * SLOT, D), F32, kind="Internal").ap()
        slot_out = nc.dram_tensor("slot_out", (SLOTS * SLOT, D), F32, kind="Internal").ap()

        def next_place():
            return -(-nc.sbuf_base // 32) * 32

        ex_base = next_place()
        ex = sb("ex", [P, EXPERTS * EW])
        sh = sb("sh", [P, EW])

        def under(e, at, *shape):
            n = int(np.prod(shape))
            flat = ex[:, e * EW + at:e * EW + at + n]
            return flat.rearrange("p (a b) -> p a b", a=shape[0])

        proj_nat = under(2, 0, DC, HID)
        k8 = under(3, 0, DC * 8, TOK).rearrange("p (c h) t -> p c h t", c=DC)
        pat_sb = under(6, 0, PC, TOK)
        wp_sb = under(6, PC * TOK, PC, D)
        qkv0_sb = under(6, PC * (TOK + D), DC, 2 * D + KVW)
        w1_sb = under(6, 0, DC, HID)
        fc_nat = under(6, DC * HID, HC, D)
        def rounded_at(name, base, at, shape):
            return nc.alloc_sbuf_tensor_at(name, [P] + shape, F32R, offset=base + 4 * at)

        fcT = sb("fcT", [P, DC, HID], F32R)
        w2_sb = nc.alloc_sbuf_tensor_at("w2_sb", [P, HC, D], F32, offset=next_place())
        projT = sb("projT", [P, HC, D], F32R)
        x_hi = rounded_at("x_hi", ex_base, 3 * EW, [DC, TOK])
        x_lo = rounded_at("x_lo", ex_base, 3 * EW + DC * TOK, [DC, TOK])
        t4 = rounded_at("t4", ex_base, 3 * EW + 2 * DC * TOK, [TOK])
        r_lo = rounded_at("r_lo", ex_base, 6 * EW, [HC, TOK])
        uT = rounded_at("uT", ex_base, 2 * EW + DC * HID, [HID])
        qkv1_sb = sb("qkv1_sb", [P, DC, 3 * D])
        wo_sb = sb("wo_sb", [P, DC, D])
        hT = sb("hT", [P, DC, PAD])
        BIG = DC * PAD + 4 * TOK + 32 * SEQ
        r_hi = rounded_at("r_hi", next_place(), 0, [HC, TOK])
        big = sb("big", [P, BIG])
        mid = big[:, 0:HC * TOK].rearrange("p (a b) -> p a b", a=HC)
        qT = big[:, 0:DC * PAD].rearrange("p (a b) -> p a b", a=DC)
        pT = big[:, DC * PAD + 4 * TOK:BIG].rearrange("p (t q i) -> p t q i", t=16, q=2)
        vbd = sb("vbd", [P, 2, IMAGES // 2, D])
        soft = sb("soft", [P, 2, 32, 64])
        oT = sb("oT", [P, DC, TOK])
        xT = sb("xT", [P, DC, TOK])
        tm = sb("tm", [P, NT, D])
        cst = sb("cst", [P, CONSTS])
        small = sb("small", [P, 512])
        _s = [0]

        def sm(n):
            a = _s[0]
            _s[0] += n
            return small[:, a:a + n]

        pbias = sb("pbias", [P, DC])
        pos_sb = sb("pos_sb", [P, DC, SEQ])
        u_sb = sb("u_sb", [P, HC, RANK])
        v_sb = sb("v_sb", [P, DC, RANK])
        fb_sb = sb("fb_sb", [RANK, RANK])
        gate_sb = sb("gate_sb", [P, 1])
        fb4 = under(4, HC * 4 * 32, 4, 32)[0:RANK]
        relus = xT[:, :, :].rearrange("p a b -> p (a b)").rearrange("p (n t) -> p n t", n=4)
        squares = under(4, (HC + 1) * 4 * 32, 4, HALF)
        u4 = under(4, 0, HC, 4 * 32).rearrange("p m (g r) -> p m g r", g=4)
        t1 = oT[0:RANK, 0, :]
        lnw = sb("lnw", [P, DC])
        lnb = sb("lnb", [P, DC])
        router_sb = sb("router_sb", [P, DC, EXPERTS])

        def const(name):
            a, n = CONST[name]
            return cst[:, a:a + n]

        ident, ones = const("ident"), const("ones")
        fc_scale, proj_scale = sm(HC), sm(DC)
        fc_half, fc_nhalf, proj_half, proj_nhalf = sm(HC), sm(HC), sm(DC), sm(DC)
        fc_rs = sm(HC)
        smax, ssum, srec = sm(32), sm(32), sm(32)
        stats_all, mv_all, veps_all, rstd_all = sm(6 * NT), sm(2 * NT), sm(NT), sm(NT)
        stats, mv, veps, rstd = stats_all[:, 0:6 * TH], mv_all[:, 0:2 * TH], veps_all[:, 0:TH], rstd_all[:, 0:TH]
        veps2 = sm(TH)
        mhalf, rstd2 = sm(NT), sm(TH)
        raws = [xT[:, :, :].rearrange("p a b -> p (a b)"), pT.rearrange("p t q i -> p (t q i)")]
        swps = [tm[:, :, :].rearrange("p a b -> p (a b)")[:, 0:4 * HALF],
                soft[:, 1, :, :].rearrange("p a b -> p (a b)")[:, 0:4 * HALF]]
        below = soft[:, :, :, :].rearrange("p a b c -> p (a b c)")[:, 0:2048]
        vflat = vbd[:, :, :, :].rearrange("p a b c -> p (a b c)")
        xn = vflat[:, 0:NT * D].rearrange("p (a b) -> p a b", a=NT)
        xe = vflat[:, NT * D:2 * NT * D].rearrange("p (a b) -> p a b", a=NT)
        lnw_row = vflat[:, 2 * NT * D:2 * NT * D + D]
        lnb_row = vflat[:, 2 * NT * D + D:2 * NT * D + 2 * D]
        sflat = soft[:, :, :, :].rearrange("p a b c -> p (a b c)")
        slot_x = sflat[:, 0:SLOTS * D].rearrange("p (a b) -> p a b", a=SLOTS)
        xsT = sflat[:, SLOTS * D:SLOTS * D + 2 * DC * SLOT].rearrange("p (n c t) -> p n c t", n=2, c=DC)
        shmid = big[:, 0:IC * TOK].rearrange("p (a b) -> p a b", a=IC)
        _b = IC * TOK
        mids = big[:, _b:_b + 2 * INNER].rearrange("p (n a) -> p n a", n=2)
        hmT = oT[:, :, :].rearrange("p a b -> p (a b)")[:, 0:2 * INNER].rearrange("p (n c t) -> p n c t", n=2, c=IC)
        yout = big[:, _b + 2 * INNER:_b + 2 * INNER + 2 * D].rearrange("p (n d) -> p n d", n=2)
        zero = vflat[:, 2 * NT * D + 2 * D:2 * NT * D + 3 * D]
        yt, fin = xn, xe
        lg, gt8, ohot, tmp8 = sm(48), sm(48), sm(48), sm(48)
        lmax, eidx, score, posf = sm(NT), sm(NT), sm(NT), sm(NT)
        rank, npart, first = sm(NT), sm(NT), sm(NT)
        cnt, nslot, sstart, send = sm(8), sm(8), sm(8), sm(8)
        eslot = sm(SLOTS)
        posi = sb("posi", [P, NT], I32)
        eint = sb("eint", [P, SLOTS], I32)
        wk = sb("wk", [P, SLOTS * EXPERTS])
        ohsum = wk[:, 0:NT * EXPERTS]

        ps = ctx.enter_context(nc.psum_tensor("ps", [P, 8, 512], F32))

        def bank(i):
            return ps[:, i, :]

        L = {n: sem("in_" + n) for n in (
            "patches0", "patches1", "patches2", "patches3", "patches4", "patches5", "wp0", "wp1", "wp2",
            "wp3", "wp4", "wp5", "small", "consts", "qkv0",
            "w1", "w2", "fc", "proj", "qkv1", "wo", "shared", "rows")}
        in_ex = [sem(f"in_ex{e}") for e in range(EXPERTS)]
        dve_step = sem("dve_step")
        embedded = sem("embedded")
        h_ready = sem("h_ready")
        pads_zero = sem("pads_zero")
        qk_done = sem("qk_done")
        raw_out = sem("raw_out")
        swapped = sem("swapped")
        cos_done = sem("cos_done")
        sin_done = sem("sin_done")
        roped = sem("roped")
        k_zero = sem("k_zero")
        k_roped = sem("k_roped")
        k_ready = sem("k_ready")
        k_ready2 = sem("k_ready2")
        v_done = sem("v_done")
        v_out = sem("v_out")
        s_done = sem("s_done")
        s_out = sem("s_out")
        s_sub = sem("s_sub")
        s_exp = sem("s_exp")
        p_ready = sem("p_ready")
        pt_done = sem("pt_done")
        pt_out = sem("pt_out")
        o_done = sem("o_done")
        o_out = sem("o_out")
        up_done = sem("up_done")
        up_act = sem("up_act")
        relu_ready = sem("relu_ready")
        hi_ready = sem("hi_ready")
        sq_ready = sem("sq_ready")
        x_hi_ready = sem("x_hi_ready")
        x_lo_ready = sem("x_lo_ready")
        t_hi_ready = sem("t_hi_ready")
        t_lo_ready = sem("t_lo_ready")
        u_zero = sem("u_zero")
        fb_ready = sem("fb_ready")
        fb_zero = sem("fb_zero")
        mid_ready = sem("mid_ready")
        down_done = sem("down_done")
        x_ready = sem("x_ready")
        tm_done = sem("tm_done")
        rstd2_ready = sem("rstd2_ready")
        xn_ready = sem("xn_ready")
        xe_sum = sem("xe_sum")
        var_ready = sem("var_ready")
        rstd_ready = sem("rstd_ready")
        tm_ready = sem("tm_ready")
        fm_done = sem("fm_done")
        tern_ready = sem("tern_ready")
        consts_set = sem("consts_set")
        tern_done = sem("tern_done")
        tern_out = sem("tern_out")
        u_ready = sem("u_ready")
        r_done = sem("r_done")
        r_out = sem("r_out")
        vb_zero = sem("vb_zero")
        sh_act = sem("sh_act")
        route_done = sem("route_done")
        route_s = sem("route_s")
        score_t = sem("score_t")
        pos_ready = sem("pos_ready")
        xe_ready = sem("xe_ready")
        zero_ready = sem("zero_ready")
        slots_zero = sem("slots_zero")
        scattered = sem("scattered")
        slot_ld = [sem(f"slot_ld{s}") for s in range(SLOTS)]
        xs_done, xs_out = sem("xs_done"), sem("xs_out")
        gu_done, th_done, mids_ready = sem("gu_done"), sem("th_done"), sem("mids_ready")
        gated = sem("gated")
        hmT_done, hmT_out = sem("hmT_done"), sem("hmT_out")
        y_done, y_out = sem("y_done"), sem("y_out")
        y_st = [sem(f"y_st{i}") for i in range(2)]
        y_back = [sem(f"y_back{t}") for t in range(NT)]
        shdown_done, base_ready = sem("shdown_done"), sem("base_ready")
        sum_ready = sem("sum_ready")
        fin_ready = sem("fin_ready")
        s_out_dma = sem("s_out_dma")

        def model(n, H):
            return 4 + 2 * H if n < 2 else 6 * H

        def normed(n, H):
            return 4 + 2 * H if n < 2 else 2 + 2 * H

        EARLY = 2

        def shared_bank(t):
            return 4 + t if t < EARLY else 1 + t - EARLY

        def cols(H):
            return slice(H * HALF, (H + 1) * HALF)

        block = ctx.enter_context(nc.Block())

        def key_places(H, groups):
            k = raws[H][:, 2 * HALF:4 * HALF].rearrange("p (c t) -> p c t", c=DC)
            for g in groups:
                rows = slice(32 * g, 32 * g + 32)
                for hh in range(2):
                    yield k8[rows, :, 2 * g + hh, cols(H)], k[rows], const("odd")[rows, hh:hh + 1]

        def h_at(stage, H):
            return 4 * stage + 2 * H + 2

        @block.sync
        def _(sp):
            for k in range(PC):
                sp.dma_start(pat_sb[:, k, :], patches[k]).then_inc(L[f"patches{k}"], 16)
            for dst, src in ((pbias[:], patch_bias), (pos_sb[:], pos), (u_sb[:], u), (v_sb[:], v), (fb_sb[:], fast_b),
                             (gate_sb[:], gate), (lnw[:], ln_w), (lnb[:], ln_b), (router_sb[:], router)):
                sp.dma_start(dst, src).then_inc(L["small"], 16)
            sp.dma_start(cst[:], consts).then_inc(L["consts"], 16)
            sp.dma_start(qkv0_sb, qkv0).then_inc(L["qkv0"], 16)
            sp.dma_start(proj_nat, w_proj).then_inc(L["proj"], 16)
            sp.dma_start(w2_sb[:], w2).then_inc(L["w2"], 16)
            sp.wait_ge(embedded, 4)
            sp.dma_start(w1_sb, w1).then_inc(L["w1"], 16)
            sp.dma_start(fc_nat, w_fc).then_inc(L["fc"], 16)
            sp.dma_start(qkv1_sb[:], qkv1).then_inc(L["qkv1"], 16)
            sp.dma_start(wo_sb[:], w_out).then_inc(L["wo"], 16)
            sp.dma_start(sh[:], shared).then_inc(L["shared"], 16)
            for e in (0, 1, 2, 6, 7, 3, 4, 5):
                if e == 2:
                    sp.wait_ge(down_done, 8)
                if e == 3:
                    sp.wait_ge(s_done, 2 * SETS)
                sp.dma_start(ex[:, e * EW:(e + 1) * EW], experts[e]).then_inc(in_ex[e], 16)
            sp.wait_ge(o_done, 2 * SETS)
            sp.dma_start(lnw_row[0:TILE, :], ln_w_row).then_inc(L["rows"], 16)
            sp.dma_start(lnb_row[0:TILE, :], ln_b_row).then_inc(L["rows"], 16)
            sp.wait_ge(zero_ready, 1)
            for s in range(SLOTS):
                sp.dma_start(slot_in[s * SLOT:(s + 1) * SLOT, :], zero).then_inc(slots_zero, 16)
            sp.wait_ge(scattered, 16 * NT)
            for s in range(SLOTS):
                sp.dma_start(slot_x[:, s, :], slot_in[s * SLOT:(s + 1) * SLOT, :]).then_inc(slot_ld[s], 16)
            for s in range(SLOTS):
                sp.wait_ge(y_out, s + 1)
                sp.dma_start(slot_out[s * SLOT:(s + 1) * SLOT, :], yout[:, s % 2, :]).then_inc(y_st[s % 2], 16)
            for H in range(2):
                sp.wait_ge(fin_ready, H + 1)
                sp.dma_start(out[H * HALF:(H + 1) * HALF, :].rearrange("(t p) d -> p t d", p=TILE),
                             fin[0:TILE, TH * H:TH * H + TH, :]).then_inc(s_out_dma, 16)
            sp.wait_ge(s_out_dma, 16 * 2)

        @block.gpsimd
        def _(pool):
            nc.gpsimd.memset(hT[:, :, TOK:PAD], 0.0).then_inc(pads_zero, 1)
            nc.gpsimd.memset(qT[:, :, TOK:PAD], 0.0).then_inc(pads_zero, 1)
            for g in range(4):
                nc.gpsimd.memset(k8[:, :, 2 * g:2 * g + 2, :], 0.0).then_inc(k_zero, 1)
            nc.gpsimd.memset(vbd[:, :, :, :], 0.0).then_inc(vb_zero, 1)
            nc.gpsimd.memset(soft[:, 0, :, SEQ:64], 0.0).then_inc(vb_zero, 1)
            nc.gpsimd.memset(mhalf, -0.5).then_inc(consts_set, 1)
            pool.wait_ge(consts_set, 1)

            def rope(layer):
                for H in range(2):
                    n = 2 * layer + H
                    raw, swp = raws[H], swps[H]
                    pool.wait_ge(L["consts"], 16)
                    pool.wait_ge(swapped, n + 1)
                    q = raw[:, 0:2 * HALF]
                    q3 = q.rearrange("p (a t) -> p a t", t=SEQ)
                    nc.gpsimd.tensor_tensor(q3, q3, const("cos").unsqueeze(1).to_broadcast([P, 16, SEQ]),
                                            ALU.mult).then_inc(cos_done, 1)
                    pool.wait_ge(cos_done, n + 1)
                    pool.wait_ge(sin_done, n + 1)
                    if layer and H == 0:
                        pool.wait_ge(down_done, 8)
                    nc.gpsimd.tensor_tensor(qT[:, :, cols(H)], q.rearrange("p (a t) -> p a t", a=2),
                                            swp[:, 0:2 * HALF].rearrange("p (a t) -> p a t", a=2),
                                            ALU.add).then_inc(roped, 1)
                pool.wait_ge(k_roped, 2 * layer + 2)
                pool.wait_ge(roped, 2 * layer + 2)
                nc.gpsimd.memset(soft[:, 1, :, SEQ:64], 0.0).then_inc(vb_zero, 1)

            def rsqrt(n):
                pool.wait_ge(var_ready, n + 1)
                if n:
                    pool.wait_ge(tm_ready, n)
                nc.gpsimd.tensor_tensor(rstd[0:TILE, :], veps[0:TILE, :], mhalf[0:TILE, 0:TH],
                                        ALU.pow).then_inc(rstd_ready, 1)

            rope(0)
            pool.wait_ge(s_done, SETS)
            nc.gpsimd.memset(fb4[:, :, :], 0.0).then_inc(fb_zero, 1)
            pool.wait_ge(fb_zero, 1)
            pool.wait_ge(L["small"], 16 * 9)
            nc.gpsimd.tensor_copy(fb4[:, :, 0:RANK],
                                  fb_sb[:, :].unsqueeze(1).to_broadcast([RANK, 4, RANK])).then_inc(fb_ready, 1)
            pool.wait_ge(s_done, SETS)
            nc.gpsimd.memset(u4, 0.0).then_inc(u_zero, 1)
            for n in range(2):
                rsqrt(n)
            for i in range(2 * HC):
                pool.wait_ge(relu_ready, i + 1)
                if i >= 4:
                    pool.wait_ge(mid_ready, 2 * HC + i - 3)
                nc.gpsimd.tensor_tensor(squares[:, i % 4, :], relus[:, i % 4, :], relus[:, i % 4, :],
                                        ALU.mult).then_inc(sq_ready, 1)
            pool.wait_ge(tern_ready, HC + DC)
            nc.gpsimd.memset(soft[:, 0, :, SEQ:64], 0.0).then_inc(vb_zero, 1)
            pool.wait_ge(up_done, 4 * HC)
            pool.wait_ge(mid_ready, 4 * HC)
            nc.gpsimd.memset(under(3, 0, 1, (2 * DC + 1) * TOK), 0.0).then_inc(k_zero, 1)
            nc.gpsimd.memset(under(4, 0, 1, (HC + 1) * 4 * 32 + 4 * HALF), 0.0).then_inc(k_zero, 1)
            for n in range(2, 4):
                rsqrt(n)
            pool.wait_ge(down_done, 8)
            nc.gpsimd.memset(qT[:, :, TOK:PAD], 0.0).then_inc(pads_zero, 1)
            rope(1)
            pool.wait_ge(o_done, 2 * SETS)
            nc.gpsimd.memset(zero, 0.0).then_inc(zero_ready, 1)
            for n in range(4, 6):
                pool.wait_ge(var_ready, n + 1)
                pool.wait_ge(tm_ready, n)
                nc.gpsimd.tensor_tensor(rstd2[0:TILE, :], veps2[0:TILE, :], mhalf[0:TILE, 0:TH],
                                        ALU.pow).then_inc(rstd2_ready, 1)
                rsqrt(n)
            pool.wait_ge(L["rows"], 32)
            pool.wait_ge(tm_ready, 6)
            B6 = [TILE, NT, D]
            nc.gpsimd.tensor_tensor(xe[0:TILE], xn[0:TILE], lnw_row[0:TILE, :].unsqueeze(1).to_broadcast(B6),
                                    ALU.mult).then_inc(xe_sum, 1)
            pool.wait_ge(xe_sum, 1)
            nc.gpsimd.tensor_tensor(xe[0:TILE], xe[0:TILE], lnb_row[0:TILE, :].unsqueeze(1).to_broadcast(B6),
                                    ALU.add).then_inc(xe_sum, 1)
            pool.wait_ge(slots_zero, 16 * SLOTS)
            for t in range(NT):
                pool.wait_ge(pos_ready, 1)
                pool.wait_ge(xe_ready, t + 1)
                pool.indirect_dma_start(slot_in, bass.IndirectOffsetOnAxis(ap=posi[0:TILE, t:t + 1], axis=0),
                                        xe[0:TILE, t, :], None).then_inc(scattered, 16)
            pool.wait_ge(y_st[0], 16 * (SLOTS // 2))
            pool.wait_ge(y_st[1], 16 * (SLOTS // 2))
            for t in range(NT):
                pool.indirect_dma_start(yt[0:TILE, t, :], None, slot_out,
                                        bass.IndirectOffsetOnAxis(ap=posi[0:TILE, t:t + 1], axis=0)
                                        ).then_inc(y_back[t], 16)
            for H in range(2):
                pool.wait_ge(var_ready, 7 + H)
                nc.gpsimd.tensor_tensor(rstd_all[0:TILE, TH * H:TH * H + TH], veps_all[0:TILE, TH * H:TH * H + TH],
                                        mhalf[0:TILE, 0:TH], ALU.pow).then_inc(rstd_ready, 1)

        @block.scalar
        def _(act):
            def rope_in(layer, H):
                n = 2 * layer + H
                raw = raws[H]
                if layer and H:
                    act.wait_ge(down_done, 8)
                for i in range(4):
                    act.wait_ge(qk_done, 4 * n + i + 1)
                    nc.scalar.activation(raw[:, i * HALF:(i + 1) * HALF], ps[:, i, 0:HALF], ACT.Copy,
                                         scale=0.25 if i < 2 else 1.0).then_inc(raw_out, 1)

            def v_in_grouped():
                act.wait_ge(vb_zero, 1)
                act.wait_ge(v_done, 1)
                for q in range(2):
                    for hh in range(2):
                        src = ps[64 * q:64 * q + SEQ, 4, :].rearrange("p (a c) -> p a c", c=HD)
                        dst = vbd[64 * hh:64 * hh + SEQ, q, :, :].rearrange("p r (k b c) -> p (r k) b c", k=4, b=2)
                        nc.scalar.activation(dst[:, :, :, HD * hh:HD * hh + HD],
                                             src.unsqueeze(2).to_broadcast([SEQ, 32, 2, HD]),
                                             ACT.Copy).then_inc(v_out, 1)

            def v_in(s):
                act.wait_ge(v_done, s + 2)
                for q in range(2):
                    for hh in range(2):
                        src = ps[64 * q:64 * q + SEQ, 7, :].rearrange("p (r b c) -> p r b c", r=2, b=8)
                        dst = vbd[64 * hh:64 * hh + SEQ, q, 2 * s:2 * s + 2, :].rearrange("p r (b c) -> p r b c", b=8)
                        last = nc.scalar.activation(dst[:, :, :, HD * hh:HD * hh + HD],
                                                    src[:, :, :, HD * hh:HD * hh + HD], ACT.Copy)
                last.then_inc(v_out, 1)

            def softmax_exp(n):
                for h in range(2):
                    act.wait_ge(s_sub, 2 * n + h + 1)
                    x = soft[:, n % 2, 16 * h:16 * h + 16, 0:SEQ]
                    nc.scalar.activation(x, x, ACT.Exp).then_inc(s_exp, 1)

            def attn_out(n, last):
                for r in range(4):
                    act.wait_ge(pt_done, 4 * n + r + 1)
                    if r == 0 and n:
                        act.wait_ge(o_done, n)
                    src = ps[:, 4 + r % 2, :].rearrange("p (t q i) -> p t q i", t=4, q=2)[:, :, :, 0:SEQ]
                    nc.scalar.activation(pT[:, 4 * r:4 * r + 4, :, :], src, ACT.Copy).then_inc(pt_out, 1)
                if not last:
                    softmax_exp(n + 1)
                act.wait_ge(o_done, n + 1)
                s = n % SETS
                nc.scalar.activation(oT[:, :, s * 4 * SEQ:(s + 1) * 4 * SEQ],
                                     ps[:, 6, 0:8 * SEQ].rearrange("p (c t) -> p c t", c=DC),
                                     ACT.Copy).then_inc(o_out, 1)

            def keys_in(layer, H):
                act.wait_ge(k_roped, 2 * layer + H + 1)
                if H == 0:
                    act.wait_ge(k_zero, 4 + 2 * layer)
                for dst, src, mask in key_places(H, range(2, 4)):
                    last = nc.scalar.activation(dst, src, ACT.Copy, scale=mask)
                last.then_inc(k_ready2, 1)

            def first_tanh(i):
                act.wait_ge(up_done, i + 1)
                nc.scalar.activation(mid[:, i % HC, cols(i // HC)], ps[:, i % 4, 0:HALF], ACT.Tanh,
                                     scale=0.5).then_inc(up_act, 1)

            def attention(layer):
                rope_in(layer, 0)
                rope_in(layer, 1)
                keys_in(layer, 0)
                if layer == 0:
                    v_in_grouped()
                else:
                    v_in(0)
                keys_in(layer, 1)
                n0 = SETS * layer
                softmax_exp(n0)
                for s in range(SETS):
                    if layer and s < SETS - 1:
                        v_in(s + 1)
                    if layer == 0 and s == SETS - 1:
                        for i in range(4):
                            first_tanh(i)
                    attn_out(n0 + s, s == SETS - 1)

            for k in range(PC):
                act.dma_start(wp_sb[:, k, :], w_patch[:, k, :]).then_inc(L[f"wp{k}"], 16)
            attention(0)
            for i in range(4, 2 * HC):
                first_tanh(i)
            def ternary_out(r):
                act.wait_ge(tern_done, r + 1)
                if r < 4:
                    dst = fcT[:, r // 2, (r % 2) * 512:(r % 2) * 512 + 512]
                else:
                    dst = projT[:, 2 * (r - 4):2 * (r - 4) + 2, :].rearrange("p a b -> p (a b)")
                nc.scalar.activation(dst, bank(r % 4), ACT.Copy).then_inc(tern_out, 1)

            def x_high(H):
                for m in range(2):
                    act.wait_ge(fm_done, 2 * H + m + 1)
                    nc.scalar.activation(x_hi[:, m, cols(H)], ps[:, 4 + 2 * H + m, 0:HALF],
                                         ACT.Copy).then_inc(x_hi_ready, 1)

            for r in range(4):
                ternary_out(r)
            x_high(0)
            for r in range(4, 8):
                ternary_out(r)
            for r in range(2):
                act.wait_ge(r_done, r + 1)
                nc.scalar.activation(uT[:, r * 512:(r + 1) * 512], bank(r), ACT.Copy).then_inc(r_out, 1)
            for H in range(2):
                act.wait_ge(r_done, 3 + 2 * H)
                nc.scalar.activation(t1[:, cols(H)], ps[0:RANK, 2, 0:HALF], ACT.Copy).then_inc(r_out, 1)
                act.wait_ge(r_done, 4 + 2 * H)
                nc.scalar.activation(t4[:, cols(H)], ps[:, 3, 0:HALF], ACT.Copy).then_inc(t_hi_ready, 1)
                for i in range(HC * H, HC * H + HC):
                    act.wait_ge(up_done, 2 * HC + i + 1)
                    if i >= 4:
                        act.wait_ge(sq_ready, i - 3)
                    nc.scalar.activation(relus[:, i % 4, :], ps[:, i % 4, 0:HALF], ACT.Relu,
                                         scale=fc_scale[:, i % HC:i % HC + 1]).then_inc(relu_ready, 1)
                    act.wait_ge(relu_ready, i + 1)
                    nc.scalar.activation(r_hi[:, i % HC, cols(H)], relus[:, i % 4, :],
                                         ACT.Square).then_inc(hi_ready, 1)
                    if i == 2:
                        x_high(1)
            attention(1)
            for i in range(2 * IC):
                if i == 3:
                    act.wait_ge(route_s, 1)
                    nc.scalar.activation(score[0:TILE, :], lmax[0:TILE, :], ACT.Tanh, scale=0.5).then_inc(score_t, 1)
                act.wait_ge(up_done, 4 * HC + 2 * i + 1)
                nc.scalar.activation(shmid[:, i % IC, cols(i // IC)], ps[:, 2 * (i % 2), 0:HALF], ACT.Tanh,
                                     scale=0.5).then_inc(sh_act, 1)
            def tokens_out(s):
                act.wait_ge(xs_done, s + 1)
                if s >= 2:
                    act.wait_ge(gu_done, s - 1)
                nc.scalar.activation(xsT[:, s % 2, :, :], bank(0)[:, 0:2 * SLOT].rearrange("p (c t) -> p c t", c=DC),
                                     ACT.Copy).then_inc(xs_out, 1)

            def gate_tanh(s):
                act.wait_ge(gu_done, s + 1)
                if s >= 2:
                    act.wait_ge(hmT_done, s - 1)
                nc.scalar.activation(mids[:, s % 2, :], bank(1 + 2 * (s % 2)), ACT.Tanh, scale=0.5).then_inc(th_done, 1)

            tokens_out(0)
            gate_tanh(0)
            tokens_out(1)
            for s in range(SLOTS):
                act.wait_ge(hmT_done, s + 1)
                if s >= 2:
                    act.wait_ge(y_done, s - 1)
                nc.scalar.activation(hmT[:, s % 2, :, :], bank(5).rearrange("p (c t) -> p c t", c=IC),
                                     ACT.Copy).then_inc(hmT_out, 1)
                if s + 1 < SLOTS:
                    gate_tanh(s + 1)
                if s + 2 < SLOTS:
                    tokens_out(s + 2)
                act.wait_ge(y_done, s + 1)
                if s >= 2:
                    act.wait_ge(y_st[s % 2], 16 * (s // 2))
                nc.scalar.activation(yout[:, s % 2, :], bank(6)[:, 0:D], ACT.Copy).then_inc(y_out, 1)

        @block.vector
        def _(dve):
            chain = [0]

            def link(ins):
                chain[0] += 1
                ins.then_inc(dve_step, 1)
                dve.wait_ge(dve_step, chain[0])

            V = nc.vector
            dve.wait_ge(L["small"], 16 * 9)
            for i in range(4):
                H, m = i // 2, i % 2
                dve.wait_ge(embedded, i + 1)
                V.scalar_tensor_tensor(
                    hT[:, m, cols(H)].rearrange("p (b t) -> p b t", t=SEQ),
                    ps[:, i, 0:HALF].rearrange("p (b t) -> p b t", t=SEQ), pbias[:, m:m + 1],
                    pos_sb[:, m, :].unsqueeze(1).to_broadcast([P, 8, SEQ]), ALU.add, ALU.add).then_inc(h_ready, 1)

            def ternary_scale(nat, half, nhalf, scale, name):
                dve.wait_ge(L[name], 16)
                link(V.tensor_reduce(scale, nat, AX.X, ALU.add, apply_absolute_value=True))
                link(V.tensor_scalar(scale, scale, 1.0 / nat.shape[2], 1e-5, ALU.mult, ALU.max))
                V.tensor_scalar(half, scale, 0.5, None, ALU.mult)
                link(V.tensor_scalar(nhalf, scale, -0.5, None, ALU.mult))

            def ternary(nat, half, nhalf, b, scratch_read):
                n = nat.shape[2]
                scratch = below[:, (b % 2) * n:(b % 2) * n + n]
                if scratch_read > 0:
                    dve.wait_ge(tern_ready, scratch_read)
                link(V.tensor_scalar(scratch, nat[:, b, :], nhalf[:, b:b + 1], None, ALU.is_lt))
                V.scalar_tensor_tensor(nat[:, b, :], nat[:, b, :], half[:, b:b + 1], scratch,
                                       ALU.is_gt, ALU.subtract).then_inc(tern_ready, 1)

            def rope_mid(layer, H):
                n = 2 * layer + H
                raw, swp = raws[H], swps[H]
                dve.wait_ge(raw_out, 4 * n + 4)
                V.stream_shuffle(swp, raw[:, 0:4 * HALF], [(i // HD) * HD + (i + HD // 2) % HD for i in range(32)]
                                 ).then_inc(swapped, 1)
                dve.wait_ge(swapped, n + 1)
                s4 = swp.rearrange("p (a t) -> p a t", t=SEQ)
                dve.wait_ge(L["consts"], 16)
                V.tensor_tensor(s4, s4, const("sin").unsqueeze(1).to_broadcast([P, 32, SEQ]),
                                ALU.mult).then_inc(sin_done, 1)
                k = raw[:, 2 * HALF:4 * HALF]
                k3 = k.rearrange("p (a t) -> p a t", t=SEQ)
                link(V.tensor_tensor(k3, k3, const("cos").unsqueeze(1).to_broadcast([P, 16, SEQ]), ALU.mult))
                dve.wait_ge(sin_done, n + 1)
                V.tensor_tensor(k, k, swp[:, 2 * HALF:4 * HALF], ALU.add).then_inc(k_roped, 1)
                dve.wait_ge(k_roped, n + 1)

            def rope_k(layer, H):
                if H == 0:
                    dve.wait_ge(k_zero, 4 + 2 * layer)
                for dst, src, mask in key_places(H, range(0, 2)):
                    last = V.tensor_scalar(dst, src, mask, None, ALU.mult)
                last.then_inc(k_ready, 1)

            def scores_in(n):
                dve.wait_ge(s_done, n + 1)
                if n >= 2:
                    dve.wait_ge(pt_done, 4 * (n - 1))
                if n % SETS < 2:
                    dve.wait_ge(vb_zero, 2 + 2 * (n // SETS) + n % SETS)
                src = ps[:, 0:4, 0:8 * SEQ].rearrange("p g (s j) -> p g s j", j=SEQ)
                dst = soft[:, n % 2, :, 0:SEQ].rearrange("p (g s) j -> p g s j", g=4)
                mask = const("causal").unsqueeze(1).unsqueeze(1).to_broadcast([P, 4, 8, SEQ])
                V.tensor_tensor(dst, src, mask, ALU.add).then_inc(s_out, 1)

            def scores_max(n):
                x = soft[:, n % 2, :, 0:SEQ]
                dve.wait_ge(s_out, n + 1)
                link(V.tensor_reduce(smax, x, AX.X, ALU.max))
                for h in range(2):
                    part = slice(16 * h, 16 * h + 16)
                    V.tensor_tensor(x[:, part, :], x[:, part, :],
                                    smax[:, part].unsqueeze(2).to_broadcast([P, 16, SEQ]),
                                    ALU.subtract).then_inc(s_sub, 1)

            def scores_norm(n):
                x = soft[:, n % 2, :, 0:SEQ]
                for h in range(2):
                    part = slice(16 * h, 16 * h + 16)
                    dve.wait_ge(s_exp, 2 * n + h + 1)
                    last = V.tensor_reduce(ssum[:, part], x[:, part, :], AX.X, ALU.add)
                link(last)
                link(V.reciprocal(srec, ssum))
                V.tensor_tensor(x, x, srec.unsqueeze(2).to_broadcast([P, 32, SEQ]), ALU.mult).then_inc(p_ready, 1)

            def attention(layer):
                rope_mid(layer, 0)
                rope_k(layer, 0)
                rope_mid(layer, 1)
                rope_k(layer, 1)
                n0 = SETS * layer
                scores_in(n0)
                scores_max(n0)
                for s in range(SETS):
                    scores_norm(n0 + s)
                    if s < SETS - 1:
                        scores_in(n0 + s + 1)
                        scores_max(n0 + s + 1)

            def residual(n, H, scale=None):
                for m in range(2):
                    dve.wait_ge(down_done, 4 * n + 2 * H + m + 1)
                    s = 1.0 if scale is None else scale(m)
                    V.scalar_tensor_tensor(xT[:, m, cols(H)], ps[:, model(n, H) + m, 0:HALF], s, hT[:, m, cols(H)],
                                           ALU.mult, ALU.add).then_inc(x_ready, 1)

            def moments(src, n, twice=False):
                for t in range(TH):
                    last = V.bn_stats(stats[0:TILE, 6 * t:6 * t + 6], src(t))
                link(last)
                for t in range(TH):
                    last = V.bn_aggr(mv[0:TILE, 2 * t:2 * t + 2], stats[0:TILE, 6 * t:6 * t + 6])
                link(last)
                if twice:
                    V.tensor_scalar(veps2[0:TILE, :], mv[0:TILE, 1:2 * TH:2], 1.0 + EPS, EPS * EPS, ALU.mult, ALU.add)
                V.tensor_scalar(veps[0:TILE, :], mv[0:TILE, 1:2 * TH:2], EPS, None, ALU.add).then_inc(var_ready, 1)

            def normalize(dst, src, t):
                return V.tensor_scalar(dst, src, mv[0:TILE, 2 * t:2 * t + 1], rstd[0:TILE, t:t + 1],
                                       ALU.subtract, ALU.mult)

            def norm(n, H):
                dve.wait_ge(tm_done, 2 * n + H + 1)
                if n:
                    dve.wait_ge(fm_done, 4 * (n - 1) + 2 * H + 2)

                def rows(t):
                    return ps[0:TILE, model(n, H) + t // 2, (t % 2) * D:(t % 2) * D + D]

                moments(rows, 2 * n + H, n == 2)
                if n == 2:
                    dve.wait_ge(rstd2_ready, H + 1)
                    for t in range(TH):
                        last = V.tensor_scalar(xn[0:TILE, TH * H + t, :], rows(t), mv[0:TILE, 2 * t:2 * t + 1],
                                               rstd2[0:TILE, t:t + 1], ALU.subtract, ALU.mult)
                    last.then_inc(xn_ready, 1)
                if n == 2 and H:
                    shared_gate(0)
                dve.wait_ge(rstd_ready, 2 * n + H + 1)
                for t in range(TH):
                    last = normalize(tm[0:TILE, TH * H + t, :], rows(t), t)
                last.then_inc(tm_ready, 1)

            def feature_major(n, H):
                for m in range(2):
                    dve.wait_ge(fm_done, 4 * n + 2 * H + m + 1)
                    V.tensor_copy(hT[:, m, cols(H)], ps[:, 4 + 2 * H + m, 0:HALF]).then_inc(h_ready, 1)

            def x_low(H):
                for m in range(2):
                    dve.wait_ge(x_hi_ready, 2 * H + m + 1)
                    V.tensor_tensor(x_lo[:, m, cols(H)], ps[:, 4 + 2 * H + m, 0:HALF],
                                    x_hi[:, m, cols(H)].bitcast(F32), ALU.subtract).then_inc(x_lo_ready, 1)

            def t_low(H):
                dve.wait_ge(t_hi_ready, H + 1)
                for g in (1, 3):
                    rows = slice(32 * g, 32 * g + 32)
                    V.tensor_tensor(t4[rows, cols(H)], ps[rows, 3, 0:HALF], t4[rows, cols(H)].bitcast(F32),
                                    ALU.subtract).then_inc(t_lo_ready, 1)

            def square_low(i):
                dve.wait_ge(hi_ready, i + 1)
                dve.wait_ge(sq_ready, i + 1)
                r = (slice(None), i % HC, cols(i // HC))
                V.tensor_tensor(r_lo[r], squares[:, i % 4, :], r_hi[r].bitcast(F32),
                                ALU.subtract).then_inc(mid_ready, 1)

            attention(0)
            for i in range(2 * HC):
                dve.wait_ge(up_act, i + 1)
                m = mid[:, i % HC, cols(i // HC)]
                V.scalar_tensor_tensor(m, m, 1.0, ps[:, i % 4, 0:HALF], ALU.add, ALU.mult).then_inc(mid_ready, 1)
                if i == 0:
                    ternary_scale(fc_nat, fc_half, fc_nhalf, fc_scale, "fc")
                elif i < 2 + HC and i > 1:
                    ternary(fc_nat, fc_half, fc_nhalf, i - 2, i - 3)
                elif i == 3 + HC:
                    ternary_scale(proj_nat, proj_half, proj_nhalf, proj_scale, "proj")
            for b in range(DC):
                ternary(proj_nat, proj_half, proj_nhalf, b, HC)
            link(V.reciprocal(fc_rs, fc_scale))
            link(V.tensor_scalar(fc_rs, fc_rs, gate_sb[:, 0:1], None, ALU.mult))
            link(V.tensor_tensor(u_sb[:], u_sb[:], fc_rs.unsqueeze(2).to_broadcast([P, HC, RANK]), ALU.mult))
            dve.wait_ge(u_zero, 1)
            B4 = [P, HC, 2, RANK]
            whole = u_sb[:, :, :].unsqueeze(2).to_broadcast(B4)
            u_hi, u_lo = u4[:, :, 0:2, 0:RANK].bitcast(F32R), u4[:, :, 2:4, 0:RANK].bitcast(F32R)
            link(V.tensor_copy(u_hi, whole))
            V.tensor_tensor(u_lo, whole, u4[:, :, 0:2, 0:RANK], ALU.subtract).then_inc(u_ready, 1)
            residual(0, 0, lambda m: 0.5)
            norm(0, 0)
            residual(0, 1, lambda m: 0.5)
            x_low(0)
            feature_major(0, 0)
            norm(0, 1)
            for H in range(2):
                t_low(H)
                for i in range(HC * H, HC * H + HC):
                    square_low(i)
                    if i == 1:
                        x_low(1)
                        feature_major(0, 1)
            residual(1, 0, lambda m: proj_scale[:, m:m + 1])
            norm(1, 0)
            residual(1, 1, lambda m: proj_scale[:, m:m + 1])
            feature_major(1, 0)
            norm(1, 1)
            feature_major(1, 1)
            attention(1)
            def shared_gate(i):
                dve.wait_ge(sh_act, i + 1)
                m = shmid[:, i % IC, cols(i // IC)]
                link(V.scalar_tensor_tensor(m, m, 1.0, ps[:, 2 * (i % 2), 0:HALF], ALU.add, ALU.mult))
                dve.wait_ge(up_done, 4 * HC + 2 * i + 2)
                V.scalar_tensor_tensor(m, m, 0.5, ps[:, 2 * (i % 2) + 1, 0:HALF], ALU.mult,
                                       ALU.mult).then_inc(mid_ready, 1)

            def experts_input(H):
                for m in range(2):
                    dve.wait_ge(fm_done, 8 + 2 * H + m + 1)
                    V.tensor_scalar(hT[:, m, cols(H)], ps[:, normed(2, H) + m, 0:HALF], lnw[:, m:m + 1],
                                    lnb[:, m:m + 1], ALU.mult, ALU.add).then_inc(h_ready, 1)

            residual(2, 0)
            norm(2, 0)
            residual(2, 1)
            experts_input(0)
            norm(2, 1)
            experts_input(1)
            shared_gate(1)

            T8 = [TILE, NT, EXPERTS]

            def t8(a):
                return a[0:TILE, :].rearrange("p (t e) -> p t e", e=EXPERTS)

            iota = const("iota")[0:TILE, :].unsqueeze(1).to_broadcast(T8)
            dve.wait_ge(route_done, 1)
            link(V.tensor_copy(lg[0:TILE, :], ps[0:TILE, 4, 0:NT * EXPERTS]))
            V.tensor_reduce(lmax[0:TILE, :], t8(lg), AX.X, ALU.max).then_inc(route_s, 1)
            dve.wait_ge(route_s, 1)
            link(V.tensor_tensor(t8(gt8), t8(lg), lmax[0:TILE, :].unsqueeze(2).to_broadcast(T8), ALU.is_lt))
            link(V.scalar_tensor_tensor(t8(gt8), t8(gt8), float(EXPERTS), iota, ALU.mult, ALU.add))
            link(V.tensor_reduce(eidx[0:TILE, :], t8(gt8), AX.X, ALU.min))
            link(V.tensor_tensor(t8(ohot), iota, eidx[0:TILE, :].unsqueeze(2).to_broadcast(T8), ALU.is_equal))
            for t in range(NT):
                here = slice(t * EXPERTS, (t + 1) * EXPERTS)
                if t == 0:
                    V.tensor_copy(ohsum[0:TILE, here], ohot[0:TILE, here]).then_inc(route_s, 1)
                else:
                    dve.wait_ge(route_s, 1 + t)
                    V.tensor_tensor(ohsum[0:TILE, here], ohsum[0:TILE, (t - 1) * EXPERTS:t * EXPERTS],
                                    ohot[0:TILE, here], ALU.add).then_inc(route_s, 1)
            shared_gate(2)
            dve.wait_ge(score_t, 1)
            link(V.tensor_scalar(score[0:TILE, :], score[0:TILE, :], 1.0, 0.5, ALU.add, ALU.mult))
            dve.wait_ge(xe_sum, 2)
            for t in range(NT):
                V.tensor_scalar(xe[0:TILE, t, :], xe[0:TILE, t, :], score[0:TILE, t:t + 1], None,
                                ALU.mult).then_inc(xe_ready, 1)
            shared_gate(3)
            dve.wait_ge(route_done, 2)
            V.tensor_copy(cnt, ps[:, 6, 0:EXPERTS])
            ohot8 = t8(ohot)
            link(V.tensor_tensor(tmp8[0:TILE, :], ps[0:TILE, 5, 0:NT * EXPERTS], ohot[0:TILE, :], ALU.mult))
            link(V.tensor_reduce(rank[0:TILE, :], t8(tmp8), AX.X, ALU.add))
            w6 = wk[0:TILE, 0:NT * STEPS].rearrange("p (t k) -> p t k", k=STEPS)
            link(V.tensor_tensor(w6, rank[0:TILE, :].unsqueeze(2).to_broadcast([TILE, NT, STEPS]),
                                 const("steps")[0:TILE, :].unsqueeze(1).to_broadcast([TILE, NT, STEPS]), ALU.is_ge))
            link(V.tensor_reduce(npart[0:TILE, :], w6, AX.X, ALU.add))
            w8 = wk[:, 0:EXPERTS * STEPS].rearrange("p (e k) -> p e k", k=STEPS)
            link(V.tensor_tensor(w8, cnt.unsqueeze(2).to_broadcast([P, EXPERTS, STEPS]),
                                 const("steps").unsqueeze(1).to_broadcast([P, EXPERTS, STEPS]), ALU.is_gt))
            link(V.tensor_reduce(nslot, w8, AX.X, ALU.add))
            w8 = wk[:, 0:EXPERTS * EXPERTS].rearrange("p (e k) -> p e k", k=EXPERTS)
            link(V.tensor_tensor(w8, nslot.unsqueeze(1).to_broadcast([P, EXPERTS, EXPERTS]),
                                 const("before").rearrange("p (e k) -> p e k", k=EXPERTS), ALU.mult))
            link(V.tensor_reduce(sstart, w8, AX.X, ALU.add))
            V.tensor_tensor(t8(lg), ohot8, sstart[0:TILE, :].unsqueeze(1).to_broadcast(T8), ALU.mult)
            link(V.tensor_tensor(send, sstart, nslot, ALU.add))
            ws = wk[:, :].rearrange("p (s e) -> p s e", e=EXPERTS)
            V.tensor_reduce(first[0:TILE, :], t8(lg), AX.X, ALU.add)
            link(V.tensor_tensor(ws, const("slot").unsqueeze(2).to_broadcast([P, SLOTS, EXPERTS]),
                                 send.unsqueeze(1).to_broadcast([P, SLOTS, EXPERTS]), ALU.is_ge))
            link(V.tensor_reduce(eslot, ws, AX.X, ALU.add))
            row, n = posf[0:TILE, :], npart[0:TILE, :]
            link(V.scalar_tensor_tensor(row, n, float(PART), rank[0:TILE, :], ALU.mult, ALU.add))
            link(V.tensor_scalar(n, n, 1.0, None, ALU.min))
            V.tensor_scalar(eslot, eslot, float(EXPERTS - 1), None, ALU.min)
            V.scalar_tensor_tensor(first[0:TILE, :], first[0:TILE, :], -1.0, eidx[0:TILE, :], ALU.add, ALU.subtract)
            link(V.scalar_tensor_tensor(row, eidx[0:TILE, :], float(SLOT), row, ALU.mult, ALU.add))
            link(V.tensor_scalar(first[0:TILE, :], first[0:TILE, :], float(SLOT), -float(PART), ALU.mult, ALU.add))
            link(V.tensor_tensor(first[0:TILE, :], first[0:TILE, :], n, ALU.mult))
            link(V.scalar_tensor_tensor(row, row, float(PART), first[0:TILE, :], ALU.add, ALU.add))
            V.tensor_copy(posi[0:TILE, :], row).then_inc(pos_ready, 1)
            V.tensor_copy(eint[:, :], eslot).then_inc(pos_ready, 1)
            for i in range(4, 2 * IC):
                shared_gate(i)

            def base(t):
                dve.wait_ge(shdown_done, t + 1)
                V.scalar_tensor_tensor(tm[0:TILE, t, :], tm[0:TILE, t, :], 2.0, ps[0:TILE, shared_bank(t), 0:D],
                                       ALU.mult, ALU.add).then_inc(base_ready, 1)

            for t in range(EARLY):
                base(t)
            for s in range(SLOTS):
                dve.wait_ge(th_done, s + 1)
                h = mids[:, s % 2, :]
                V.scalar_tensor_tensor(h, h, 1.0, bank(1 + 2 * (s % 2)), ALU.add, ALU.mult).then_inc(gated, 1)
                dve.wait_ge(gated, s + 1)
                V.scalar_tensor_tensor(h, h, 0.5, bank(2 + 2 * (s % 2)), ALU.mult, ALU.mult).then_inc(mids_ready, 1)
            for t in range(EARLY, NT):
                base(t)
            for H in range(2):
                for t in range(TH * H, TH * H + TH):
                    dve.wait_ge(base_ready, t + 1)
                    dve.wait_ge(y_back[t], 16)
                    V.tensor_tensor(yt[0:TILE, t, :], yt[0:TILE, t, :], tm[0:TILE, t, :],
                                    ALU.add).then_inc(sum_ready, 1)
                    if t > TH * H:
                        dve.wait_ge(sum_ready, t)
                        V.bn_stats(stats_all[0:TILE, 6 * t - 6:6 * t], yt[0:TILE, t - 1, :])
                dve.wait_ge(sum_ready, t + 1)
                link(V.bn_stats(stats_all[0:TILE, 6 * t:6 * t + 6], yt[0:TILE, t, :]))
                for t in range(TH * H, TH * H + TH):
                    last = V.bn_aggr(mv_all[0:TILE, 2 * t:2 * t + 2], stats_all[0:TILE, 6 * t:6 * t + 6])
                link(last)
                V.tensor_scalar(veps_all[0:TILE, TH * H:TH * H + TH], mv_all[0:TILE, 2 * TH * H + 1:2 * TH * (H + 1):2],
                                EPS, None, ALU.add).then_inc(var_ready, 1)
                dve.wait_ge(rstd_ready, 7 + H)
                for t in range(TH * H, TH * H + TH):
                    last = V.tensor_scalar(fin[0:TILE, t, :], yt[0:TILE, t, :], mv_all[0:TILE, 2 * t:2 * t + 1],
                                           rstd_all[0:TILE, t:t + 1], ALU.subtract, ALU.mult)
                last.then_inc(fin_ready, 1)

        @block.tensor
        def _(pe):
            mm, tr = nc.tensor.matmul, nc.tensor.transpose
            for k in range(PC):
                pe.wait_ge(L[f"wp{k}"], 16)
                pe.wait_ge(L[f"patches{k}"], 16)
                for i in range(4):
                    H, m = i // 2, i % 2
                    last = mm(ps[:, i, 0:HALF], wp_sb[:, k, m * P:(m + 1) * P], pat_sb[:, k, cols(H)],
                              start=(k == 0), stop=(k == PC - 1))
                    if k == PC - 1:
                        last.then_inc(embedded, 1)

            def projections(layer, w, stage, between):
                for H in range(2):
                    if H and between:
                        between()
                    pe.wait_ge(h_ready, h_at(stage, H))
                    if H:
                        pe.wait_ge(raw_out, 4 * (2 * layer + 1))
                    for i in range(4):
                        for k in range(DC):
                            last = mm(ps[:, i, 0:HALF], w[:, k, i * P:(i + 1) * P], hT[:, k, cols(H)],
                                      start=(k == 0), stop=(k == DC - 1))
                        last.then_inc(qk_done, 1)
                pe.wait_ge(h_ready, h_at(stage, 1))
                if layer == 0:
                    for b in range(IMAGES):
                        for k in range(DC):
                            last = mm(ps[64 * (b % 2):64 * (b % 2) + SEQ, 4, (b // 2) * KVW:(b // 2 + 1) * KVW],
                                      hT[:, k, SEQ * b:SEQ * b + SEQ], w[:, k, 2 * D:2 * D + KVW],
                                      start=(k == 0), stop=(k == DC - 1))
                    last.then_inc(v_done, 1)

            def set_values(s):
                if s:
                    pe.wait_ge(v_out, 4 + s)
                for r in range(2):
                    for q in range(2):
                        b = 4 * s + 2 * r + q
                        for k in range(DC):
                            last = mm(ps[64 * q:64 * q + SEQ, 7, r * D:(r + 1) * D],
                                      hT[:, k, SEQ * b:SEQ * b + SEQ], qkv1_sb[:, k, 2 * D:3 * D],
                                      start=(k == 0), stop=(k == DC - 1))
                last.then_inc(v_done, 1)

            def scores(n):
                s = n % SETS
                if n % SETS:
                    pe.wait_ge(s_out, n)
                for r in range(2):
                    for c in range(DC):
                        for q in range(2):
                            b = 4 * s + 2 * r + q
                            last = mm(ps[64 * q:64 * q + 64, 2 * r + c, 0:8 * SEQ], qT[:, c, SEQ * b:SEQ * b + 64],
                                      k8[:, c, :, SEQ * b:SEQ * b + SEQ], start=True, stop=True)
                last.then_inc(s_done, 1)

            def values(n, layer):
                s = n % SETS
                pe.wait_ge(p_ready, n + 1)
                for r in range(4):
                    if 4 * n + r >= 2:
                        pe.wait_ge(pt_out, 4 * n + r - 1)
                    for j in range(4):
                        t = 4 * r + j
                        last = tr(ps[:, 4 + r % 2, j * P:(j + 1) * P],
                                  soft[:, n % 2, 2 * t:2 * t + 2, :].rearrange("p a b -> p (a b)"), ident)
                    last.then_inc(pt_done, 1)
                if n == 2 * SETS - 1:
                    token_major(2, 0)
                pe.wait_ge(pt_out, 4 * n + 4)
                if n:
                    pe.wait_ge(o_out, n)
                for r in range(2):
                    for q in range(2):
                        for c in range(DC):
                            for g in range(4):
                                t = 4 * (2 * r + c) + g
                                at = c * 4 * SEQ + (2 * r + q) * SEQ
                                last = mm(ps[32 * g:32 * g + 32, 6, at:at + SEQ],
                                          vbd[:, q, 2 * s + r, (4 * c + g) * 32:(4 * c + g) * 32 + 32],
                                          pT[:, t, q, :], start=True, stop=True)
                last.then_inc(o_done, 1)

            def attention(layer, w, stage, between=None, before_last=None):
                projections(layer, w, stage, between)
                n0 = SETS * layer
                if layer:
                    set_values(0)
                pe.wait_ge(roped, 2 * layer + 1)
                pe.wait_ge(k_ready, 2 * layer + 1)
                pe.wait_ge(k_ready2, 2 * layer + 1)
                pe.wait_ge(raw_out, 8 * layer + 8)
                pe.wait_ge(pads_zero, 2 + layer)
                scores(n0)
                for s in range(SETS):
                    if s == 0:
                        pe.wait_ge(roped, 2 * layer + 2)
                    if s == 1:
                        pe.wait_ge(k_ready, 2 * layer + 2)
                        pe.wait_ge(k_ready2, 2 * layer + 2)
                    if s < SETS - 1:
                        scores(n0 + s + 1)
                        if layer:
                            set_values(s + 1)
                    pe.wait_ge(v_out, 4 + s + 1 if layer else 4)
                    if s == SETS - 1 and before_last:
                        before_last()
                    values(n0 + s, layer)

            def down(n, H, w, src, depth, wait, chunks=(0, 1)):
                for m in chunks:
                    for k in range(depth):
                        if m == 0:
                            wait(k)
                        last = mm(ps[:, model(n, H) + m, 0:HALF], w[:, k, m * P:(m + 1) * P], src[:, k, cols(H)],
                                  start=(k == 0), stop=(k == depth - 1))
                    last.then_inc(down_done, 1)

            def token_major(n, H):
                pe.wait_ge(x_ready, 4 * n + 2 * H + 2)
                for t in range(TH):
                    for m in range(2):
                        at = (t % 2) * D + m * P
                        last = tr(ps[0:TILE, model(n, H) + t // 2, at:at + P],
                                  xT[:, m, H * HALF + t * TILE:H * HALF + (t + 1) * TILE], ident)
                last.then_inc(tm_done, 1)

            def back(n, H, src):
                for m in range(2):
                    for t in range(TH):
                        last = tr(ps[:, normed(n, H) + m, t * TILE:(t + 1) * TILE],
                                  src[0:TILE, TH * H + t, m * P:(m + 1) * P], ident[0:TILE, 0:TILE])
                    last.then_inc(fm_done, 1)

            pe.wait_ge(L["qkv0"], 16)
            pe.wait_ge(L["consts"], 16)
            pe.wait_ge(h_ready, 4)
            def first_up(i):
                H, m = i // HC, i % HC
                if i >= 4:
                    pe.wait_ge(mid_ready, i - 3)
                for k in range(DC):
                    last = mm(ps[:, i % 4, 0:HALF], w1_sb[:, k, m * P:(m + 1) * P], oT[:, k, cols(H)],
                              start=(k == 0), stop=(k == DC - 1))
                last.then_inc(up_done, 1)

            def first_chunks():
                pe.wait_ge(L["w1"], 16)
                pe.wait_ge(o_out, 2)
                pe.wait_ge(s_out, 4)
                for i in range(4):
                    first_up(i)

            attention(0, qkv0_sb, 0, before_last=first_chunks)

            pe.wait_ge(o_out, 4)
            for i in range(4, 2 * HC):
                first_up(i)
            pe.wait_ge(L["w2"], 16)
            down(0, 0, w2_sb, mid, HC, lambda k: pe.wait_ge(mid_ready, k + 1))
            down(0, 1, w2_sb, mid, HC, lambda k: pe.wait_ge(mid_ready, HC + k + 1), chunks=(0,))
            token_major(0, 0)
            down(0, 1, w2_sb, mid, HC, lambda k: None, chunks=(1,))
            def transpose_ternary(r):
                pe.wait_ge(tern_ready, 4 * (r % 2) + 4 if r < 4 else HC + DC)
                if r >= 4:
                    pe.wait_ge(tern_out, r - 3)
                for j in range(4):
                    if r < 4:
                        k, m = r // 2, 4 * (r % 2) + j
                        src = fc_nat[:, m, k * P:(k + 1) * P]
                    else:
                        k, m = 2 * (r - 4) + j // 2, j % 2
                        src = proj_nat[:, m, k * P:(k + 1) * P]
                    last = tr(ps[:, r % 4, j * P:(j + 1) * P], src, ident)
                last.then_inc(tern_done, 1)

            for r in range(4):
                transpose_ternary(r)
            pe.wait_ge(tm_ready, 1)
            back(0, 0, tm)
            token_major(0, 1)
            for r in range(4, 8):
                transpose_ternary(r)
            pe.wait_ge(tern_out, 6)
            pe.wait_ge(u_ready, 1)
            for r in range(2):
                for j in range(4):
                    last = tr(bank(r)[:, j * P:(j + 1) * P], u4[:, 4 * r + j, :, :].rearrange("p g r -> p (g r)"),
                              ident)
                last.then_inc(r_done, 1)
            pe.wait_ge(tern_out, 8)
            pe.wait_ge(r_out, 2)
            pe.wait_ge(fb_ready, 1)
            for H in range(2):
                if H:
                    pe.wait_ge(relu_ready, HC)
                pe.wait_ge(h_ready, h_at(1, H))
                for k in range(DC):
                    last = mm(ps[0:RANK, 2, 0:HALF], v_sb[:, k, :], hT[:, k, cols(H)], start=(k == 0), stop=(k == 1))
                last.then_inc(r_done, 1)
                pe.wait_ge(r_out, 3 + H)
                mm(ps[:, 3, 0:HALF], fb4[:, :, :].rearrange("p g r -> p (g r)"), t1[:, cols(H)], start=True,
                   stop=True).then_inc(r_done, 1)
                pe.wait_ge(x_lo_ready, 2 * H + 2)
                for m in range(HC):
                    i = HC * H + m
                    if m == 3:
                        pe.wait_ge(t_lo_ready, 2 * H + 2)
                    if m >= 4:
                        pe.wait_ge(relu_ready, i - 3)
                    for k in range(DC):
                        for x in (x_hi, x_lo):
                            mm(ps[:, i % 4, 0:HALF], fcT[:, k, m * P:(m + 1) * P], x[:, k, cols(H)],
                               start=(k == 0 and x is x_hi), stop=False)
                    pe.wait_ge(t_lo_ready, 2 * H + 2)
                    mm(ps[:, i % 4, 0:HALF], uT[:, m * P:(m + 1) * P], t4[:, cols(H)], start=False,
                       stop=True).then_inc(up_done, 1)
                    if i == 2:
                        pe.wait_ge(tm_ready, 2)
                        back(0, 1, tm)

            def down_parts(H, chunks=(0, 1)):
                for m in chunks:
                    for k in range(HC):
                        if m == 0:
                            pe.wait_ge(mid_ready, (2 + H) * HC + k + 1)
                        for x in (r_hi, r_lo):
                            last = mm(ps[:, 4 + 2 * H + m, 0:HALF], projT[:, k, m * P:(m + 1) * P],
                                      x[:, k, cols(H)], start=(k == 0 and x is r_hi), stop=(k == HC - 1 and x is r_lo))
                    last.then_inc(down_done, 1)

            down_parts(0)
            down_parts(1, chunks=(0,))
            token_major(1, 0)
            down_parts(1, chunks=(1,))
            pe.wait_ge(tm_ready, 3)
            back(1, 0, tm)
            token_major(1, 1)

            def second_half_back():
                pe.wait_ge(tm_ready, 4)
                back(1, 1, tm)

            pe.wait_ge(L["qkv1"], 16)
            def first_half_out():
                pe.wait_ge(L["wo"], 16)
                pe.wait_ge(o_out, 6)
                pe.wait_ge(s_out, 8)
                down(2, 0, wo_sb, oT, DC, lambda k: None)

            attention(1, qkv1_sb, 2, second_half_back, first_half_out)
            pe.wait_ge(o_out, 8)
            down(2, 1, wo_sb, oT, DC, lambda k: None)
            token_major(2, 1)
            pe.wait_ge(xn_ready, 1)
            back(2, 0, xn)

            def shared_up(i):
                H, m = i // IC, i % IC
                pe.wait_ge(h_ready, h_at(3, H))
                if i >= 2:
                    pe.wait_ge(mid_ready, 4 * HC + i - 1)
                for g, at in ((0, GATE0), (1, UP0)):
                    for k in range(DC):
                        last = mm(ps[:, 2 * (i % 2) + g, 0:HALF],
                                  sh[:, at + k * INNER + m * P:at + k * INNER + (m + 1) * P], hT[:, k, cols(H)],
                                  start=(k == 0), stop=(k == DC - 1))
                    last.then_inc(up_done, 1)

            def shared_down(t):
                for k in range(IC):
                    last = mm(ps[0:TILE, shared_bank(t), 0:D], shmid[:, k, t * TILE:(t + 1) * TILE],
                              sh[:, DOWN0 + k * D:DOWN0 + (k + 1) * D], start=(k == 0), stop=(k == IC - 1))
                last.then_inc(shdown_done, 1)

            pe.wait_ge(L["shared"], 16)
            pe.wait_ge(tm_ready, 5)
            for i in range(2):
                shared_up(i)
            pe.wait_ge(xn_ready, 2)
            back(2, 1, xn)
            shared_up(2)
            pe.wait_ge(h_ready, h_at(3, 1))
            for t in range(NT):
                for k in range(DC):
                    last = mm(ps[0:TILE, 4, t * EXPERTS:(t + 1) * EXPERTS], hT[:, k, t * TILE:(t + 1) * TILE],
                              router_sb[:, k, :], start=(k == 0), stop=(k == DC - 1))
            last.then_inc(route_done, 1)
            shared_up(3)
            pe.wait_ge(route_s, 1 + NT)
            after_first = slice(EXPERTS, NT * EXPERTS)
            mm(ps[0:TILE, 5, 0:NT * EXPERTS], const("tri")[0:TILE, :], ohot[0:TILE, :], start=True, stop=False)
            mm(ps[0:TILE, 5, after_first], ones[0:TILE, 0:TILE], ohsum[0:TILE, 0:(NT - 1) * EXPERTS],
               start=False, stop=True)
            last = mm(ps[:, 6, 0:EXPERTS], ones[0:TILE, :], ohsum[0:TILE, (NT - 1) * EXPERTS:NT * EXPERTS],
                      start=True, stop=True)
            last.then_inc(route_done, 1)
            for i in range(4, 2 * IC):
                shared_up(i)
            pe.wait_ge(pos_ready, 2)
            for t in range(EARLY):
                shared_down(t)

            expert = [None] * SLOTS

            def slot_tokens(s):
                pe.wait_ge(slot_ld[s], 16)
                if s:
                    pe.wait_ge(xs_out, s)
                for c in range(DC):
                    last = tr(bank(0)[:, c * P:(c + 1) * P], slot_x[:, s, c * P:(c + 1) * P], ident)
                last.then_inc(xs_done, 1)

            def slot_up(s, part):
                steps = [(g, at, k) for g, at in ((0, GATE0), (1, UP0)) for k in range(DC)]
                if part == 0:
                    expert[s] = pe.value_load(eint[0:1, s:s + 1], min_val=0, max_val=EXPERTS - 1)
                    pe.wait_ge(xs_out, s + 1)
                    if s >= 2:
                        pe.wait_ge(mids_ready, s - 1)
                    steps = steps[:-1]
                else:
                    steps = steps[-1:]
                for g, at, k in steps:
                    into, begin = bank(1 + 2 * (s % 2) + g), at + k * INNER
                    mm(into[0:PART, :], xsT[:, s % 2, k, 0:PART], ex[:, bass.ds(expert[s] * EW + begin, INNER)],
                       start=(k == 0), stop=(k == DC - 1))
                    last = mm(into[PART:SLOT, :], xsT[:, s % 2, k, PART:SLOT],
                              ex[:, s * EW + begin:s * EW + begin + INNER], start=(k == 0), stop=(k == DC - 1))
                if part:
                    last.then_inc(gu_done, 1)

            def slot_middle(s):
                pe.wait_ge(mids_ready, s + 1)
                if s:
                    pe.wait_ge(hmT_out, s)
                for c in range(IC):
                    last = tr(bank(5)[:, c * P:(c + 1) * P], mids[:, s % 2, c * P:(c + 1) * P], ident)
                last.then_inc(hmT_done, 1)

            def slot_down(s):
                pe.wait_ge(hmT_out, s + 1)
                if s:
                    pe.wait_ge(y_out, s)
                for k in range(IC):
                    begin = DOWN0 + k * D
                    mm(bank(6)[0:PART, 0:D], hmT[:, s % 2, k, 0:PART], ex[:, bass.ds(expert[s] * EW + begin, D)],
                       start=(k == 0), stop=(k == IC - 1))
                    last = mm(bank(6)[PART:SLOT, 0:D], hmT[:, s % 2, k, PART:SLOT],
                              ex[:, s * EW + begin:s * EW + begin + D], start=(k == 0), stop=(k == IC - 1))
                last.then_inc(y_done, 1)

            pe.wait_ge(mid_ready, 4 * HC + 2 * IC)
            pe.wait_ge(base_ready, EARLY)
            for e in range(EXPERTS):
                pe.wait_ge(in_ex[e], 16)
            slot_tokens(0)
            slot_up(0, 0)
            slot_up(0, 1)
            slot_tokens(1)
            for s in range(SLOTS):
                if s + 1 < SLOTS:
                    slot_up(s + 1, 0)
                slot_middle(s)
                if s + 1 < SLOTS:
                    slot_up(s + 1, 1)
                if s + 2 < SLOTS:
                    slot_tokens(s + 2)
                slot_down(s)
            pe.wait_ge(mids_ready, SLOTS)
            for t in range(EARLY, NT):
                shared_down(t)


def chunked(w):
    return np.ascontiguousarray(w.reshape(w.shape[0] // P, P, w.shape[1]).transpose(1, 0, 2))


def constants():
    c = np.zeros((P, CONSTS), np.float32)

    def put(name, a):
        at, n = CONST[name]
        c[:, at:at + n] = a

    p = np.arange(P)[:, None]
    freq = (np.float32(1.0) / np.float32(10000.0) ** (np.arange(0, HD, 2, dtype=np.float32) / np.float32(HD)))
    ang = np.arange(SEQ, dtype=np.float32)[None, :] * freq[p[:, 0] % (HD // 2)][:, None]
    put("ident", np.eye(P))
    put("cos", np.cos(ang))
    put("sin", np.sin(ang) * np.where(p % HD < HD // 2, -1.0, 1.0))
    put("odd", (p // HD % 2 == np.arange(2)[None, :]))
    put("causal", np.where(np.arange(SEQ)[None, :] <= p % 64, 0.0, -1e30))
    put("iota", np.arange(EXPERTS)[None, :])
    put("steps", PART * np.arange(1, STEPS + 1)[None, :])
    e = np.arange(EXPERTS)
    put("before", (e[None, :] < e[:, None]).reshape(1, -1))
    put("slot", np.arange(SLOTS)[None, :])
    put("tri", p < np.arange(TILE)[None, :])
    put("ones", 1.0)
    return c


def kernel(x, L0_tok_W_proj, L0_tok_b_proj, L0_tok_pos_emb, L0_attn_Wq, L0_attn_Wk, L0_attn_Wv, L0_attn_W1,
           L0_attn_W2, L0_ffn_fast_b, L0_ffn_w_fc, L0_ffn_w_proj, L0_ffn_u, L0_ffn_v, L0_ffn_gate, L1_attn_Wqkv,
           L1_attn_Wout, L1_ffn_ln_w, L1_ffn_ln_b, L1_ffn_router_w, L1_ffn_gate_w, L1_ffn_up_w, L1_ffn_down_w,
           L1_ffn_sh_gate, L1_ffn_sh_up, L1_ffn_sh_down):
    import concourse.bacc as bacc
    from concourse.bass_utils import run_bass_kernel_spmd

    def a(v):
        return np.asarray(v)

    def heads(w):
        return np.repeat(a(w).reshape(4, HD, D), 4, axis=0).reshape(D, D).T

    def expert(g, u, d):
        return np.concatenate([chunked(m).reshape(P, -1) for m in (g, u, d)], axis=1)

    ims = a(x).reshape(IMAGES, 6, 16, 6, 16, 3).transpose(2, 4, 5, 0, 1, 3).reshape(PC, P, TOK)
    rows = {
        "patches": ims,
        "w_patch": chunked(a(L0_tok_W_proj).T),
        "patch_bias": a(L0_tok_b_proj).reshape(DC, P).T,
        "pos": chunked(a(L0_tok_pos_emb).T),
        "qkv0": chunked(np.concatenate([a(L0_attn_Wq).T, heads(L0_attn_Wk), a(L0_attn_Wv).T], axis=1)),
        "w1": chunked(a(L0_attn_W1).T),
        "w2": chunked(a(L0_attn_W2).T),
        "w_fc": chunked(a(L0_ffn_w_fc)),
        "w_proj": chunked(a(L0_ffn_w_proj)),
        "u": chunked(a(L0_ffn_u)),
        "v": chunked(a(L0_ffn_v).T),
        "fast_b": a(L0_ffn_fast_b).T,
        "gate": np.broadcast_to(a(L0_ffn_gate).reshape(1, 1), (P, 1)),
        "qkv1": chunked(a(L1_attn_Wqkv)),
        "w_out": chunked(a(L1_attn_Wout)),
        "ln_w": a(L1_ffn_ln_w).reshape(DC, P).T,
        "ln_b": a(L1_ffn_ln_b).reshape(DC, P).T,
        "ln_w_row": np.broadcast_to(a(L1_ffn_ln_w).reshape(1, D), (TILE, D)),
        "ln_b_row": np.broadcast_to(a(L1_ffn_ln_b).reshape(1, D), (TILE, D)),
        "router": chunked(a(L1_ffn_router_w)),
        "experts": np.stack([expert(a(L1_ffn_gate_w)[e], a(L1_ffn_up_w)[e], a(L1_ffn_down_w)[e])
                             for e in range(EXPERTS)]),
        "shared": expert(a(L1_ffn_sh_gate), a(L1_ffn_sh_up), a(L1_ffn_sh_down)),
        "consts": constants(),
    }
    nc = bacc.Bacc("TRN2", target_bir_lowering=False, num_devices=1)
    arrays, args = {}, []
    for name, v in rows.items():
        v = np.ascontiguousarray(v)
        arrays["in_" + name] = v
        args.append(nc.dram_tensor("in_" + name, v.shape, mybir.dt.from_np(v.dtype), kind="ExternalInput").ap())
    args.append(nc.dram_tensor("result", (TOK, D), F32, kind="ExternalOutput").ap())
    program(nc, *args)
    r = run_bass_kernel_spmd(nc, [arrays], core_ids=[0])
    return r.results[0]["result"].reshape(IMAGES, SEQ, D)
```
